# Optimizing a Trainium2 kernel written in Bass

```python
import numpy as np
import jax
import jax.numpy as jnp

def _softmax(x, axis=-1):
    return jax.nn.softmax(x, axis=axis)

def _gelu(x):
    return jax.nn.gelu(x, approximate=True)

def _silu(x):
    return jax.nn.silu(x)

def _sigmoid(x):
    return jax.nn.sigmoid(x)

def _layernorm(x, axis=-1, eps=1e-05):
    m = jnp.mean(x, axis=axis, keepdims=True)
    v = jnp.var(x, axis=axis, keepdims=True)
    return (x - m) / jnp.sqrt(v + eps)

def _scatter_add(tgt, idx, src, axis=0):
    return tgt.at[idx].add(src)

def _segment_sum(src, seg, n):
    return jax.ops.segment_sum(src, seg, n)
kernel_name = 'mk_gps_d2_gnn_r64_843e61'

def setup_inputs(seed: int=0):
    np.random.seed(seed)
    _w = jnp.asarray

    def _rec_inputs():
        import jax
        import jax.numpy as jnp
        _gk = jax.random.key(seed)
        x = -0.0001538 + 1 * jax.random.normal(jax.random.fold_in(_gk, 1), (128, 768), jnp.float32)
        src = jax.random.randint(jax.random.fold_in(_gk, 2), (2048,), 0, 128, jnp.int32)
        dst = jnp.minimum((128 * jax.random.uniform(jax.random.fold_in(_gk, 3), (2048,)) ** 2.0).astype(jnp.int32), 8191)
        _o = jnp.argsort(dst, stable=True)
        src = src[_o]
        dst = dst[_o]
        return (x, src, dst)
    x, src, dst = _rec_inputs()

    def _L0_gnn_setup():
        import jax, jax.numpy as jnp
        import numpy as np
        N_NODES = 128
        N_EDGES = 512
        D = 768
        H1 = 8
        NEG_SLOPE = 0.2

        def gat_conv(x, src, dst, W, a_src, a_dst, b, heads, out_ch):
            n = x.shape[0]
            h = (x @ W).reshape(n, heads, out_ch)
            alpha_src = jnp.einsum('nhc,hc->nh', h, a_src)
            alpha_dst = jnp.einsum('nhc,hc->nh', h, a_dst)
            e = jax.nn.leaky_relu(alpha_src[src] + alpha_dst[dst], NEG_SLOPE)
            m = jax.ops.segment_max(e, dst, num_segments=n)
            m = jnp.where(jnp.isfinite(m), m, 0.0)
            p = jnp.exp(e - m[dst])
            denom = jax.ops.segment_sum(p, dst, num_segments=n)
            alpha = p / denom[dst]
            msg = h[src] * alpha[:, :, None]
            out = jax.ops.segment_sum(msg, dst, num_segments=n)
            return out.reshape(n, heads * out_ch) + b
        key = jax.random.key(seed)
        ks = jax.random.split(key, 10)
        s = 0.02
        x = jax.random.normal(ks[0], (N_NODES, D), dtype=jnp.float32)
        edge_index = jax.random.randint(ks[1], (2, N_EDGES), 0, N_NODES, dtype=jnp.int64)
        W1 = jax.random.normal(ks[2], (D, H1 * D), dtype=jnp.float32) * s
        a_src1 = jax.random.normal(ks[3], (H1, D), dtype=jnp.float32) * s
        a_dst1 = jax.random.normal(ks[4], (H1, D), dtype=jnp.float32) * s
        b1 = jnp.zeros((H1 * D,), dtype=jnp.float32)
        W2 = jax.random.normal(ks[5], (H1 * D, D), dtype=jnp.float32) * s
        a_src2 = jax.random.normal(ks[6], (1, D), dtype=jnp.float32) * s
        a_dst2 = jax.random.normal(ks[7], (1, D), dtype=jnp.float32) * s
        b2 = jnp.zeros((D,), dtype=jnp.float32)
        return {'x': x, 'edge_index': edge_index, 'W1': W1, 'a_src1': a_src1, 'a_dst1': a_dst1, 'b1': b1, 'W2': W2, 'a_src2': a_src2, 'a_dst2': a_dst2, 'b2': b2}
    _L0_gnn_all = _L0_gnn_setup()
    _L0_gnn_in = {k: v for k, v in _L0_gnn_all.items() if k in ('W1', 'a_src1', 'a_dst1', 'b1', 'W2', 'a_src2', 'a_dst2', 'b2')}
    del _L0_gnn_all

    def _L0_mix_setup():
        import jax, jax.numpy as jnp
        import numpy as np
        B, N, DIM, H = (8, 64, 768, 12)
        HD = DIM // H
        SCALE = HD ** (-0.5)
        key = jax.random.key(seed)
        ks = jax.random.split(key, 6)
        x = jax.random.normal(ks[0], (B, N, DIM), dtype=jnp.float32)
        Wqkv = jax.random.normal(ks[1], (3 * DIM, DIM), dtype=jnp.float32) * DIM ** (-0.5)
        Wp = jax.random.normal(ks[2], (DIM, DIM), dtype=jnp.float32) * DIM ** (-0.5)
        bp = jnp.zeros((DIM,), dtype=jnp.float32)
        w_q = jax.random.normal(ks[3], (H, HD), dtype=jnp.float32)
        w_k = jax.random.normal(ks[4], (H, HD), dtype=jnp.float32)
        return {'x': x, 'Wqkv': Wqkv, 'Wp': Wp, 'bp': bp, 'w_q': w_q, 'w_k': w_k}
    _L0_mix_all = _L0_mix_setup()
    _L0_mix_in = {k: v for k, v in _L0_mix_all.items() if k in ('Wqkv', 'Wp', 'bp', 'w_q', 'w_k')}
    del _L0_mix_all

    def _L0_ffn_setup():
        import jax, jax.numpy as jnp
        import numpy as np
        B, S, D = (2, 32, 768)
        E, K, F = (8, 2, 1536)

        def _swiglu(xf, wg, wu, wd):
            return jax.nn.silu(xf @ wg.T) * (xf @ wu.T) @ wd.T
        key = jax.random.key(seed)
        ks = jax.random.split(key, 9)
        scale = 0.02
        x = jax.random.normal(ks[0], (B, S, D), dtype=jnp.float32)
        w_router = jax.random.normal(ks[1], (E, D), dtype=jnp.float32) * scale
        expert_bias = jnp.zeros((E,), dtype=jnp.float32)
        Wg = jax.random.normal(ks[2], (E, F, D), dtype=jnp.float32) * scale
        Wu = jax.random.normal(ks[3], (E, F, D), dtype=jnp.float32) * scale
        Wd = jax.random.normal(ks[4], (E, D, F), dtype=jnp.float32) * scale
        sg = jax.random.normal(ks[5], (F, D), dtype=jnp.float32) * scale
        su = jax.random.normal(ks[6], (F, D), dtype=jnp.float32) * scale
        sd = jax.random.normal(ks[7], (D, F), dtype=jnp.float32) * scale
        return {'x': x, 'w_router': w_router, 'expert_bias': expert_bias, 'Wg': Wg, 'Wu': Wu, 'Wd': Wd, 'sg': sg, 'su': su, 'sd': sd}
    _L0_ffn_all = _L0_ffn_setup()
    _L0_ffn_in = {k: v for k, v in _L0_ffn_all.items() if k in ('w_router', 'expert_bias', 'Wg', 'Wu', 'Wd', 'sg', 'su', 'sd')}
    del _L0_ffn_all

    def _L1_gnn_setup():
        import jax, jax.numpy as jnp
        import numpy as np
        N = 50000
        E = 25000
        IN_DIM = 768
        HID = 256
        OUT_DIM = 768
        HEADS = 4
        NEG_SLOPE = 0.2

        def gat_conv(x, src, dst, W, a_src, a_dst, bias, heads):
            n = x.shape[0]
            h = (x @ W).reshape(n, heads, -1)
            alpha_s = (h * a_src[None]).sum(-1)
            alpha_d = (h * a_dst[None]).sum(-1)
            e = jax.nn.leaky_relu(alpha_s[src] + alpha_d[dst], NEG_SLOPE)
            m = jax.ops.segment_max(e, dst, num_segments=n)
            e = jnp.exp(e - m[dst])
            denom = jax.ops.segment_sum(e, dst, num_segments=n)
            alpha = e / (denom[dst] + 1e-16)
            out = jax.ops.segment_sum(h[src] * alpha[:, :, None], dst, num_segments=n)
            return out.reshape(n, -1) + bias
        key = jax.random.key(seed)
        ks = jax.random.split(key, 12)
        C1 = HID // HEADS
        x = jax.random.normal(ks[0], (N, IN_DIM), dtype=jnp.float32)
        edge_index = jax.random.randint(ks[1], (2, E), 0, N, dtype=jnp.int64)
        sc = lambda f: 1.0 / np.sqrt(f)
        W1 = jax.random.normal(ks[2], (IN_DIM, HEADS * C1), jnp.float32) * sc(IN_DIM)
        a_src1 = jax.random.normal(ks[3], (HEADS, C1), jnp.float32) * sc(C1)
        a_dst1 = jax.random.normal(ks[4], (HEADS, C1), jnp.float32) * sc(C1)
        b1 = jnp.zeros((HEADS * C1,), jnp.float32)
        W2 = jax.random.normal(ks[5], (HID, HID), jnp.float32) * sc(HID)
        a_src2 = jax.random.normal(ks[6], (1, HID), jnp.float32) * sc(HID)
        a_dst2 = jax.random.normal(ks[7], (1, HID), jnp.float32) * sc(HID)
        b2 = jnp.zeros((HID,), jnp.float32)
        Wm1 = jax.random.normal(ks[8], (HID, HID), jnp.float32) * sc(HID)
        bm1 = jnp.zeros((HID,), jnp.float32)
        Wm2 = jax.random.normal(ks[9], (HID, OUT_DIM), jnp.float32) * sc(HID)
        bm2 = jnp.zeros((OUT_DIM,), jnp.float32)
        return {'x': x, 'edge_index': edge_index, 'W1': W1, 'a_src1': a_src1, 'a_dst1': a_dst1, 'b1': b1, 'W2': W2, 'a_src2': a_src2, 'a_dst2': a_dst2, 'b2': b2, 'Wm1': Wm1, 'bm1': bm1, 'Wm2': Wm2, 'bm2': bm2}
    _L1_gnn_all = _L1_gnn_setup()
    _L1_gnn_in = {k: v for k, v in _L1_gnn_all.items() if k in ('W1', 'a_src1', 'a_dst1', 'b1', 'W2', 'a_src2', 'a_dst2', 'b2', 'Wm1', 'bm1', 'Wm2', 'bm2')}
    del _L1_gnn_all

    def _L1_mix_setup():
        import jax, jax.numpy as jnp
        import numpy as np
        NUM_HEADS = 12

        def _l2_norm(t):
            return t / jnp.linalg.norm(t, axis=-2, keepdims=True)

        def _reference_tuple_inner(x, w_qkv, w_proj, b_proj):
            B, N, C = x.shape
            H = NUM_HEADS
            D = C // H
            qkv = (x @ w_qkv).reshape(B, N, 3, H, D).transpose(2, 0, 3, 1, 4)
            q, k, v = (qkv[0], qkv[1], qkv[2])
            q = _l2_norm(q)
            kT = _l2_norm(k).transpose(0, 1, 3, 2)
            sum_k = kT.sum(axis=-1)
            D_inv = 1.0 / (N + jnp.einsum('bhnd,bhd->bhd', q, sum_k))
            attn_matrix = jnp.einsum('bhnd,bhdn->bhdn', q, kT) * D_inv[..., None]
            matrix = jnp.einsum('bhnd,bhdn->bdhn', v, kT)
            y = jnp.einsum('bdhn,bhdn->bhnd', matrix, attn_matrix)
            y = y.transpose(0, 2, 1, 3).reshape(B, N, C)
            out = y @ w_proj + b_proj
            return (out, attn_matrix)
        key = jax.random.key(seed)
        k1, k2, k3 = jax.random.split(key, 3)
        B, N, C = (64, 1024, 768)
        x = jax.random.normal(k1, (B, N, C), dtype=jnp.float32)
        w_qkv = jax.random.normal(k2, (C, 3 * C), dtype=jnp.float32) * 0.02
        w_proj = jax.random.normal(k3, (C, C), dtype=jnp.float32) * 0.02
        b_proj = jnp.zeros((C,), dtype=jnp.float32)
        return {'x': x, 'w_qkv': w_qkv, 'w_proj': w_proj, 'b_proj': b_proj}
    _L1_mix_all = _L1_mix_setup()
    _L1_mix_in = {k: v for k, v in _L1_mix_all.items() if k in ('w_qkv', 'w_proj', 'b_proj')}
    del _L1_mix_all

    def _L1_ffn_setup():
        import jax, jax.numpy as jnp
        import numpy as np
        B, T, D = (2, 32, 768)
        S, R, M, K = (8, 16, 64, 4)
        H, G = (32, 256)

        def _ssinf3(x, P, C, W1, b1, W2, b2, G1, g1b, G2, g2b):
            shp = x.shape
            xf = x.reshape(-1, shp[-1])
            z = jnp.einsum('nd,sdr->nsr', xf, P)
            scores = jnp.einsum('nsr,smr->nsm', z, C)
            topv, topi = jax.lax.top_k(scores, K)
            w = jax.nn.softmax(topv, axis=-1)
            sidx = jnp.arange(S)[None, :, None]
            W1g = W1[sidx, topi]
            b1g = b1[sidx, topi]
            W2g = W2[sidx, topi]
            b2g = b2[sidx, topi]
            h = jax.nn.gelu(jnp.einsum('nsr,nskrh->nskh', z, W1g) + b1g)
            yl = jnp.einsum('nskh,nskhr->nskr', h, W2g) + b2g
            comb = jnp.einsum('nskr,nsk->nsr', yl, w)
            comb = comb.reshape(xf.shape[0], S * R)
            out = jax.nn.gelu(comb @ G1 + g1b) @ G2 + g2b
            return out.reshape(shp)
        key = jax.random.key(seed)
        k = jax.random.split(key, 8)
        rn = lambda kk, shape, s: jax.random.normal(kk, shape, dtype=jnp.float32) * s
        return {'x': rn(k[0], (B, T, D), 1.0), 'P': rn(k[1], (S, D, R), D ** (-0.5)), 'C': rn(k[2], (S, M, R), R ** (-0.5)), 'W1': rn(k[3], (S, M, R, H), R ** (-0.5)), 'b1': jnp.zeros((S, M, H), jnp.float32), 'W2': rn(k[4], (S, M, H, R), H ** (-0.5)), 'b2': jnp.zeros((S, M, R), jnp.float32), 'G1': rn(k[5], (S * R, G), (S * R) ** (-0.5)), 'g1b': jnp.zeros((G,), jnp.float32), 'G2': rn(k[6], (G, D), G ** (-0.5)), 'g2b': jnp.zeros((D,), jnp.float32)}
    _L1_ffn_all = _L1_ffn_setup()
    _L1_ffn_in = {k: v for k, v in _L1_ffn_all.items() if k in ('P', 'C', 'W1', 'b1', 'W2', 'b2', 'G1', 'g1b', 'G2', 'g2b')}
    del _L1_ffn_all
    return {'x': x, 'src': src, 'dst': dst, 'L0_gnn_W1': _L0_gnn_in['W1'], 'L0_gnn_a_src1': _L0_gnn_in['a_src1'], 'L0_gnn_a_dst1': _L0_gnn_in['a_dst1'], 'L0_gnn_b1': _L0_gnn_in['b1'], 'L0_gnn_W2': _L0_gnn_in['W2'], 'L0_gnn_a_src2': _L0_gnn_in['a_src2'], 'L0_gnn_a_dst2': _L0_gnn_in['a_dst2'], 'L0_gnn_b2': _L0_gnn_in['b2'], 'L0_mix_Wqkv': _L0_mix_in['Wqkv'], 'L0_mix_Wp': _L0_mix_in['Wp'], 'L0_mix_bp': _L0_mix_in['bp'], 'L0_mix_w_q': _L0_mix_in['w_q'], 'L0_mix_w_k': _L0_mix_in['w_k'], 'L0_ffn_w_router': _L0_ffn_in['w_router'], 'L0_ffn_expert_bias': _L0_ffn_in['expert_bias'], 'L0_ffn_Wg': _L0_ffn_in['Wg'], 'L0_ffn_Wu': _L0_ffn_in['Wu'], 'L0_ffn_Wd': _L0_ffn_in['Wd'], 'L0_ffn_sg': _L0_ffn_in['sg'], 'L0_ffn_su': _L0_ffn_in['su'], 'L0_ffn_sd': _L0_ffn_in['sd'], 'L1_gnn_W1': _L1_gnn_in['W1'], 'L1_gnn_a_src1': _L1_gnn_in['a_src1'], 'L1_gnn_a_dst1': _L1_gnn_in['a_dst1'], 'L1_gnn_b1': _L1_gnn_in['b1'], 'L1_gnn_W2': _L1_gnn_in['W2'], 'L1_gnn_a_src2': _L1_gnn_in['a_src2'], 'L1_gnn_a_dst2': _L1_gnn_in['a_dst2'], 'L1_gnn_b2': _L1_gnn_in['b2'], 'L1_gnn_Wm1': _L1_gnn_in['Wm1'], 'L1_gnn_bm1': _L1_gnn_in['bm1'], 'L1_gnn_Wm2': _L1_gnn_in['Wm2'], 'L1_gnn_bm2': _L1_gnn_in['bm2'], 'L1_mix_w_qkv': _L1_mix_in['w_qkv'], 'L1_mix_w_proj': _L1_mix_in['w_proj'], 'L1_mix_b_proj': _L1_mix_in['b_proj'], 'L1_ffn_P': _L1_ffn_in['P'], 'L1_ffn_C': _L1_ffn_in['C'], 'L1_ffn_W1': _L1_ffn_in['W1'], 'L1_ffn_b1': _L1_ffn_in['b1'], 'L1_ffn_W2': _L1_ffn_in['W2'], 'L1_ffn_b2': _L1_ffn_in['b2'], 'L1_ffn_G1': _L1_ffn_in['G1'], 'L1_ffn_g1b': _L1_ffn_in['g1b'], 'L1_ffn_G2': _L1_ffn_in['G2'], 'L1_ffn_g2b': _L1_ffn_in['g2b']}

def reference(x, src, dst, L0_gnn_W1, L0_gnn_a_src1, L0_gnn_a_dst1, L0_gnn_b1, L0_gnn_W2, L0_gnn_a_src2, L0_gnn_a_dst2, L0_gnn_b2, L0_mix_Wqkv, L0_mix_Wp, L0_mix_bp, L0_mix_w_q, L0_mix_w_k, L0_ffn_w_router, L0_ffn_expert_bias, L0_ffn_Wg, L0_ffn_Wu, L0_ffn_Wd, L0_ffn_sg, L0_ffn_su, L0_ffn_sd, L1_gnn_W1, L1_gnn_a_src1, L1_gnn_a_dst1, L1_gnn_b1, L1_gnn_W2, L1_gnn_a_src2, L1_gnn_a_dst2, L1_gnn_b2, L1_gnn_Wm1, L1_gnn_bm1, L1_gnn_Wm2, L1_gnn_bm2, L1_mix_w_qkv, L1_mix_w_proj, L1_mix_b_proj, L1_ffn_P, L1_ffn_C, L1_ffn_W1, L1_ffn_b1, L1_ffn_W2, L1_ffn_b2, L1_ffn_G1, L1_ffn_g1b, L1_ffn_G2, L1_ffn_g2b):
    import jax
    import jax.numpy as jnp

    def _L0_gnn_ref(x, edge_index, W1, a_src1, a_dst1, b1, W2, a_src2, a_dst2, b2):
        import jax, jax.numpy as jnp
        import numpy as np
        N_NODES = 128
        N_EDGES = 512
        D = 768
        H1 = 8
        NEG_SLOPE = 0.2

        def gat_conv(x, src, dst, W, a_src, a_dst, b, heads, out_ch):
            n = x.shape[0]
            h = (x @ W).reshape(n, heads, out_ch)
            alpha_src = jnp.einsum('nhc,hc->nh', h, a_src)
            alpha_dst = jnp.einsum('nhc,hc->nh', h, a_dst)
            e = jax.nn.leaky_relu(alpha_src[src] + alpha_dst[dst], NEG_SLOPE)
            m = jax.ops.segment_max(e, dst, num_segments=n)
            m = jnp.where(jnp.isfinite(m), m, 0.0)
            p = jnp.exp(e - m[dst])
            denom = jax.ops.segment_sum(p, dst, num_segments=n)
            alpha = p / denom[dst]
            msg = h[src] * alpha[:, :, None]
            out = jax.ops.segment_sum(msg, dst, num_segments=n)
            return out.reshape(n, heads * out_ch) + b
        n = x.shape[0]
        loops = jnp.arange(n, dtype=edge_index.dtype)
        src = jnp.concatenate([edge_index[0], loops])
        dst = jnp.concatenate([edge_index[1], loops])
        h = gat_conv(x, src, dst, W1, a_src1, a_dst1, b1, H1, D)
        h = jax.nn.elu(h)
        out = gat_conv(h, src, dst, W2, a_src2, a_dst2, b2, 1, D)
        return out

    def _L0_mix_ref(x, Wqkv, Wp, bp, w_q, w_k):
        import jax, jax.numpy as jnp
        import numpy as np
        B, N, DIM, H = (8, 64, 768, 12)
        HD = DIM // H
        SCALE = HD ** (-0.5)
        b, n, c = x.shape
        qkv = x @ Wqkv.T
        qkv = qkv.reshape(b, n, 3, H, HD).transpose(2, 0, 3, 1, 4)
        q, k, v = (qkv[0], qkv[1], qkv[2])
        alpha = jnp.einsum('bhnc,hc->bhn', q, w_q) * SCALE
        alpha = jax.nn.softmax(alpha, axis=-1)
        global_q = jnp.einsum('bhn,bhnc->bhc', alpha, q)
        p = global_q[:, :, None, :] * k
        beta = jnp.einsum('bhnc,hc->bhn', p, w_k) * SCALE
        beta = jax.nn.softmax(beta, axis=-1)
        global_k = jnp.einsum('bhn,bhnc->bhc', beta, k)
        u = global_k[:, :, None, :] * v
        q_flat = q.transpose(0, 2, 1, 3).reshape(b, n, c)
        u_flat = u.transpose(0, 2, 1, 3).reshape(b, n, c)
        return u_flat @ Wp.T + bp + q_flat

    def _L0_ffn_ref(x, w_router, expert_bias, Wg, Wu, Wd, sg, su, sd):
        import jax, jax.numpy as jnp
        import numpy as np
        B, S, D = (2, 32, 768)
        E, K, F = (8, 2, 1536)

        def _swiglu(xf, wg, wu, wd):
            return jax.nn.silu(xf @ wg.T) * (xf @ wu.T) @ wd.T
        b, s, d = x.shape
        xf = x.reshape(-1, d)
        T = xf.shape[0]
        e = w_router.shape[0]
        logits = xf @ w_router.T
        scores = jax.nn.softmax(logits, axis=-1)
        selection = scores + expert_bias[None, :]
        _, top_idx = jax.lax.top_k(selection, K)
        top_s = jnp.take_along_axis(scores, top_idx, axis=-1)
        top_s = top_s / (jnp.sum(top_s, axis=-1, keepdims=True) + 1e-09)
        comb = jnp.zeros((T, e), dtype=x.dtype).at[jnp.arange(T)[:, None], top_idx].add(top_s)

        def body(acc, p):
            wg, wu, wd, c = p
            return (acc + c[:, None] * _swiglu(xf, wg, wu, wd), None)
        routed, _ = jax.lax.scan(body, jnp.zeros_like(xf), (Wg, Wu, Wd, comb.T))
        out = routed + _swiglu(xf, sg, su, sd)
        return out.reshape(b, s, d)

    def _L1_gnn_ref(x, edge_index, W1, a_src1, a_dst1, b1, W2, a_src2, a_dst2, b2, Wm1, bm1, Wm2, bm2):
        import jax, jax.numpy as jnp
        import numpy as np
        N = 50000
        E = 25000
        IN_DIM = 768
        HID = 256
        OUT_DIM = 768
        HEADS = 4
        NEG_SLOPE = 0.2

        def gat_conv(x, src, dst, W, a_src, a_dst, bias, heads):
            n = x.shape[0]
            h = (x @ W).reshape(n, heads, -1)
            alpha_s = (h * a_src[None]).sum(-1)
            alpha_d = (h * a_dst[None]).sum(-1)
            e = jax.nn.leaky_relu(alpha_s[src] + alpha_d[dst], NEG_SLOPE)
            m = jax.ops.segment_max(e, dst, num_segments=n)
            e = jnp.exp(e - m[dst])
            denom = jax.ops.segment_sum(e, dst, num_segments=n)
            alpha = e / (denom[dst] + 1e-16)
            out = jax.ops.segment_sum(h[src] * alpha[:, :, None], dst, num_segments=n)
            return out.reshape(n, -1) + bias
        n = x.shape[0]
        loops = jnp.arange(n, dtype=edge_index.dtype)
        src = jnp.concatenate([edge_index[0], loops])
        dst = jnp.concatenate([edge_index[1], loops])
        h = gat_conv(x, src, dst, W1, a_src1, a_dst1, b1, HEADS)
        h = jax.nn.relu(h)
        h = gat_conv(h, src, dst, W2, a_src2, a_dst2, b2, 1)
        h = jax.nn.relu(h)
        h = jax.nn.relu(h @ Wm1 + bm1)
        return h @ Wm2 + bm2

    def _L1_mix_ref(x, w_qkv, w_proj, b_proj):
        import jax, jax.numpy as jnp
        import numpy as np
        NUM_HEADS = 12

        def _l2_norm(t):
            return t / jnp.linalg.norm(t, axis=-2, keepdims=True)

        def _reference_tuple_inner(x, w_qkv, w_proj, b_proj):
            B, N, C = x.shape
            H = NUM_HEADS
            D = C // H
            qkv = (x @ w_qkv).reshape(B, N, 3, H, D).transpose(2, 0, 3, 1, 4)
            q, k, v = (qkv[0], qkv[1], qkv[2])
            q = _l2_norm(q)
            kT = _l2_norm(k).transpose(0, 1, 3, 2)
            sum_k = kT.sum(axis=-1)
            D_inv = 1.0 / (N + jnp.einsum('bhnd,bhd->bhd', q, sum_k))
            attn_matrix = jnp.einsum('bhnd,bhdn->bhdn', q, kT) * D_inv[..., None]
            matrix = jnp.einsum('bhnd,bhdn->bdhn', v, kT)
            y = jnp.einsum('bdhn,bhdn->bhnd', matrix, attn_matrix)
            y = y.transpose(0, 2, 1, 3).reshape(B, N, C)
            out = y @ w_proj + b_proj
            return (out, attn_matrix)
        return _reference_tuple_inner(x, w_qkv, w_proj, b_proj)[0]

    def _L1_ffn_ref(x, P, C, W1, b1, W2, b2, G1, g1b, G2, g2b):
        import jax, jax.numpy as jnp
        import numpy as np
        B, T, D = (2, 32, 768)
        S, R, M, K = (8, 16, 64, 4)
        H, G = (32, 256)

        def _ssinf3(x, P, C, W1, b1, W2, b2, G1, g1b, G2, g2b):
            shp = x.shape
            xf = x.reshape(-1, shp[-1])
            z = jnp.einsum('nd,sdr->nsr', xf, P)
            scores = jnp.einsum('nsr,smr->nsm', z, C)
            topv, topi = jax.lax.top_k(scores, K)
            w = jax.nn.softmax(topv, axis=-1)
            sidx = jnp.arange(S)[None, :, None]
            W1g = W1[sidx, topi]
            b1g = b1[sidx, topi]
            W2g = W2[sidx, topi]
            b2g = b2[sidx, topi]
            h = jax.nn.gelu(jnp.einsum('nsr,nskrh->nskh', z, W1g) + b1g)
            yl = jnp.einsum('nskh,nskhr->nskr', h, W2g) + b2g
            comb = jnp.einsum('nskr,nsk->nsr', yl, w)
            comb = comb.reshape(xf.shape[0], S * R)
            out = jax.nn.gelu(comb @ G1 + g1b) @ G2 + g2b
            return out.reshape(shp)
        return _ssinf3(x, P, C, W1, b1, W2, b2, G1, g1b, G2, g2b)
    edge_index = jnp.stack([src, dst])
    xn = _layernorm(x, axis=-1)
    x = x + _L0_gnn_ref(xn, edge_index, L0_gnn_W1, L0_gnn_a_src1, L0_gnn_a_dst1, L0_gnn_b1, L0_gnn_W2, L0_gnn_a_src2, L0_gnn_a_dst2, L0_gnn_b2) + _L0_mix_ref(xn[None], L0_mix_Wqkv, L0_mix_Wp, L0_mix_bp, L0_mix_w_q, L0_mix_w_k)[0]
    x = x + _L0_ffn_ref(_layernorm(x, axis=-1)[None], L0_ffn_w_router, L0_ffn_expert_bias, L0_ffn_Wg, L0_ffn_Wu, L0_ffn_Wd, L0_ffn_sg, L0_ffn_su, L0_ffn_sd)[0]
    xn = _layernorm(x, axis=-1)
    x = x + _L1_gnn_ref(xn, edge_index, L1_gnn_W1, L1_gnn_a_src1, L1_gnn_a_dst1, L1_gnn_b1, L1_gnn_W2, L1_gnn_a_src2, L1_gnn_a_dst2, L1_gnn_b2, L1_gnn_Wm1, L1_gnn_bm1, L1_gnn_Wm2, L1_gnn_bm2) + _L1_mix_ref(xn[None], L1_mix_w_qkv, L1_mix_w_proj, L1_mix_b_proj)[0]
    x = x + _L1_ffn_ref(_layernorm(x, axis=-1)[None], L1_ffn_P, L1_ffn_C, L1_ffn_W1, L1_ffn_b1, L1_ffn_W2, L1_ffn_b2, L1_ffn_G1, L1_ffn_g1b, L1_ffn_G2, L1_ffn_g2b)[0]
    return x

_drawn_inputs = setup_inputs


def setup_inputs(seed=0):
    import zlib

    import numpy as np

    out = dict(_drawn_inputs(seed))
    spreads = {'L0_gnn_b1': (0.0, 0.1),
     'L0_gnn_b2': (0.0, 0.1),
     'L0_mix_bp': (0.0, 0.1),
     'L0_ffn_expert_bias': (0.0, 0.1),
     'L1_gnn_b1': (0.0, 0.403),
     'L1_gnn_b2': (0.0, 0.1),
     'L1_gnn_bm1': (0.0, 0.1),
     'L1_gnn_bm2': (0.0, 0.1),
     'L1_mix_b_proj': (0.0, 0.1),
     'L1_ffn_b1': (0.0, 0.726),
     'L1_ffn_b2': (0.0, 0.472),
     'L1_ffn_g1b': (0.0, 0.274),
     'L1_ffn_g2b': (0.0, 0.1)}
    factors = {'L0_gnn_a_src1': 3.471,
     'L0_gnn_a_dst1': 8.0,
     'L0_gnn_a_src2': 8.0,
     'L0_gnn_a_dst2': 8.0,
     'L1_gnn_a_src1': 2.859,
     'L1_gnn_a_dst1': 7.998,
     'L1_gnn_a_src2': 8.0,
     'L1_gnn_a_dst2': 26.386,
     'L1_mix_w_qkv': 200.0,
     'L1_mix_w_proj': 200.0}
    for name, (base, spread) in spreads.items():
        noise = np.random.default_rng([zlib.crc32(name.encode()), seed]).standard_normal(out[name].shape)
        drawn = base * np.exp(spread * noise) if base else spread * noise
        out[name] = jnp.asarray(drawn.astype(out[name].dtype))
    for name, factor in factors.items():
        out[name] = (out[name] * factor).astype(out[name].dtype)
    return out
```

```python
from contextlib import ExitStack

import concourse.bass as bass
from concourse import mybir

P = 128
N = 128
D = 768
KD = D // P
HALF = D // 2
SLOT = 3072
R = 6
S = 3
H0 = 8
FS = 27
FB = 512

QKV0 = 0
TAIL0 = 27
FFN0 = 32
L1 = FFN0 + 3 * FS
NCH = L1 + 9

F32 = mybir.dt.float32
F32R = mybir.dt.float32r
BF16 = mybir.dt.bfloat16
I32 = mybir.dt.int32
U32 = mybir.dt.uint32
ALU = mybir.AluOpType
ACT = mybir.ActivationFunctionType
AX = mybir.AxisListType.X

PC = {}
_at = 0
for _n, _w in (("a1T", 96), ("b1T", 48), ("wr", 48), ("ebias", 8), ("gb1", 2), ("gb2", 2), ("bm1", 2), ("fg1b", 2)):
    PC[_n] = (_at, _at + _w)
    _at += _w
NSMALL = _at

FC = {}
_at = 0
for _n, _w in (("P", 768), ("C", 512), ("W1", 4096), ("W2", 2048), ("b2", 512), ("G1", 256)):
    FC[_n] = (_at, _at + _w)
    _at += _w
NF = _at
EPS = 1e-5
BIG = -1e30


def chunk_len(c):
    if c in (4, 6, 8, L1 + 1, L1 + 5):
        return 1536
    if c in (29, 30, L1 + 6, L1 + 7):
        return 2304
    if c == NCH - 1:
        return 2560
    return SLOT


def landed_at(c):
    return 16 * (c // R + 1)


def build(nc, x_d, src_d, dst_d, stream_d, small_d, wqb_d, wk_d, a2b_d, ga_d, brow_d, fw_d, g2_d, out_d):
    with ExitStack() as ctx:
        def sb(name, shape, dt=F32):
            return ctx.enter_context(nc.sbuf_tensor(name, shape, dt))

        def sem(name):
            return ctx.enter_context(nc.semaphore(name))

        ps = ctx.enter_context(nc.psum_tensor("ps", [P, 8, 512], F32))

        raw = sb("raw", [P, R, SLOT])
        whi = sb("whi", [P, S, SLOT], F32R)
        wlo = sb("wlo", [P, S, SLOT], F32R)
        small = sb("small", [P, NSMALL])
        pa = sb("pa", [P, 1024])
        xres = sb("xres", [P, D])
        xn = sb("xn", [P, D])
        xTh = sb("xTh", [P, KD, P], F32R)
        xTl = sb("xTl", [P, KD, P], F32R)
        ident = sb("ident", [P, P])
        ones = sb("ones", [P, P])
        iota = sb("iota", [P, P])
        cnt = sb("cnt", [P, P])
        cneg = sb("cneg", [P, P])
        brow = sb("brow", [97, D])
        stat = sb("stat", [P, 160])
        qkv = sb("qkv", [P, 3 * D])
        hsb = sb("hsb", [P, 2, D])
        hTs = sb("hTs", [P, D])
        yb = sb("yb", [P, D])
        eb = sb("eb", [P, D])
        oTh = sb("oTh", [P, D], F32R)
        oTl = sb("oTl", [P, D], F32R)
        gz = sb("gz", [P, 1536])
        gqm = sb("gqm", [P, D])

        def sm(name):
            a, b = PC[name]
            return small[:, a:b]

        fbase = raw[:, 2:5, :].rearrange("p s c -> p (s c)")

        def fw(name):
            a, b = FC[name]
            return fbase[:, a:b]

        al = stat[:, 0:8]
        mx = stat[:, 8:12]
        nm = stat[:, 12:16]
        den = stat[:, 16:20]
        rcp = stat[:, 20:24]
        bst = stat[:, 24:36]
        mv = stat[:, 36:38]
        rstd = stat[:, 38:39]
        mhalf = stat[:, 39:51]
        comb = stat[:, 51:78]
        veps = stat[:, 78:79]
        mixa = stat[:, 80:92]
        mst = stat[:, 92:96]
        edg = stat[:, 96:128]
        awt = sb("awt", [12, P])
        soh = qkv[:, 0:1024].bitcast(BF16).rearrange("p (t n) -> p t n", t=16)
        doh = qkv[:, 1024:2048].bitcast(BF16).rearrange("p (t n) -> p t n", t=16)
        hm = eb[0:12, :]
        wkm = gz[0:12, 384:384 + D]
        zt1, ATs, dg = gz[:, 0:P], gz[:, P:2 * P], gz[:, 2 * P:3 * P]
        hsf = hsb[:].rearrange("p a n -> p (a n)")
        asb = [hsf[:, 0:FB], hsf[:, FB:2 * FB]]
        hhb = [gz[:, 0:FB], gz[:, FB:2 * FB]]
        L1Z, L1D, L1AT = gz[:, 0:512], gz[:, 512:1024], gz[:, 1024:1536]
        qT, kT, vT = hsb[:, 0, :], hsb[:, 1, :], hTs[:]
        gT, gT2 = yb[:, 0:256], yb[:, 256:512]
        zp, zT, fT = yb[:, 0:256], yb[:, 256:512], yb[:, 512:768]
        scs, wT, ww = gz[:, 0:512], gz[:, 512:1024], gz[:, 1024:1536]
        eq = fbase[:, 8192:9216]
        hg = [hsf[:, 0:512], hsf[:, 512:1024], hsf[:, 1024:1536], xn[:, 0:512]]
        yt, cb, cT = eb[:, 0:512], eb[:, 512:640], eb[:, 640:768]
        tv, ti, tif, tw, tden, yr = (gqm[:, a:b] for a, b in ((0, 64), (64, 128), (128, 160), (160, 192), (192, 200), (200, 232)))

        landed = [sem(f"landed{i}") for i in range(R)]
        hi_ready = sem("hi_ready")
        lo_ready = sem("lo_ready")
        used = sem("used")
        x_in = sem("x_in")
        edges_in = sem("edges_in")
        small_in = sem("small_in")
        wq_in = sem("wq_in")
        wk_in = sem("wk_in")
        brow_in = sem("brow_in")
        as2_in = sem("as2_in")
        ad2_in = sem("ad2_in")
        ga_in = sem("ga_in")
        fw_in = sem("fw_in")
        g2_in = sem("g2_in")
        out_in = sem("out_in")
        pool_chain = sem("pool_chain")
        consts = sem("consts")
        dve_chain = sem("dve_chain")
        onehots = sem("onehots")
        count_out = sem("count_out")
        ln_var = sem("ln_var")
        ln_rstd = sem("ln_rstd")
        xn_ready = sem("xn_ready")
        xT_out = sem("xT_out")
        xTh_ready = sem("xTh_ready")
        xTl_ready = sem("xTl_ready")
        qkv_copied = sem("qkv_copied")
        mix_pe = sem("mix_pe")
        mix_dve = sem("mix_dve")
        mix_act = sem("mix_act")
        h_copied = sem("h_copied")
        hb_out = sem("hb_out")
        hT_out = sem("hT_out")
        hT_copied = sem("hT_copied")
        al_out = sem("al_out")
        diag_ready = sem("diag_ready")
        E_out = sem("E_out")
        score_ready = sem("score_ready")
        exp_done = sem("exp_done")
        A_ready = sem("A_ready")
        AT_out = sem("AT_out")
        AT_copied = sem("AT_copied")
        agg_out = sem("agg_out")
        y_ready = sem("y_ready")
        ey_done = sem("ey_done")
        elu_ready = sem("elu_ready")
        oTh_ready = sem("oTh_ready")
        oTl_ready = sem("oTl_ready")
        g_copied = sem("g_copied")
        F_out = sem("F_out")
        x_ready = sem("x_ready")
        router_out = sem("router_out")
        rexp_done = sem("rexp_done")
        rscore = sem("rscore")
        comb_ready = sem("comb_ready")
        silu_done = sem("silu_done")
        hh_ready = sem("hh_ready")
        T_out = sem("T_out")
        hTh_ready = sem("hTh_ready")
        hTl_ready = sem("hTl_ready")
        l1_pe = sem("l1_pe")
        l1_act = sem("l1_act")
        l1_dve = sem("l1_dve")
        l1_pool = sem("l1_pool")
        f_pe = sem("f_pe")
        f_act = sem("f_act")
        f_dve = sem("f_dve")
        f_pool = sem("f_pool")
        hid_out = sem("hid_out")
        gelu_done = sem("gelu_done")
        Y_out = sem("Y_out")
        Y_read = sem("Y_read")

        def wait(eng, s, v):
            if not (isinstance(v, int) and v <= 0):
                eng.wait_ge(s, v)

        class Chain:

            def __init__(self, eng, s):
                self.eng, self.s, self.base, self.k = eng, s, 0, 0

            def link(self, ins):
                self.k += 1
                ins.then_inc(self.s, 1)
                self.eng.wait_ge(self.s, self.base + self.k)

        block = ctx.enter_context(nc.Block())

        @block.sync
        def _(sp):
            def load(c, k, land_extra=0):
                n = chunk_len(k)
                sp.dma_start(raw[:, k % R, 0:n], stream_d[c, :, 0:n] if isinstance(c, int)
                             else stream_d[bass.ds(c, 1), :, 0:n].rearrange("a p n -> (a p) n")).then_inc(landed[k % R], 16)

            sp.dma_start(xres[:], x_d).then_inc(x_in, 16)
            sp.dma_start(edg[:, 0:16].bitcast(I32), src_d).then_inc(edges_in, 16)
            sp.dma_start(edg[:, 16:32].bitcast(I32), dst_d).then_inc(edges_in, 16)
            for c in range(R):
                load(c, c)
            for c in range(R, 9):
                sp.wait_ge(lo_ready, c - R + 1)
                load(c, c)
            with sp.Fori(9, TAIL0, R) as c:
                for k in range(R):
                    sp.wait_ge(lo_ready, c + (k - R + 1))
                    load(c + k, 9 + k)
            for c in range(TAIL0, 34):
                if c == 28:
                    sp.wait_ge(mix_dve, 9)
                    sp.dma_start(pa[:, 0:D], a2b_d[:, 0:D]).then_inc(as2_in, 16)
                    sp.dma_start(qkv[:, D:2 * D], a2b_d[:, D:2 * D]).then_inc(ad2_in, 16)
                sp.wait_ge(lo_ready, c - R + 1)
                load(c, c)
            with sp.Fori(34, L1 - 1, R) as c:
                for k in range(R):
                    sp.wait_ge(lo_ready, c + (k - R + 1))
                    load(c + k, 34 + k)
            for c in range(L1 - 1, NCH):
                if c == L1:
                    sp.wait_ge(x_ready, 1)
                    sp.dma_start(pa[:, 0:1024], ga_d).then_inc(ga_in, 16)
                sp.wait_ge(lo_ready, c - R + 1)
                load(c, c)
            sp.wait_ge(lo_ready, L1 + 6)
            sp.dma_start(fbase[:, 0:NF], fw_d).then_inc(fw_in, 16)
            sp.wait_ge(l1_pe, 5)
            sp.dma_start(qkv[:, 0:2 * D], g2_d).then_inc(g2_in, 16)
            sp.wait_ge(x_ready, 4)
            sp.dma_start(out_d, xres[:]).then_inc(out_in, 16)
            sp.wait_ge(out_in, 16)

        @block.gpsimd
        def _(pool):
            ch = Chain(pool, pool_chain)
            ch.link(nc.gpsimd.memset(ident[:], 0.0))
            nc.gpsimd.affine_select(out=ident[:], in_=ident[:], compare_op=ALU.not_equal, fill=1.0, base=0,
                                    pattern=[[-1, P]], channel_multiplier=1).then_inc(consts, 1)
            nc.gpsimd.memset(ones[:], 1.0).then_inc(consts, 1)
            nc.gpsimd.iota(iota[:], pattern=[[1, P]], base=0, channel_multiplier=0,
                           allow_small_or_imprecise_dtypes=True).then_inc(consts, 1)
            nc.gpsimd.memset(mhalf, -0.5).then_inc(consts, 1)
            ch.link(nc.gpsimd.memset(hm, 0.0))
            nc.gpsimd.memset(brow[96:97, :], 0.0).then_inc(consts, 1)
            nc.gpsimd.affine_select(out=hm.rearrange("p (h c) -> p h c", c=64),
                                    in_=hm.rearrange("p (h c) -> p h c", c=64),
                                    compare_op=ALU.not_equal, fill=1.0, base=0,
                                    pattern=[[-1, 12], [0, 64]], channel_multiplier=1).then_inc(consts, 1)

            def rsqrt(n):
                pool.wait_ge(ln_var, n)
                nc.gpsimd.tensor_tensor(rstd, veps, mhalf[:, 0:1], ALU.pow).then_inc(ln_rstd, 1)

            pool.wait_ge(consts, 6)
            rsqrt(1)
            rsqrt(2)
            rsqrt(3)
            pool.wait_ge(l1_dve, 2)
            nc.gpsimd.tensor_tensor(stat[:, 112:124], stat[:, 100:112], mhalf, ALU.pow).then_inc(l1_pool, 1)
            pool.wait_ge(lo_ready, NCH - 1)
            pool.wait_ge(l1_pe, 12)
            for i, slot in enumerate((5, 0, 1)):
                ch.link(nc.gpsimd.memset(raw[:, slot, :], 0.0))
            pool.wait_ge(fw_in, 16)
            w2 = fw("W2").rearrange("p (b r) -> p b r", r=16)
            for i, slot in enumerate((5, 0, 1)):
                nb = min(48, P - 48 * i)
                bd = raw[:, slot, 0:nb * 64].rearrange("p (b m r) -> p b m r", m=4, r=16)
                for m in range(4):
                    ch.link(nc.gpsimd.tensor_copy(bd[32 * m:32 * m + 32, :, m, :],
                                                  w2[32 * m:32 * m + 32, 48 * i:48 * i + nb, :]))
            nc.gpsimd.memset(mhalf[:, 0:1], -0.5).then_inc(f_pool, 1)
            pool.wait_ge(f_pool, 1)
            rsqrt(4)

        @block.scalar
        def _(act):
            def hi(c, k, land, need=None):
                n = chunk_len(k)
                act.wait_ge(landed[k % R], land)
                need = c - S + 1 if need is None else need
                wait(act, used, need)
                nc.scalar.activation(whi[:, k % S, 0:n], raw[:, k % R, 0:n], ACT.Copy).then_inc(hi_ready, 1)

            def his(c):
                hi(c, c, landed_at(c))

            def copy(out, in_, s):
                nc.scalar.activation(out, in_, ACT.Copy).then_inc(s, 1)

            def xT_hi(n):
                act.wait_ge(xT_out, n)
                copy(xTh[:].rearrange("p (a b) n -> p a (b n)", a=2), ps[:, 2:4, 0:HALF], xTh_ready)

            act.dma_start(small[:], small_d).then_inc(small_in, 16)
            act.dma_start(pa[:, 0:D], wqb_d).then_inc(wq_in, 16)
            act.dma_start(brow[0:2, :], brow_d[0:2, :]).then_inc(brow_in, 16)
            act.dma_start(brow[32:34, :], brow_d[2:4, :]).then_inc(brow_in, 16)
            act.dma_start(brow[64:65, :], brow_d[4:5, :]).then_inc(brow_in, 16)

            act.dma_start(wkm, wk_d).then_inc(wk_in, 16)

            def qkv_copy(i, bank):
                act.wait_ge(used, i + 1)
                n = 512 if i < 4 else 256
                copy(qkv[:, 512 * i:512 * i + n], ps[:, bank, 0:n], qkv_copied)

            def mix_softmax(n):
                act.wait_ge(mix_dve, n)
                nc.scalar.activation(awt[:], ps[0:12, 5, 128:256], ACT.Exp, bias=mst[0:12, 1:2], scale=0.125,
                                     accum_out=mst[0:12, 2:3]).then_inc(mix_act, 1)

            def h_copy(h, d, part, s, v):
                act.wait_ge(s, v)
                wait(act, agg_out, h - 1)
                n = 512 if part == 0 else 256
                copy(hsb[:, d, 512 * part:512 * part + n], ps[:, part, 0:n], h_copied)

            def soft_exp(n):
                act.wait_ge(score_ready, n)
                nc.scalar.activation(zt1, zt1, ACT.Exp, bias=nm[:, 0:1]).then_inc(exp_done, 1)

            def AT_copy(n):
                act.wait_ge(AT_out, n)
                copy(ATs, ps[:, 4, 128:256], AT_copied)

            def hT_copy(h):
                act.wait_ge(hT_out, h + 1)
                wait(act, al_out, h)
                copy(hTs[:, 0:512], ps[:, 7, :], hT_copied)
                copy(hTs[:, 512:768], ps[:, 4, 256:512], hT_copied)

            def elu_exp(n):
                act.wait_ge(y_ready, n)
                nc.scalar.activation(eb[:], yb[:], ACT.Exp).then_inc(ey_done, 1)

            def o_hi(n, free):
                act.wait_ge(elu_ready, n)
                wait(act, used, free)
                copy(oTh[:], yb[:], oTh_ready)

            xT_hi(1)
            his(0)
            his(1)
            his(2)
            act.wait_ge(count_out, 1)
            qkv_copy(0, 0)
            his(3)
            qkv_copy(1, 1)
            his(4)
            qkv_copy(2, 2)
            mix_softmax(2)
            his(5)
            qkv_copy(3, 3)
            act.wait_ge(mix_pe, 2)
            copy(mixa, ps[:, 5, 256:268], mix_act)
            his(6)
            qkv_copy(4, 7)
            his(7)
            h_copy(0, 0, 0, used, 6)
            his(8)
            h_copy(0, 0, 1, used, 7)
            hT_copy(0)
            mix_softmax(6)
            his(9)
            h_copy(1, 1, 0, used, 8)
            act.wait_ge(mix_pe, 6)
            copy(mixa, ps[:, 5, 256:268], mix_act)
            his(10)
            soft_exp(1)
            h_copy(1, 1, 1, used, 9)
            AT_copy(1)
            hT_copy(1)
            elu_exp(1)
            o_hi(1, 0)

            def step(h, c, d, k, land):
                hi(c + 2, k + 2, land(k + 2))
                h_copy(h, d, 0, used, c + 1)
                soft_exp(h)
                h_copy(h, d, 1, hb_out, h - 1)
                hi(c + 3, k + 3, land(k + 3))
                AT_copy(h)
                hi(c + 4, k + 4, land(k + 4))
                hT_copy(h)
                elu_exp(h)
                o_hi(h, c + 3)

            with act.Fori(2, H0, 2) as h:
                for d in range(2):
                    step(h + d, 3 * h + (3 + 3 * d), d, 9 + 3 * d, lambda k: 8 * h + (landed_at(k) - 16))

            soft_exp(8)
            his(29)
            AT_copy(8)
            elu_exp(8)
            o_hi(8, 28)
            act.wait_ge(mix_pe, 9)
            copy(xTh[:].rearrange("p b n -> p (b n)")[:, 0:512], ps[:, 7, :], mix_act)
            copy(xTh[:].rearrange("p b n -> p (b n)")[:, 512:768], ps[:, 4, 256:512], mix_act)
            hi(30, 30, landed_at(30), need=30)
            hi(31, 31, landed_at(31), need=30)
            hi(32, 32, landed_at(32), need=30)
            his(33)
            act.wait_ge(used, 32)
            copy(hsb[:, 0, :].rearrange("p (a n) -> p a n", a=2), ps[:, 5:7, 0:HALF], g_copied)
            soft_exp(9)
            AT_copy(9)
            xT_hi(2)
            act.wait_ge(rscore, 1)
            nc.scalar.activation(stat[:, 128:136], stat[:, 128:136], ACT.Exp, bias=nm[:, 0:1],
                                 accum_out=den[:, 0:1]).then_inc(rexp_done, 1)

            def silu(j, d, done):
                act.wait_ge(used, done)
                wait(act, hh_ready, j - 1)
                nc.scalar.activation(asb[d], ps[:, d, :], ACT.Silu).then_inc(silu_done, 1)

            def hT_hi(j, free):
                act.wait_ge(T_out, j + 1)
                act.wait_ge(used, free)
                copy(oTh[:, 0:FB], ps[:, 4, :], hTh_ready)

            his(34)
            silu(0, 0, 33)
            his(35)

            def fstep(j, c, d, k, land):
                hi(c + 2, k + 2, land(k + 2))
                silu(j, d, c + 1)
                hT_hi(j - 1, c)
                hi(c + 3, k + 3, land(k + 3))
                hi(c + 4, k + 4, land(k + 4))

            with act.Fori(1, FS, 2) as j:
                for d in range(2):
                    fstep(j + d, 3 * j + (31 + 3 * d), 1 - d, 34 + 3 * d,
                          lambda k: 8 * j + (landed_at(k) - 8))
            hT_hi(FS - 1, L1 - 1)
            his(L1 + 1)
            xT_hi(3)
            his(L1 + 2)

            def l1_copy(out, in_, n, s=l1_pe):
                act.wait_ge(s, n)
                copy(out, in_, l1_act)

            def relu2(out, col, name, n):
                act.wait_ge(l1_pe, n)
                for b in range(2):
                    nc.scalar.activation(out[:, b * P:(b + 1) * P], ps[:, 7, col + b * P:col + (b + 1) * P], ACT.Relu,
                                         bias=sm(name)[:, b:b + 1]).then_inc(l1_act, 1)

            halves = lambda t: t.rearrange("p (a n) -> p a n", a=2)
            l1_copy(qkv[:, 0:512], ps[:, 0, :], L1 + 1, used)
            l1_copy(gqm[:, 0:256], ps[:, 5, 0:256], L1 + 2, used)
            his(L1 + 3)
            l1_copy(qkv[:, 512:1024], ps[:, 1, :], L1 + 3, used)
            his(L1 + 4)
            act.wait_ge(score_ready, 10)
            for h in range(4):
                nc.scalar.activation(L1Z[:, h * P:(h + 1) * P], L1Z[:, h * P:(h + 1) * P], ACT.Exp,
                                     bias=nm[:, h:h + 1]).then_inc(exp_done, 1)
            l1_copy(qkv[:, 1024:1536], ps[:, 2, :], L1 + 4, used)
            his(L1 + 5)
            l1_copy(qkv[:, 1536:2048], ps[:, 3, :], L1 + 5, used)
            l1_copy(L1AT, ps[:, 6, :], 2)
            his(L1 + 6)
            l1_copy(qkv[:, 2048:2304], ps[:, 4, 0:256], L1 + 6, used)
            relu2(gT, 0, "gb1", 3)
            l1_copy(halves(qT), ps[:, 0:2, 0:HALF], 4)
            l1_copy(halves(kT), ps[:, 2:4, 0:HALF], 5)
            l1_copy(gqm[:, 256:512], ps[:, 5, 256:512], 6)
            l1_copy(halves(vT), ps[:, 0:2, 0:HALF], 7)
            his(L1 + 7)
            act.wait_ge(score_ready, 11)
            nc.scalar.activation(L1Z[:, 0:P], L1Z[:, 0:P], ACT.Exp, bias=nm[:, 0:1]).then_inc(exp_done, 1)
            l1_copy(L1AT[:, 0:P], ps[:, 6, 0:P], 9)
            relu2(gT, 0, "gb2", 10)
            relu2(gT2, 256, "bm1", 11)
            act.wait_ge(l1_dve, 3)
            copy(xTh[:].rearrange("p b n -> p (b n)"), qT, l1_act)

            act.wait_ge(xT_out, 4)
            copy(hTs[:].rearrange("p (a n) -> p a n", a=2), ps[:, 2:4, 0:HALF], f_act)
            act.wait_ge(f_pe, 2)
            copy(zT, ps[:, 3, 0:256], f_act)
            act.wait_ge(f_pe, 3)
            copy(scs, ps[:, 4, :], f_act)
            act.wait_ge(f_dve, 2)
            nc.scalar.activation(tw, tw, ACT.Exp).then_inc(f_act, 1)
            act.wait_ge(f_pe, 4)
            copy(wT, ps[:, 4, :], f_act)
            for w in range(8):
                for s4 in range(4):
                    act.wait_ge(hid_out, 4 * w + s4 + 1)
                    wait(act, Y_out, 4 * (w - 1) + s4 + 1)
                    nc.scalar.activation(hg[s4], ps[:, s4, :], ACT.Gelu_apprx_tanh).then_inc(gelu_done, 1)
            act.wait_ge(f_pe, 6)
            copy(cT, ps[:, 0, 0:P], f_act)
            for b in range(2):
                act.wait_ge(f_pe, 7)
                nc.scalar.activation(fT[:, b * P:(b + 1) * P], ps[:, 1, b * P:(b + 1) * P], ACT.Gelu_apprx_tanh,
                                     bias=sm("fg1b")[:, b:b + 1]).then_inc(f_act, 1)

        @block.vector
        def _(dve):
            ch = Chain(dve, dve_chain)
            link = ch.link
            V = nc.vector

            def lo(c, k):
                n = chunk_len(k)
                dve.wait_ge(hi_ready, c + 1)
                V.tensor_tensor(wlo[:, k % S, 0:n], raw[:, k % R, 0:n], whi[:, k % S, 0:n].bitcast(F32),
                                ALU.subtract).then_inc(lo_ready, 1)

            def los(c):
                lo(c, c)

            def layernorm(n):
                V.bn_stats(bst[:, 0:6], xres[:, 0:HALF])
                link(V.bn_stats(bst[:, 6:12], xres[:, HALF:D]))
                link(V.bn_aggr(mv, bst))
                V.tensor_scalar(veps, mv[:, 1:2], EPS, None, ALU.add).then_inc(ln_var, 1)
                dve.wait_ge(ln_rstd, n)
                V.tensor_scalar(xn[:], xres[:], mv[:, 0:1], rstd, ALU.subtract, ALU.mult).then_inc(xn_ready, 1)

            def xT_lo(n):
                dve.wait_ge(xTh_ready, n)
                V.tensor_tensor(xTl[:].rearrange("p (a b) n -> p a (b n)", a=2), ps[:, 2:4, 0:HALF],
                                xTh[:].bitcast(F32).rearrange("p (a b) n -> p a (b n)", a=2),
                                ALU.subtract).then_inc(xTl_ready, 1)

            dve.wait_ge(x_in, 16)
            layernorm(1)
            dve.wait_ge(edges_in, 32)
            dve.wait_ge(consts, 6)
            link(V.tensor_copy(edg, edg.bitcast(I32)))
            for t in range(16):
                V.tensor_scalar(soh[:, t, :], iota[:], edg[:, t:t + 1], None, ALU.is_equal)
                ins = V.tensor_scalar(doh[:, t, :], iota[:], edg[:, 16 + t:17 + t], None, ALU.is_equal)
            ins.then_inc(onehots, 1)
            xT_lo(1)
            los(0)
            dve.wait_ge(count_out, 1)
            link(V.tensor_tensor(cnt[:], ps[:, 4, 0:P], ident[:], ALU.add))
            V.tensor_scalar(cneg[:], cnt[:], 0.5, BIG, ALU.is_lt, ALU.mult)
            los(1)
            dve.wait_ge(wk_in, 16)
            link(V.tensor_tensor(wkm, wkm, hm, ALU.mult))
            los(2)

            def head_scores():
                V.tensor_reduce(mixa, xn[:].rearrange("p (h c) -> p h c", c=64), AX, ALU.add).then_inc(mix_dve, 1)

            halves = lambda t: t.rearrange("p (a n) -> p a n", a=2)

            def mix_max(n_pe):
                dve.wait_ge(mix_pe, n_pe)
                link(V.tensor_reduce(mst[0:12, 0:1], ps[0:12, 5, 128:256], AX, ALU.max))
                V.tensor_scalar(mst[0:12, 1:2], mst[0:12, 0:1], -0.125, None, ALU.mult).then_inc(mix_dve, 1)

            def mix_norm(n_act):
                dve.wait_ge(mix_act, n_act)
                link(V.reciprocal(mst[0:12, 3:4], mst[0:12, 2:3]))
                V.tensor_scalar(awt[:], awt[:], mst[0:12, 3:4], None, ALU.mult).then_inc(mix_dve, 1)

            dve.wait_ge(wq_in, 16)
            dve.wait_ge(qkv_copied, 2)
            link(V.tensor_tensor(xn[:], qkv[:, 0:D], pa[:, 0:D], ALU.mult))
            head_scores()
            los(3)
            mix_max(1)
            mix_norm(1)
            los(4)
            los(5)
            los(6)
            dve.wait_ge(mix_pe, 3)
            V.tensor_tensor(halves(gqm[0:12, :]), ps[0:12, 5:7, 0:HALF], halves(wkm), ALU.mult).then_inc(mix_dve, 1)
            los(7)
            dve.wait_ge(qkv_copied, 3)
            dve.wait_ge(mix_pe, 4)
            link(V.tensor_tensor(halves(xn[:]), ps[:, 5:7, 0:HALF], halves(qkv[:, D:2 * D]), ALU.mult))
            head_scores()
            los(8)

            def alpha_diag(h):
                dve.wait_ge(al_out, h + 1)
                wait(dve, E_out, h)
                link(V.tensor_copy(al[:, 0:2], ps[:, 4, 0:2]))
                V.tensor_scalar(dg, ident[:], al[:, 0:1], None, ALU.mult).then_inc(diag_ready, 1)

            def scores(n, e_ap, z, ad):
                dve.wait_ge(E_out, n)
                link(V.tensor_scalar(z, e_ap, ad, None, ALU.add))
                link(V.scalar_tensor_tensor(z, z, 0.2, z, ALU.mult, ALU.max))
                link(V.tensor_tensor(z, z, cneg[:], ALU.add))
                link(V.tensor_reduce(mx[:, 0:1], z, AX, ALU.max))
                V.tensor_scalar(nm[:, 0:1], mx[:, 0:1], -1.0, None, ALU.mult).then_inc(score_ready, 1)

            def weights(n, z):
                dve.wait_ge(exp_done, n)
                link(V.tensor_tensor(z, z, cnt[:], ALU.mult))
                link(V.tensor_reduce(den[:, 0:1], z, AX, ALU.add))
                link(V.reciprocal(rcp[:, 0:1], den[:, 0:1]))
                V.tensor_scalar(z, z, rcp[:, 0:1], None, ALU.mult).then_inc(A_ready, 1)

            def bias_add(h):
                dve.wait_ge(agg_out, h + 1)
                a0 = PC["b1T"][0]
                for half in range(2):
                    b = (small[:, a0 + 6 * h + 3 * half:a0 + 6 * h + 3 * half + 3] if isinstance(h, int)
                         else small[:, bass.ds(h * 6 + (a0 + 3 * half), 3)])
                    ins = V.tensor_tensor(yb[:, HALF * half:HALF * (half + 1)].rearrange("p (b n) -> p b n", n=P),
                                          ps[:, 2 + half, 0:HALF].rearrange("p (b n) -> p b n", n=P),
                                          b.unsqueeze(2).broadcast_to([P, 3, P]), ALU.add)
                ins.then_inc(y_ready, 1)

            def elu(n):
                dve.wait_ge(ey_done, n)
                link(V.tensor_scalar(eb[:], eb[:], 1.0, -1.0, ALU.min, ALU.add))
                V.scalar_tensor_tensor(yb[:], yb[:], 0.0, eb[:], ALU.max, ALU.add).then_inc(elu_ready, 1)

            def o_lo(n):
                dve.wait_ge(oTh_ready, n)
                V.tensor_tensor(oTl[:], yb[:], oTh[:].bitcast(F32), ALU.subtract).then_inc(oTl_ready, 1)

            def bias_add(h):
                dve.wait_ge(agg_out, h + 1)
                a0 = PC["b1T"][0]
                for half in range(2):
                    b = (small[:, a0 + 6 * h + 3 * half:a0 + 6 * h + 3 * half + 3] if isinstance(h, int)
                         else small[:, bass.ds(h * 6 + (a0 + 3 * half), 3)])
                    ins = V.tensor_tensor(yb[:, HALF * half:HALF * (half + 1)].rearrange("p (b n) -> p b n", n=P),
                                          ps[:, 2 + half, 0:HALF].rearrange("p (b n) -> p b n", n=P),
                                          b.unsqueeze(2).broadcast_to([P, 3, P]), ALU.add)
                    ins.then_inc(y_ready, 1) if half else None

            mix_max(5)
            mix_norm(3)
            alpha_diag(0)
            los(9)
            scores(1, ps[:, 4, P:2 * P], zt1, al[:, 1:2])
            weights(1, zt1)
            los(10)
            dve.wait_ge(mix_pe, 7)
            V.tensor_tensor(halves(gqm[0:12, :]), ps[0:12, 5:7, 0:HALF], halves(hm), ALU.mult).then_inc(mix_dve, 1)
            dve.wait_ge(mix_pe, 8)
            dve.wait_ge(qkv_copied, 5)
            V.tensor_tensor(halves(qkv[:, 2 * D:3 * D]), ps[:, 5:7, 0:HALF], halves(qkv[:, 2 * D:3 * D]),
                            ALU.mult).then_inc(mix_dve, 1)
            bias_add(0)
            elu(1)
            o_lo(1)
            alpha_diag(1)

            def step(h, c, d, k):
                lo(c + 2, k + 2)
                scores(h, ps[:, 4, P:2 * P], zt1, al[:, 1:2])
                weights(h, zt1)
                lo(c + 3, k + 3)
                lo(c + 4, k + 4)
                bias_add(h - 1)
                elu(h)
                o_lo(h)
                alpha_diag(h)

            per = 2 * (4 + 3 + 1 + 1)
            k0 = ch.k
            with dve.Fori(2, H0, 2) as h:
                ch.base, ch.k = (per // 2) * h + (k0 - per), 0
                for d in range(2):
                    step(h + d, 3 * h + (3 + 3 * d), d, 9 + 3 * d)
                assert ch.k == per
            ch.base, ch.k = 0, k0 + per * (H0 - 2) // 2

            scores(8, ps[:, 4, P:2 * P], zt1, al[:, 1:2])
            weights(8, zt1)
            los(29)
            bias_add(7)
            elu(8)
            o_lo(8)
            dve.wait_ge(mix_act, 6)
            V.tensor_tensor(xTl[:].rearrange("p b n -> p (b n)")[:, 0:512], ps[:, 7, :],
                            xTh[:].rearrange("p b n -> p (b n)")[:, 0:512].bitcast(F32), ALU.subtract)
            V.tensor_tensor(xTl[:].rearrange("p b n -> p (b n)")[:, 512:768], ps[:, 4, 256:512],
                            xTh[:].rearrange("p b n -> p (b n)")[:, 512:768].bitcast(F32), ALU.subtract).then_inc(mix_dve, 1)
            los(30)
            los(31)
            los(32)
            link(V.tensor_tensor(xres[:], xres[:], qkv[:, 0:D], ALU.add))
            dve.wait_ge(as2_in, 16)
            dve.wait_ge(ad2_in, 16)
            dve.wait_ge(g_copied, 1)
            for i, a in enumerate((pa[:, 0:D], qkv[:, D:2 * D])):
                link(V.tensor_tensor(eb[:], hsb[:, 0, :], a, ALU.mult))
                link(V.tensor_reduce(al[:, i:i + 1], eb[:], AX, ALU.add))
            V.tensor_scalar(dg, ident[:], al[:, 0:1], None, ALU.mult).then_inc(diag_ready, 1)
            scores(9, ps[:, 4, P:2 * P], zt1, al[:, 1:2])
            weights(9, zt1)
            los(33)

            def residual(n, b0, s, v):
                dve.wait_ge(s, v)
                V.tensor_tensor(xres[:].rearrange("p (a n) -> p a n", a=2), ps[:, b0:b0 + 2, 0:HALF],
                                xres[:].rearrange("p (a n) -> p a n", a=2), ALU.add).then_inc(x_ready, 1)
                dve.wait_ge(x_ready, n)

            residual(1, 0, F_out, 1)
            layernorm(2)
            xT_lo(2)

            sc = stat[:, 128:136]
            sel = stat[:, 136:144]
            v8 = stat[:, 144:152]
            dve.wait_ge(router_out, 1)
            link(V.tensor_copy(sc, ps[:, 7, 0:8]))
            link(V.tensor_reduce(mx[:, 0:1], sc, AX, ALU.max))
            V.tensor_scalar(nm[:, 0:1], mx[:, 0:1], -1.0, None, ALU.mult).then_inc(rscore, 1)
            dve.wait_ge(rexp_done, 1)
            link(V.reciprocal(rcp[:, 0:1], den[:, 0:1]))
            link(V.tensor_scalar(sc, sc, rcp[:, 0:1], None, ALU.mult))
            link(V.tensor_tensor(sel, sc, sm("ebias"), ALU.add))
            link(V.max(v8, sel))
            link(V.max_index(stat[:, 152:160].bitcast(U32), v8, sel))
            link(V.tensor_copy(v8[:, 0:2], stat[:, 152:154].bitcast(U32)))
            link(V.tensor_scalar(sel, iota[:, 0:8], v8[:, 0:1], None, ALU.is_equal))
            link(V.scalar_tensor_tensor(sel, iota[:, 0:8], v8[:, 1:2], sel, ALU.is_equal, ALU.add))
            link(V.tensor_tensor(sel, sel, sc, ALU.mult))
            link(V.tensor_reduce(den[:, 0:1], sel, AX, ALU.add))
            link(V.tensor_scalar(den[:, 0:1], den[:, 0:1], 1e-9, None, ALU.add))
            link(V.reciprocal(rcp[:, 0:1], den[:, 0:1]))
            link(V.memset(comb[:, 24:27], 1.0))
            link(V.tensor_scalar(comb[:, 0:24].rearrange("p (e t) -> p e t", t=3),
                                 sel.unsqueeze(2).broadcast_to([P, 8, 3]), rcp[:, 0:1], None, ALU.mult))

            def hT_lo(j):
                dve.wait_ge(hTh_ready, j + 1)
                V.tensor_tensor(oTl[:, 0:FB], ps[:, 4, :], oTh[:, 0:FB].bitcast(F32), ALU.subtract).then_inc(hTl_ready, 1)

            def hid(j, d, done):
                dve.wait_ge(silu_done, j + 1)
                dve.wait_ge(used, done)
                wait(dve, T_out, j - 1)
                cj = comb[:, j:j + 1] if isinstance(j, int) else stat[:, bass.ds(j + 51, 1)]
                V.scalar_tensor_tensor(hhb[d], asb[d], cj, ps[:, 2 + d, :], ALU.mult, ALU.mult).then_inc(hh_ready, 1)

            los(34)
            hid(0, 0, 34)
            los(35)

            def fstep(j, c, d, k):
                lo(c + 2, k + 2)
                hT_lo(j - 1)
                lo(c + 3, k + 3)
                hid(j, d, c + 2)
                lo(c + 4, k + 4)

            with dve.Fori(1, FS, 2) as j:
                for d in range(2):
                    fstep(j + d, 3 * j + (31 + 3 * d), 1 - d, 34 + 3 * d)
            hT_lo(FS - 1)
            residual(2, 5, used, L1)
            layernorm(3)
            los(L1 + 1)
            xT_lo(3)

            los(L1 + 2)
            dve.wait_ge(ga_in, 16)
            dve.wait_ge(l1_act, 2)
            al4 = [al[:, 0:4], al[:, 4:8]]
            for i in range(2):
                link(V.tensor_tensor(eb[:, 0:256], gqm[:, 0:256], pa[:, 256 * i:256 * i + 256], ALU.mult))
                link(V.tensor_reduce(al4[i], eb[:, 0:256].rearrange("p (h c) -> p h c", c=64), AX, ALU.add))
            for h in range(4):
                ins = V.tensor_scalar(L1D[:, h * P:(h + 1) * P], ident[:], al[:, h:h + 1], None, ALU.mult)
            ins.then_inc(diag_ready, 1)
            los(L1 + 3)
            dve.wait_ge(l1_pe, 1)
            hd = lambda t, h: t[:, h * P:(h + 1) * P]
            for h in range(4):
                ins = V.tensor_scalar(hd(L1Z, h), ps[:, 6, h * P:(h + 1) * P], al[:, 4 + h:5 + h], None, ALU.add)
            link(ins)
            link(V.scalar_tensor_tensor(L1Z, L1Z, 0.2, L1Z, ALU.mult, ALU.max))
            for h in range(4):
                ins = V.tensor_tensor(hd(L1Z, h), hd(L1Z, h), cneg[:], ALU.add)
            link(ins)
            link(V.tensor_reduce(mx, L1Z.rearrange("p (h n) -> p h n", n=P), AX, ALU.max))
            V.tensor_scalar(nm, mx, -1.0, None, ALU.mult).then_inc(score_ready, 1)
            dve.wait_ge(exp_done, 13)
            for h in range(4):
                ins = V.tensor_tensor(hd(L1Z, h), hd(L1Z, h), cnt[:], ALU.mult)
            link(ins)
            link(V.tensor_reduce(den, L1Z.rearrange("p (h n) -> p h n", n=P), AX, ALU.add))
            link(V.tensor_scalar(den, den, 1e-16, None, ALU.add))
            link(V.reciprocal(rcp, den))
            for h in range(4):
                ins = V.tensor_scalar(hd(L1Z, h), hd(L1Z, h), rcp[:, h:h + 1], None, ALU.mult)
            ins.then_inc(A_ready, 1)
            los(L1 + 4)
            los(L1 + 5)
            los(L1 + 6)
            dve.wait_ge(l1_act, 12)
            for i in range(2):
                link(V.tensor_tensor(eb[:, 0:256], gqm[:, 256:512], pa[:, 512 + 256 * i:768 + 256 * i], ALU.mult))
                link(V.tensor_reduce(al[:, i:i + 1], eb[:, 0:256], AX, ALU.add))
            V.tensor_scalar(hd(L1D, 0), ident[:], al[:, 0:1], None, ALU.mult).then_inc(diag_ready, 1)
            sums = stat[:, 124:136]
            sq = stat[:, 100:112]
            rn = stat[:, 112:124]
            for i, t in enumerate((qT, kT)):
                link(V.tensor_reduce(sums[:, 6 * i:6 * i + 6], t.rearrange("p (b n) -> p b n", n=P), AX, ALU.add))
                link(V.tensor_tensor(eb[:], t, t, ALU.mult))
                ins = V.tensor_reduce(sq[:, 6 * i:6 * i + 6], eb[:].rearrange("p (b n) -> p b n", n=P), AX, ALU.add)
                ins.then_inc(l1_dve, 1)
            dve.wait_ge(l1_dve, 2)
            dve.wait_ge(l1_pe, 8)
            z = hd(L1Z, 0)
            link(V.tensor_scalar(z, ps[:, 6, 0:P], al[:, 1:2], None, ALU.add))
            link(V.scalar_tensor_tensor(z, z, 0.2, z, ALU.mult, ALU.max))
            link(V.tensor_tensor(z, z, cneg[:], ALU.add))
            link(V.tensor_reduce(mx[:, 0:1], z, AX, ALU.max))
            V.tensor_scalar(nm[:, 0:1], mx[:, 0:1], -1.0, None, ALU.mult).then_inc(score_ready, 1)
            dve.wait_ge(l1_pool, 1)
            fct = stat[:, 136:142]
            link(V.tensor_tensor(sums, sums, rn, ALU.mult))
            link(V.tensor_tensor(fct, sums[:, 0:6], sums[:, 6:12], ALU.mult))
            link(V.tensor_scalar(fct, fct, float(N), None, ALU.add))
            link(V.reciprocal(fct, fct))
            link(V.tensor_tensor(rn[:, 0:6], rn[:, 0:6], fct, ALU.mult))
            dve.wait_ge(exp_done, 14)
            link(V.tensor_tensor(z, z, cnt[:], ALU.mult))
            link(V.tensor_reduce(den[:, 0:1], z, AX, ALU.add))
            link(V.tensor_scalar(den[:, 0:1], den[:, 0:1], 1e-16, None, ALU.add))
            link(V.reciprocal(rcp[:, 0:1], den[:, 0:1]))
            V.tensor_scalar(z, z, rcp[:, 0:1], None, ALU.mult).then_inc(A_ready, 1)
            b6 = lambda t: t.rearrange("p (b n) -> p b n", n=P)
            bc = lambda t: t.unsqueeze(2).broadcast_to([P, 6, P])
            link(V.tensor_tensor(b6(kT), b6(kT), bc(rn[:, 6:12]), ALU.mult))
            link(V.tensor_tensor(b6(qT), b6(qT), bc(rn[:, 0:6]), ALU.mult))
            link(V.tensor_tensor(qT, qT, kT, ALU.mult))
            dve.wait_ge(l1_act, 13)
            link(V.tensor_tensor(vT, vT, kT, ALU.mult))
            V.tensor_tensor(qT, qT, vT, ALU.mult).then_inc(l1_dve, 1)
            dve.wait_ge(l1_act, 19)
            V.tensor_tensor(xTl[:].rearrange("p b n -> p (b n)"), qT, xTh[:].rearrange("p b n -> p (b n)").bitcast(F32),
                            ALU.subtract).then_inc(l1_dve, 1)
            los(L1 + 7)
            residual(3, 2, F_out, 2)

            link(V.memset(zp, 0.0))
            V.memset(zp.rearrange("p (s c) -> p s c", c=32)[:, :, 16:17], 1.0)
            layernorm(4)
            dve.wait_ge(f_pe, 1)
            V.tensor_copy(zp.rearrange("p (s c) -> p s c", c=32)[:, :, 0:16],
                          ps[:, 6, 0:P].rearrange("p (s c) -> p s c", c=16)).then_inc(f_dve, 1)
            dve.wait_ge(f_act, 3)
            for s in range(8):
                ins = V.max(tv[:, 8 * s:8 * s + 8], scs[:, 64 * s:64 * s + 64])
            link(ins)
            v3 = tv.rearrange("p (s k) -> p s k", k=8)
            V.tensor_tensor(tw.rearrange("p (s k) -> p s k", k=4), v3[:, :, 0:4],
                            v3[:, :, 0:1].broadcast_to([P, 8, 4]), ALU.subtract).then_inc(f_dve, 1)
            for s in range(8):
                ins = V.max_index(ti[:, 8 * s:8 * s + 8].bitcast(U32), tv[:, 8 * s:8 * s + 8], scs[:, 64 * s:64 * s + 64])
            link(ins)
            link(V.tensor_copy(tif.rearrange("p (s k) -> p s k", k=4),
                               ti.bitcast(U32).rearrange("p (s k) -> p s k", k=8)[:, :, 0:4]))
            dve.wait_ge(f_act, 4)
            link(V.tensor_reduce(tden, tw.rearrange("p (s k) -> p s k", k=4), AX, ALU.add))
            link(V.reciprocal(tden, tden))
            link(V.tensor_tensor(tw.rearrange("p (s k) -> p s k", k=4), tw.rearrange("p (s k) -> p s k", k=4),
                                 tden.unsqueeze(2).broadcast_to([P, 8, 4]), ALU.mult))
            e3 = eq.rearrange("p (k m) -> p k m", m=64)
            for q in range(2):
                link(V.tensor_tensor(e3, iota[:, 0:64].unsqueeze(1).broadcast_to([P, 16, 64]),
                                     tif[:, 16 * q:16 * q + 16].unsqueeze(2).broadcast_to([P, 16, 64]), ALU.is_equal))
                link(V.tensor_tensor(e3, e3, tw[:, 16 * q:16 * q + 16].unsqueeze(2).broadcast_to([P, 16, 64]), ALU.mult))
                ins = V.tensor_reduce(ww[:, 256 * q:256 * q + 256].rearrange("p (s m) -> p s m", m=64),
                                      eq.rearrange("p (s k m) -> p s m k", k=4, m=64), AX, ALU.add)
                if q == 0:
                    link(ins)
            ins.then_inc(f_dve, 1)
            dve.wait_ge(f_dve, 3)
            dve.wait_ge(f_pe, 5)
            V.tensor_copy(cb, ps[:, 7, 0:P]).then_inc(f_dve, 1)
            dve.wait_ge(f_dve, 4)
            for w in range(8):
                g, jq = w // 4, w % 4
                for hf in range(2):
                    s = 4 * g + 2 * hf
                    dve.wait_ge(Y_out, 4 * w + 2 * hf + 2)
                    bank = 4 + 2 * (w % 2) + hf
                    wv = ww.rearrange("p (s j m) -> p s j m", j=4, m=16)[:, s:s + 2, jq, :]
                    link(V.tensor_tensor(yt.rearrange("p (s m r) -> p s m r", s=2, r=16),
                                         ps[:, bank, :].rearrange("p (s m r) -> p s m r", s=2, r=16),
                                         wv.unsqueeze(3).broadcast_to([P, 2, 16, 16]), ALU.mult))
                    link(V.tensor_reduce(yr.rearrange("p (s r) -> p s r", r=16), yt.rearrange("p (s m r) -> p s r m", s=2, r=16),
                                         AX, ALU.add))
                    ins = V.tensor_tensor(cb[:, 16 * s:16 * s + 32], cb[:, 16 * s:16 * s + 32], yr, ALU.add)
                    ins.then_inc(Y_read, 1)
                    dve.wait_ge(Y_read, 2 * w + hf + 1)
            residual(4, 2, F_out, 3)

        @block.tensor
        def _(pe):
            mm = nc.tensor.matmul

            def ready(c):
                pe.wait_ge(lo_ready, c + 1)

            def part3(out, sh, sl, wh, wl, first, last, shared=False):
                mm(out, sh, wh, start=first, stop=False, skip_group_check=shared)
                mm(out, sh, wl, start=False, stop=False, skip_group_check=shared)
                return mm(out, sl, wh, start=False, stop=last, skip_group_check=shared)

            def up(out, k, n, xh, xl):
                for t in range(KD):
                    ins = part3(out, xh[:, t, :], xl[:, t, :], whi[:, k % S, t * n:(t + 1) * n],
                                wlo[:, k % S, t * n:(t + 1) * n], t == 0, t == KD - 1)
                return ins

            def down(banks, k, off, ts, sh, sl, first=False, last=False):
                for i, t in enumerate(ts):
                    for half in range(2):
                        a = off + i * D + half * HALF
                        ins = part3(ps[:, banks[half], 0:HALF], sh[:, t * P:(t + 1) * P], sl[:, t * P:(t + 1) * P],
                                    whi[:, k % S, a:a + HALF], wlo[:, k % S, a:a + HALF],
                                    first and i == 0, last and i == len(ts) - 1)
                return ins

            def transpose6(src, n):
                pe.wait_ge(xn_ready, n)
                for b in range(KD):
                    ins = nc.tensor.transpose(ps[:, 2 + b // 3, (b % 3) * P:(b % 3 + 1) * P], src[:, b * P:(b + 1) * P], ident[:])
                ins.then_inc(xT_out, 1)

            def x_split(n):
                pe.wait_ge(xTh_ready, n)
                pe.wait_ge(xTl_ready, n)

            def bias(banks, row, n, first=False, last=False):
                pe.wait_ge(brow_in, 48)
                for half in range(2):
                    ins = mm(ps[:, banks[half], 0:HALF], ones[row:row + n, :], brow[row:row + n, half * HALF:(half + 1) * HALF],
                             start=first, stop=last)
                return ins

            pe.wait_ge(consts, 6)
            transpose6(xn, 1)
            pe.wait_ge(onehots, 1)
            for t in range(16):
                ins = mm(ps[:, 4, 0:P], doh[:, t, :], soh[:, t, :], start=t == 0, stop=t == 15)
            ins.then_inc(count_out, 1)

            def up_chunk(c, k, n, bank):
                ready(c)
                up(ps[:, bank, 0:n], k, n, xTh, xTl).then_inc(used, 1)

            def to_rows(v):
                pe.wait_ge(mix_dve, v)
                nc.tensor.transpose(ps[0:12, 5, 128:256], mixa, ident[:]).then_inc(mix_pe, 1)

            def to_columns(v):
                pe.wait_ge(mix_dve, v)
                nc.tensor.transpose(ps[:, 5, 256:268], awt[:], ident[0:12, 0:12]).then_inc(mix_pe, 1)

            def weigh(v, t):
                pe.wait_ge(mix_act, v)
                for half in range(2):
                    ins = mm(ps[0:12, 5 + half, 0:HALF], mixa, t[:, half * HALF:(half + 1) * HALF], start=True, stop=True)
                ins.then_inc(mix_pe, 1)

            def spread(v):
                pe.wait_ge(mix_dve, v)
                for half in range(2):
                    ins = mm(ps[:, 5 + half, 0:HALF], ones[0:12, :], gqm[0:12, half * HALF:(half + 1) * HALF],
                             start=True, stop=True)
                ins.then_inc(mix_pe, 1)

            def src_spread(h, n):
                pe.wait_ge(diag_ready, n)
                mm(ps[:, 4, P:2 * P], ones[:], dg, start=True, stop=True).then_inc(E_out, 1)

            def A_transpose(n):
                pe.wait_ge(A_ready, n)
                nc.tensor.transpose(ps[:, 4, P:2 * P], zt1, ident[:]).then_inc(AT_out, 1)

            def h_transpose(h, d):
                pe.wait_ge(h_copied, 2 * h + 2)
                wait(pe, hT_copied, 2 * h)
                for b in range(4):
                    nc.tensor.transpose(ps[:, 7, b * P:(b + 1) * P], hsb[:, d, b * P:(b + 1) * P], ident[:])
                wait(pe, AT_copied, h)
                for b in range(4, 6):
                    ins = nc.tensor.transpose(ps[:, 4, (b - 2) * P:(b - 1) * P], hsb[:, d, b * P:(b + 1) * P], ident[:])
                ins.then_inc(hT_out, 1)

            def aggregate(h, d):
                pe.wait_ge(AT_copied, h + 1)
                wait(pe, y_ready, h)
                for b in range(KD):
                    ins = mm(ps[:, 2 + b // 3, (b % 3) * P:(b % 3 + 1) * P], hsb[:, d, b * P:(b + 1) * P], ATs,
                             start=True, stop=True)
                ins.then_inc(agg_out, 1)

            def alphas(h):
                pe.wait_ge(hT_copied, 2 * h + 2)
                for b in range(KD):
                    a = (small[:, 12 * h + 2 * b:12 * h + 2 * b + 2] if isinstance(h, int)
                         else small[:, bass.ds(h * 12 + 2 * b, 2)])
                    ins = mm(ps[:, 4, 0:2], hTs[:, b * P:(b + 1) * P], a, start=b == 0, stop=b == KD - 1)
                ins.then_inc(al_out, 1)

            def zero_start(banks):
                for b in banks:
                    mm(ps[:, b, 0:HALF], brow[96:97, 0:P], brow[96:97, 0:HALF], start=True, stop=False)

            x_split(1)
            up_chunk(0, 0, 512, 0)
            up_chunk(1, 1, 512, 1)
            up_chunk(2, 2, 512, 2)
            to_rows(1)
            up_chunk(3, 3, 512, 3)
            to_columns(3)
            up_chunk(4, 4, 256, 7)
            weigh(2, qkv[:, 0:D])
            pe.wait_ge(qkv_copied, 1)
            up_chunk(5, 5, 512, 0)
            spread(4)
            pe.wait_ge(qkv_copied, 2)
            up_chunk(6, 6, 256, 1)
            pe.wait_ge(qkv_copied, 5)
            pe.wait_ge(small_in, 16)
            h_transpose(0, 0)
            to_rows(5)
            alphas(0)
            up_chunk(7, 7, 512, 0)
            to_columns(7)
            src_spread(0, 1)
            up_chunk(8, 8, 256, 1)
            weigh(4, qkv[:, D:2 * D])
            A_transpose(1)
            h_transpose(1, 1)
            spread(8)
            aggregate(0, 0)
            alphas(1)
            pe.wait_ge(mix_dve, 9)
            zero_start((5, 6))

            def step(h, c, d, k):
                pe.wait_ge(h_copied, 2 * h - 1)
                up_chunk(c, k, 512, 0)
                src_spread(h - 1, h)
                ready(c + 1)
                pe.wait_ge(h_copied, 2 * h)
                up(ps[:, 1, 0:256], k + 1, 256, xTh, xTl).then_inc(hb_out, 1)
                pe.wait_ge(oTl_ready, h - 1)
                down((5, 6), k + 1, 1536, (0, 1), oTh, oTl).then_inc(used, 1)
                A_transpose(h)
                h_transpose(h, d)
                aggregate(h - 1, 1 - d)
                ready(c + 2)
                down((5, 6), k + 2, 0, (2, 3, 4, 5), oTh, oTl).then_inc(used, 1)
                alphas(h)

            with pe.Fori(2, H0, 2) as h:
                for d in range(2):
                    step(h + d, 3 * h + (3 + 3 * d), d, 9 + 3 * d)

            src_spread(7, 8)
            ready(27)
            pe.wait_ge(oTl_ready, 7)
            down((5, 6), 27, 0, (0, 1), oTh, oTl)
            A_transpose(8)
            ready(28)
            down((5, 6), 28, 0, (2, 3, 4, 5), oTh, oTl).then_inc(used, 1)
            aggregate(7, 1)
            pe.wait_ge(hT_copied, 16)
            for b in range(4):
                nc.tensor.transpose(ps[:, 7, b * P:(b + 1) * P], qkv[:, 2 * D + b * P:2 * D + (b + 1) * P], ident[:])
            for b in range(4, 6):
                ins = nc.tensor.transpose(ps[:, 4, (b - 2) * P:(b - 1) * P], qkv[:, 2 * D + b * P:2 * D + (b + 1) * P], ident[:])
            ins.then_inc(mix_pe, 1)
            xhf, xlf = (t[:].rearrange("p b n -> p (b n)") for t in (xTh, xTl))
            ready(29)
            pe.wait_ge(mix_dve, 10)
            pe.wait_ge(h_copied, 16)
            down((0, 1), 29, 0, (0, 1, 2), xhf, xlf, first=True).then_inc(used, 1)
            pe.wait_ge(oTl_ready, 8)
            down((5, 6), 27, 1536, (0, 1), oTh, oTl).then_inc(used, 1)
            ready(30)
            down((0, 1), 30, 0, (3, 4, 5), xhf, xlf).then_inc(used, 1)
            ready(31)
            down((5, 6), 31, 0, (2, 3, 4, 5), oTh, oTl, last=True).then_inc(used, 1)
            bias((0, 1), 0, 2)
            src_spread(8, 9)
            A_transpose(9)
            pe.wait_ge(AT_copied, 9)
            for half in range(2):
                ins = mm(ps[:, half, 0:HALF], ATs, hsb[:, 0, half * HALF:(half + 1) * HALF], start=False, stop=True)
            ins.then_inc(F_out, 1)

            transpose6(xn, 2)
            x_split(2)
            a0 = PC["wr"][0]
            for i in range(2 * KD):
                t, x = i // 2, (xTh, xTl)[i % 2]
                ins = mm(ps[:, 7, 0:8], x[:, t, :].bitcast(F32), small[:, a0 + 8 * t:a0 + 8 * t + 8],
                         start=i == 0, stop=i == 2 * KD - 1)
            ins.then_inc(router_out, 1)
            zero_start((5, 6))

            def T(j, d):
                pe.wait_ge(hh_ready, j + 1)
                wait(pe, hTl_ready, j)
                for b in range(4):
                    ins = nc.tensor.transpose(ps[:, 4, b * P:(b + 1) * P], hhb[d][:, b * P:(b + 1) * P], ident[:])
                ins.then_inc(T_out, 1)

            up_chunk(FFN0, FFN0, 512, 0)
            up_chunk(FFN0 + 1, FFN0 + 1, 512, 2)

            def fstep(j, c, d, k):
                wait(pe, silu_done, j - 1)
                up_chunk(c, k, 512, d)
                T(j - 1, 1 - d)
                up_chunk(c + 1, k + 1, 512, 2 + d)
                ready(c + 2)
                pe.wait_ge(hTl_ready, j)
                down((5, 6), k + 2, 0, (0, 1, 2, 3), oTh, oTl).then_inc(used, 1)

            with pe.Fori(1, FS, 2) as j:
                for d in range(2):
                    fstep(j + d, 3 * j + (31 + 3 * d), 1 - d, 34 + 3 * d)
            T(FS - 1, 0)
            ready(L1 - 1)
            pe.wait_ge(hTl_ready, FS)
            down((5, 6), L1 - 1, 0, (0, 1, 2, 3), oTh, oTl, last=True).then_inc(used, 1)

            transpose6(xn, 3)
            x_split(3)
            up_chunk(L1, L1, 512, 0)
            up_chunk(L1 + 1, L1 + 1, 256, 5)
            up_chunk(L1 + 2, L1 + 2, 512, 1)

            def l1(s, v):
                pe.wait_ge(s, v)

            l1(diag_ready, 10)
            mm(ps[:, 6, :], ones[:], L1D, start=True, stop=True).then_inc(l1_pe, 1)
            up_chunk(L1 + 3, L1 + 3, 512, 2)
            up_chunk(L1 + 4, L1 + 4, 512, 3)
            l1(A_ready, 10)
            for h in range(4):
                ins = nc.tensor.transpose(ps[:, 6, h * P:(h + 1) * P], L1Z[:, h * P:(h + 1) * P], ident[:])
            ins.then_inc(l1_pe, 1)
            up_chunk(L1 + 5, L1 + 5, 256, 4)
            l1(l1_act, 6)
            for h in range(4):
                ins = mm(ps[64 * (h % 2):64 * (h % 2) + 64, 7, (h // 2) * P:(h // 2 + 1) * P],
                         gqm[:, 64 * h:64 * h + 64], L1AT[:, h * P:(h + 1) * P], start=True, stop=True)
            ins.then_inc(l1_pe, 1)

            def tr6(src, b0):
                for b in range(KD):
                    ins = nc.tensor.transpose(ps[:, b0 + b // 3, (b % 3) * P:(b % 3 + 1) * P], src[:, b * P:(b + 1) * P], ident[:])
                ins.then_inc(l1_pe, 1)

            l1(l1_act, 7)
            tr6(qkv[:, 0:D], 0)
            tr6(qkv[:, D:2 * D], 2)
            wsm = raw[:, (NCH - 1) % R, :]
            l1(landed[(NCH - 1) % R], landed_at(NCH - 1))
            l1(l1_act, 9)
            for t in range(2):
                ins = mm(ps[:, 5, 256:512], gT[:, t * P:(t + 1) * P], wsm[:, 256 * t:256 * t + 256], start=t == 0, stop=t == 1)
            ins.then_inc(l1_pe, 1)
            l1(l1_act, 10)
            tr6(qkv[:, 2 * D:3 * D], 0)
            l1(diag_ready, 11)
            mm(ps[:, 6, 0:P], ones[:], L1D[:, 0:P], start=True, stop=True).then_inc(l1_pe, 1)
            l1(l1_act, 11)
            bias((2, 3), 32, 2, first=True)
            l1(A_ready, 11)
            nc.tensor.transpose(ps[:, 6, 0:P], L1Z[:, 0:P], ident[:]).then_inc(l1_pe, 1)
            l1(l1_act, 14)
            for b in range(2):
                ins = mm(ps[:, 7, b * P:(b + 1) * P], gqm[:, 256 + b * P:256 + (b + 1) * P], L1AT[:, 0:P], start=True, stop=True)
            ins.then_inc(l1_pe, 1)
            l1(l1_act, 16)
            for b in range(2):
                for t in range(2):
                    ins = mm(ps[:, 7, 256 + b * P:256 + (b + 1) * P], wsm[:, 512 + 256 * t + b * P:512 + 256 * t + (b + 1) * P],
                             gT[:, t * P:(t + 1) * P], start=t == 0, stop=t == 1)
            ins.then_inc(l1_pe, 1)
            l1(l1_act, 18)
            for t in range(2):
                for half in range(2):
                    ins = mm(ps[:, 2 + half, 0:HALF], gT2[:, t * P:(t + 1) * P],
                             wsm[:, 1024 + D * t + half * HALF:1024 + D * t + (half + 1) * HALF], start=False, stop=False)
            ins.then_inc(l1_pe, 1)
            l1(l1_dve, 4)
            ready(L1 + 6)
            down((2, 3), L1 + 6, 0, (0, 1, 2), xhf, xlf).then_inc(used, 1)
            ready(L1 + 7)
            down((2, 3), L1 + 7, 0, (3, 4, 5), xhf, xlf, last=True).then_inc(F_out, 1)

            transpose6(xn, 4)
            pe.wait_ge(f_act, 1)
            pe.wait_ge(fw_in, 16)
            for t in range(KD):
                ins = mm(ps[:, 6, 0:P], hTs[:, t * P:(t + 1) * P], fw("P")[:, t * P:(t + 1) * P], start=t == 0, stop=t == KD - 1)
            ins.then_inc(f_pe, 1)
            pe.wait_ge(f_dve, 1)
            for g in range(2):
                ins = nc.tensor.transpose(ps[:, 3, g * P:(g + 1) * P], zp[:, g * P:(g + 1) * P], ident[:])
            ins.then_inc(f_pe, 1)
            pe.wait_ge(f_act, 2)
            for g in range(2):
                ins = mm(ps[:, 4, 256 * g:256 * g + 256], zT[:, g * P:(g + 1) * P], fw("C")[:, 256 * g:256 * g + 256],
                         start=True, stop=True)
            ins.then_inc(f_pe, 1)
            w1 = fw("W1").rearrange("p (g m) -> p g m", g=2)

            def hidden(w, s4):
                g, jq = w // 4, w % 4
                wait(pe, gelu_done, 4 * (w - 1) + s4 + 1)
                for i in range(4):
                    j = 4 * jq + i
                    ins = mm(ps[:, s4, i * P:(i + 1) * P], w1[32 * s4:32 * s4 + 17, g, j * P:(j + 1) * P],
                             zT[32 * s4:32 * s4 + 17, g * P:(g + 1) * P], start=True, stop=True)
                ins.then_inc(hid_out, 1)

            for s4 in range(4):
                hidden(0, s4)
            pe.wait_ge(f_dve, 3)
            for t in range(4):
                ins = nc.tensor.transpose(ps[:, 4, t * P:(t + 1) * P], ww[:, t * P:(t + 1) * P], ident[:])
            ins.then_inc(f_pe, 1)
            pe.wait_ge(f_act, 5)
            for t in range(4):
                ins = mm(ps[:, 7, 0:P], wT[:, t * P:(t + 1) * P], fw("b2")[:, t * P:(t + 1) * P], start=t == 0, stop=t == 3)
            ins.then_inc(f_pe, 1)
            pe.wait_ge(f_pool, 1)
            pe.wait_ge(f_dve, 4)
            for w in range(8):
                g, jq = w // 4, w % 4
                wait(pe, Y_read, 2 * (w - 1))
                for s4 in range(4):
                    pe.wait_ge(gelu_done, 4 * w + s4 + 1)
                    if w < 7:
                        hidden(w + 1, s4)
                    for i in range(4):
                        blk = (4 * g + s4) * 16 + 4 * jq + i
                        bd = raw[:, (5, 0, 1)[blk // 48], (blk % 48) * 64:(blk % 48) * 64 + 64]
                        a = 256 * (s4 % 2) + 64 * i
                        ins = mm(ps[:, 4 + 2 * (w % 2) + s4 // 2, a:a + 64], hg[s4][:, i * P:(i + 1) * P], bd,
                                 start=True, stop=True)
                    ins.then_inc(Y_out, 1)
            pe.wait_ge(Y_read, 16)
            nc.tensor.transpose(ps[:, 0, 0:P], cb, ident[:]).then_inc(f_pe, 1)
            pe.wait_ge(f_act, 6)
            for b in range(2):
                ins = mm(ps[:, 1, b * P:(b + 1) * P], fw("G1")[:, b * P:(b + 1) * P], cT, start=True, stop=True)
            ins.then_inc(f_pe, 1)
            bias((2, 3), 64, 1, first=True)
            pe.wait_ge(f_act, 8)
            pe.wait_ge(g2_in, 16)
            for t in range(2):
                for half in range(2):
                    ins = mm(ps[:, 2 + half, 0:HALF], fT[:, t * P:(t + 1) * P],
                             qkv[:, D * t + half * HALF:D * t + (half + 1) * HALF], start=False, stop=t == 1)
            ins.then_inc(F_out, 1)


def kernel(**inputs):
    import concourse.bacc as bacc
    import numpy as np
    from concourse.bass_utils import run_bass_kernel_spmd

    a = {k: np.asarray(v) for k, v in inputs.items()}

    def up(w, c0, n):
        return w[:, c0:c0 + n].reshape(KD, P, n).transpose(1, 0, 2).reshape(P, KD * n)

    def down(w, k0, n):
        return w[k0 * P:(k0 + n) * P].reshape(n, P, D).transpose(1, 0, 2).reshape(P, n * D)

    stream = np.zeros((NCH, P, SLOT), np.float32)

    def put(c, *parts):
        at = 0
        for p in parts:
            stream[c, :, at:at + p.shape[1]] = p
            at += p.shape[1]
        assert at == chunk_len(c)

    def put_qkv(cs, w):
        for i, c in enumerate(cs):
            put(c, up(w, 512 * i, 512 if i < 4 else 256))

    w1, w2 = a["L0_gnn_W1"], a["L0_gnn_W2"]
    put_qkv(range(5), a["L0_mix_Wqkv"].T)
    for h in range(2):
        put(5 + 2 * h, up(w1, D * h, 512))
        put(6 + 2 * h, up(w1, D * h + 512, 256))
    for h in range(2, H0):
        put(3 * h + 3, up(w1, D * h, 512))
        put(3 * h + 4, up(w1, D * h + 512, 256), down(w2, KD * (h - 2), 2))
        put(3 * h + 5, down(w2, KD * (h - 2) + 2, 4))
    put(27, down(w2, KD * 6, 2), down(w2, KD * 7, 2))
    put(28, down(w2, KD * 6 + 2, 4))
    wp = a["L0_mix_Wp"].T
    put(29, down(wp, 0, 3))
    put(30, down(wp, 3, 3))
    put(31, down(w2, KD * 7 + 2, 4))
    for e in range(9):
        wg, wu, wd = ((a["L0_ffn_Wg"][e], a["L0_ffn_Wu"][e], a["L0_ffn_Wd"][e]) if e < 8
                      else (a["L0_ffn_sg"], a["L0_ffn_su"], a["L0_ffn_sd"]))
        for b in range(3):
            j = 3 * e + b
            put(FFN0 if j == 0 else 31 + 3 * j, up(wg.T, FB * b, FB))
            put(FFN0 + 1 if j == 0 else 32 + 3 * j, up(wu.T, FB * b, FB))
            put(36 + 3 * j if j < FS - 1 else L1 - 1, down(wd.T, 4 * b, 4))
    put_qkv((L1, L1 + 2, L1 + 3, L1 + 4, L1 + 5), a["L1_mix_w_qkv"])
    put(L1 + 1, up(a["L1_gnn_W1"], 0, 256))
    put(L1 + 6, down(a["L1_mix_w_proj"], 0, 3))
    put(L1 + 7, down(a["L1_mix_w_proj"], 3, 3))
    sq = lambda w: w.reshape(2, P, 256).transpose(1, 0, 2).reshape(P, 512)
    put(L1 + 8, sq(a["L1_gnn_W2"]), sq(a["L1_gnn_Wm1"]), down(a["L1_gnn_Wm2"], 0, 2))

    part = lambda v, n: v.reshape(n, P).T
    a1 = np.stack([a["L0_gnn_a_src1"], a["L0_gnn_a_dst1"]], -1)
    small = np.concatenate([
        a1.reshape(H0, KD, P, 2).transpose(2, 0, 1, 3).reshape(P, 96),
        part(a["L0_gnn_b1"], 48),
        a["L0_ffn_w_router"].T.reshape(KD, P, 8).transpose(1, 0, 2).reshape(P, 48),
        np.broadcast_to(a["L0_ffn_expert_bias"], (P, 8)),
        part(a["L1_gnn_b1"], 2), part(a["L1_gnn_b2"], 2), part(a["L1_gnn_bm1"], 2), part(a["L1_ffn_g1b"], 2)], 1)
    rows = lambda v, n=P: np.broadcast_to(v.reshape(1, -1), (n, v.size))
    ga = np.concatenate([rows(a["L1_gnn_a_src1"]), rows(a["L1_gnn_a_dst1"]),
                         rows(a["L1_gnn_a_src2"]), rows(a["L1_gnn_a_dst2"])], 1)
    a2b = np.concatenate([rows(a["L0_gnn_a_src2"]), rows(a["L0_gnn_a_dst2"])], 1)
    brow = np.stack([a["L0_gnn_b2"], a["L0_mix_bp"], a["L1_gnn_bm2"], a["L1_mix_b_proj"], a["L1_ffn_g2b"]])

    fwt = np.zeros((P, NF), np.float32)

    def place(name, v):
        fwt[:, FC[name][0]:FC[name][1]] = v.reshape(P, -1)

    place("P", a["L1_ffn_P"].transpose(1, 0, 2).reshape(KD, P, P).transpose(1, 0, 2))
    cc = np.zeros((4, 32, 2, 4, 64), np.float32)
    bb = np.zeros((2, 64, 4, 8, 16), np.float32)
    ww = np.zeros((4, 32, 2, 2048), np.float32)
    for s in range(8):
        cc[s % 4, 0:16, s // 4, s % 4] = a["L1_ffn_C"][s].T
        bb[s % 2, :, s // 2, s] = a["L1_ffn_b2"][s]
        ww[s % 4, 0:16, s // 4] = a["L1_ffn_W1"][s].transpose(1, 0, 2).reshape(16, 2048)
        ww[s % 4, 16, s // 4] = a["L1_ffn_b1"][s].reshape(2048)
    place("C", cc)
    place("W1", ww)
    place("b2", bb)
    place("W2", a["L1_ffn_W2"].reshape(8, 16, 4, 32, 16).transpose(2, 3, 0, 1, 4))
    place("G1", a["L1_ffn_G1"])

    arrays = {
        "x_in_d": a["x"], "src_d": a["src"].reshape(P, 16), "dst_d": a["dst"].reshape(P, 16), "stream_d": stream,
        "small_d": small, "wqb_d": rows(a["L0_mix_w_q"]), "wk_d": rows(a["L0_mix_w_k"], 12), "a2b_d": a2b, "ga_d": ga,
        "brow_d": brow, "fw_d": fwt, "g2_d": down(a["L1_ffn_G2"], 0, 2),
    }
    arrays = {k: np.ascontiguousarray(v) for k, v in arrays.items()}
    nc = bacc.Bacc("TRN2", target_bir_lowering=False, num_devices=1)
    aps = [nc.dram_tensor(k, v.shape, mybir.dt.from_np(v.dtype), kind="ExternalInput").ap() for k, v in arrays.items()]
    out = nc.dram_tensor("out_d", (N, D), F32, kind="ExternalOutput").ap()
    build(nc, *aps, out)
    return run_bass_kernel_spmd(nc, [arrays], core_ids=[0]).results[0]["out_d"]
```

```python
from contextlib import ExitStack

import concourse.bass as bass
from concourse import mybir

P = 128
N = 128
D = 768
KD = D // P
HALF = D // 2
SLOT = 3072
R = 6
S = 3
H0 = 8
FS = 27
FB = 512

QKV0 = 0
TAIL0 = 27
FFN0 = 32
L1 = FFN0 + 3 * FS
NCH = L1 + 9

F32 = mybir.dt.float32
F32R = mybir.dt.float32r
BF16 = mybir.dt.bfloat16
I32 = mybir.dt.int32
U32 = mybir.dt.uint32
ALU = mybir.AluOpType
ACT = mybir.ActivationFunctionType
AX = mybir.AxisListType.X

PC = {}
_at = 0
for _n, _w in (("a1T", 96), ("b1T", 48), ("wr", 48), ("ebias", 8), ("gb1", 2), ("gb2", 2), ("bm1", 2), ("fg1b", 2)):
    PC[_n] = (_at, _at + _w)
    _at += _w
NSMALL = _at

FC = {}
_at = 0
for _n, _w in (("P", 2 * D), ("C", 512), ("W1", 4096), ("W2", 2048), ("b2", 128), ("G1", 512), ("one", P)):
    FC[_n] = (_at, _at + _w)
    _at += _w
NF = _at
EPS = 1e-5
UNITS = 32
BIG = -1e30


def chunk_len(c):
    if c in (4, 6, 8, L1 + 1, L1 + 5):
        return 1536
    if c in (29, 30, L1 + 6, L1 + 7):
        return 2304
    if c == NCH - 1:
        return 2560
    return SLOT


def landed_at(c):
    return 16 * (c // R + 1)


def build(nc, x_d, src_d, dst_d, stream_d, small_d, wqb_d, wk_d, a2b_d, ga_d, brow_d, fw_d, g2_d, out_d):
    with ExitStack() as ctx:
        def sb(name, shape, dt=F32):
            return ctx.enter_context(nc.sbuf_tensor(name, shape, dt))

        def sem(name):
            return ctx.enter_context(nc.semaphore(name))

        ps = ctx.enter_context(nc.psum_tensor("ps", [P, 8, 512], F32))

        raw = sb("raw", [P, R, SLOT])
        whi = sb("whi", [P, S, SLOT], F32R)
        wlo = sb("wlo", [P, S, SLOT], F32R)
        small = sb("small", [P, NSMALL])
        pa = sb("pa", [P, 1024])
        xres = sb("xres", [P, D])
        xn = sb("xn", [P, D])
        xTh = sb("xTh", [P, KD, P], F32R)
        xTl = sb("xTl", [P, KD, P], F32R)
        ident = sb("ident", [P, P])
        ones = sb("ones", [P, P])
        iota = sb("iota", [P, P])
        cnt = sb("cnt", [P, P])
        cneg = sb("cneg", [P, P])
        brow = sb("brow", [97, D])
        stat = sb("stat", [P, 160])
        qkv = sb("qkv", [P, 3 * D])
        hsb = sb("hsb", [P, 2, D])
        hTs = sb("hTs", [P, D])
        yb = sb("yb", [P, D])
        eb = sb("eb", [P, D])
        oTh = sb("oTh", [P, D], F32R)
        oTl = sb("oTl", [P, D], F32R)
        gz = sb("gz", [P, 1536])
        gqm = sb("gqm", [P, D])

        def sm(name):
            a, b = PC[name]
            return small[:, a:b]

        fbase = raw[:, 2:5, :].rearrange("p s c -> p (s c)")

        def fw(name):
            a, b = FC[name]
            return fbase[:, a:b]

        al = stat[:, 0:8]
        mx = stat[:, 8:12]
        nm = stat[:, 12:16]
        den = stat[:, 16:20]
        rcp = stat[:, 20:24]
        bst = stat[:, 24:36]
        mv = stat[:, 36:38]
        rstd = stat[:, 38:39]
        mhalf = stat[:, 39:51]
        comb = stat[:, 51:78]
        veps = stat[:, 78:79]
        mixa = stat[:, 80:92]
        mst = stat[:, 92:96]
        edg = stat[:, 96:128]
        awt = sb("awt", [12, P])
        soh = qkv[:, 0:1024].bitcast(BF16).rearrange("p (t n) -> p t n", t=16)
        doh = qkv[:, 1024:2048].bitcast(BF16).rearrange("p (t n) -> p t n", t=16)
        hm = eb[0:12, :]
        wkm = gz[0:12, 384:384 + D]
        zt1, ATs, dg = gz[:, 0:P], gz[:, P:2 * P], gz[:, 2 * P:3 * P]
        hsf = hsb[:].rearrange("p a n -> p (a n)")
        asb = [hsf[:, 0:FB], hsf[:, FB:2 * FB]]
        hhb = [gz[:, 0:FB], gz[:, FB:2 * FB]]
        L1Z, L1D, L1AT = gz[:, 0:512], gz[:, 512:1024], gz[:, 1024:1536]
        qT, kT, vT = hsb[:, 0, :], hsb[:, 1, :], hTs[:]
        gT, gT2 = yb[:, 0:256], yb[:, 256:512]
        zT, fT = yb[:, 256:512], yb[:, 512:768]
        scs, se, ww = gz[:, 0:512], gz[:, 512:1024], gz[:, 1024:1536]
        hg = raw[:, 5, 0:2048]
        zh, zl = whi[:, 0, 0:8 * P], wlo[:, 0, 0:8 * P]
        w1h = [whi[:, 2, 0:2048], wlo[:, 2, 0:2048]]
        w1l = [whi[:, 0, 1024:3072], wlo[:, 0, 1024:3072]]
        wcat, taken = raw[:, 1, 0:1024], raw[:, 1, 1024:1536]
        expand = whi[:, 1, 0:2048]
        wTs = wlo[:, 1, 0:1024]
        cT = eb[:, 0:256]
        at = FC["W1"][0]
        w1 = [fbase[:, at + 2048 * g:at + 2048 * (g + 1)] for g in range(2)]
        tv, tden = gqm[:, 0:64], gqm[:, 64:72]

        landed = [sem(f"landed{i}") for i in range(R)]
        hi_ready = sem("hi_ready")
        lo_ready = sem("lo_ready")
        used = sem("used")
        x_in = sem("x_in")
        edges_in = sem("edges_in")
        small_in = sem("small_in")
        wq_in = sem("wq_in")
        wk_in = sem("wk_in")
        brow_in = sem("brow_in")
        as2_in = sem("as2_in")
        ad2_in = sem("ad2_in")
        ga_in = sem("ga_in")
        fw_in = sem("fw_in")
        g2_in = sem("g2_in")
        out_in = sem("out_in")
        pool_chain = sem("pool_chain")
        consts = sem("consts")
        dve_chain = sem("dve_chain")
        onehots = sem("onehots")
        count_out = sem("count_out")
        ln_var = sem("ln_var")
        ln_rstd = sem("ln_rstd")
        xn_ready = sem("xn_ready")
        xT_out = sem("xT_out")
        xTh_ready = sem("xTh_ready")
        xTl_ready = sem("xTl_ready")
        qkv_copied = sem("qkv_copied")
        mix_pe = sem("mix_pe")
        mix_dve = sem("mix_dve")
        mix_act = sem("mix_act")
        h_copied = sem("h_copied")
        hb_out = sem("hb_out")
        hT_out = sem("hT_out")
        hT_copied = sem("hT_copied")
        al_out = sem("al_out")
        diag_ready = sem("diag_ready")
        E_out = sem("E_out")
        score_ready = sem("score_ready")
        exp_done = sem("exp_done")
        A_ready = sem("A_ready")
        AT_out = sem("AT_out")
        AT_copied = sem("AT_copied")
        agg_out = sem("agg_out")
        y_ready = sem("y_ready")
        ey_done = sem("ey_done")
        elu_ready = sem("elu_ready")
        oTh_ready = sem("oTh_ready")
        oTl_ready = sem("oTl_ready")
        g_copied = sem("g_copied")
        F_out = sem("F_out")
        x_ready = sem("x_ready")
        router_out = sem("router_out")
        rexp_done = sem("rexp_done")
        rscore = sem("rscore")
        comb_ready = sem("comb_ready")
        silu_done = sem("silu_done")
        hh_ready = sem("hh_ready")
        T_out = sem("T_out")
        hTh_ready = sem("hTh_ready")
        hTl_ready = sem("hTl_ready")
        l1_pe = sem("l1_pe")
        l1_act = sem("l1_act")
        l1_dve = sem("l1_dve")
        l1_pool = sem("l1_pool")
        f_pe = sem("f_pe")
        f_act = sem("f_act")
        f_dve = sem("f_dve")
        f_pool = sem("f_pool")
        hid_out = sem("hid_out")
        w1h_ready = sem("w1h_ready")
        w1l_ready = sem("w1l_ready")
        zh_ready = sem("zh_ready")
        zl_ready = sem("zl_ready")
        gelu_done = sem("gelu_done")
        Y_out = sem("Y_out")
        spread_out = sem("spread_out")
        weighted = sem("weighted")

        def wait(eng, s, v):
            if not (isinstance(v, int) and v <= 0):
                eng.wait_ge(s, v)

        class Chain:

            def __init__(self, eng, s):
                self.eng, self.s, self.base, self.k = eng, s, 0, 0

            def link(self, ins):
                self.k += 1
                ins.then_inc(self.s, 1)
                self.eng.wait_ge(self.s, self.base + self.k)

        block = ctx.enter_context(nc.Block())

        @block.sync
        def _(sp):
            def load(c, k, land_extra=0):
                n = chunk_len(k)
                sp.dma_start(raw[:, k % R, 0:n], stream_d[c, :, 0:n] if isinstance(c, int)
                             else stream_d[bass.ds(c, 1), :, 0:n].rearrange("a p n -> (a p) n")).then_inc(landed[k % R], 16)

            sp.dma_start(xres[:], x_d).then_inc(x_in, 16)
            sp.dma_start(edg[:, 0:16].bitcast(I32), src_d).then_inc(edges_in, 16)
            sp.dma_start(edg[:, 16:32].bitcast(I32), dst_d).then_inc(edges_in, 16)
            for c in range(R):
                load(c, c)
            for c in range(R, 9):
                sp.wait_ge(lo_ready, c - R + 1)
                load(c, c)
            with sp.Fori(9, TAIL0, R) as c:
                for k in range(R):
                    sp.wait_ge(lo_ready, c + (k - R + 1))
                    load(c + k, 9 + k)
            for c in range(TAIL0, 34):
                if c == 28:
                    sp.wait_ge(mix_dve, 9)
                    sp.dma_start(pa[:, 0:D], a2b_d[:, 0:D]).then_inc(as2_in, 16)
                    sp.dma_start(qkv[:, D:2 * D], a2b_d[:, D:2 * D]).then_inc(ad2_in, 16)
                sp.wait_ge(lo_ready, c - R + 1)
                load(c, c)
            with sp.Fori(34, L1 - 1, R) as c:
                for k in range(R):
                    sp.wait_ge(lo_ready, c + (k - R + 1))
                    load(c + k, 34 + k)
            for c in range(L1 - 1, NCH):
                if c == L1:
                    sp.wait_ge(x_ready, 1)
                    sp.dma_start(pa[:, 0:1024], ga_d).then_inc(ga_in, 16)
                sp.wait_ge(lo_ready, c - R + 1)
                load(c, c)
            sp.wait_ge(lo_ready, L1 + 6)
            sp.dma_start(fbase[:, 0:NF], fw_d).then_inc(fw_in, 16)
            sp.wait_ge(l1_pe, 5)
            sp.dma_start(qkv[:, 0:2 * D], g2_d).then_inc(g2_in, 16)
            sp.wait_ge(x_ready, 4)
            sp.dma_start(out_d, xres[:]).then_inc(out_in, 16)
            sp.wait_ge(out_in, 16)

        @block.gpsimd
        def _(pool):
            ch = Chain(pool, pool_chain)
            ch.link(nc.gpsimd.memset(ident[:], 0.0))
            nc.gpsimd.affine_select(out=ident[:], in_=ident[:], compare_op=ALU.not_equal, fill=1.0, base=0,
                                    pattern=[[-1, P]], channel_multiplier=1).then_inc(consts, 1)
            nc.gpsimd.memset(ones[:], 1.0).then_inc(consts, 1)
            nc.gpsimd.iota(iota[:], pattern=[[1, P]], base=0, channel_multiplier=0,
                           allow_small_or_imprecise_dtypes=True).then_inc(consts, 1)
            nc.gpsimd.memset(mhalf, -0.5).then_inc(consts, 1)
            ch.link(nc.gpsimd.memset(hm, 0.0))
            nc.gpsimd.memset(brow[96:97, :], 0.0).then_inc(consts, 1)
            nc.gpsimd.affine_select(out=hm.rearrange("p (h c) -> p h c", c=64),
                                    in_=hm.rearrange("p (h c) -> p h c", c=64),
                                    compare_op=ALU.not_equal, fill=1.0, base=0,
                                    pattern=[[-1, 12], [0, 64]], channel_multiplier=1).then_inc(consts, 1)

            def rsqrt(n):
                pool.wait_ge(ln_var, n)
                nc.gpsimd.tensor_tensor(rstd, veps, mhalf[:, 0:1], ALU.pow).then_inc(ln_rstd, 1)

            pool.wait_ge(consts, 6)
            rsqrt(1)
            rsqrt(2)
            rsqrt(3)
            pool.wait_ge(l1_dve, 2)
            nc.gpsimd.tensor_tensor(stat[:, 112:124], stat[:, 100:112], mhalf, ALU.pow).then_inc(l1_pool, 1)
            pool.wait_ge(used, L1 + 6)
            nc.gpsimd.tensor_tensor(expand.rearrange("p (m h) -> p m h", h=32),
                                    ident[:, 0:64].unsqueeze(2).broadcast_to([P, 64, 32]),
                                    ident[:, 64:128].unsqueeze(2).broadcast_to([P, 64, 32]), ALU.add).then_inc(f_pool, 1)
            rsqrt(4)
            pool.wait_ge(F_out, 2)
            b8 = lambda t: t.rearrange("p (s n) -> p s n", s=8)
            nc.gpsimd.tensor_tensor(b8(zh), *(ident[:].unsqueeze(1).broadcast_to([P, 8, P]),) * 2, ALU.subtract)
            nc.gpsimd.tensor_tensor(b8(zl), *(ident[:].unsqueeze(1).broadcast_to([P, 8, P]),) * 2,
                                    ALU.subtract).then_inc(f_pool, 1)

        @block.scalar
        def _(act):
            def hi(c, k, land, need=None):
                n = chunk_len(k)
                act.wait_ge(landed[k % R], land)
                need = c - S + 1 if need is None else need
                wait(act, used, need)
                nc.scalar.activation(whi[:, k % S, 0:n], raw[:, k % R, 0:n], ACT.Copy).then_inc(hi_ready, 1)

            def his(c):
                hi(c, c, landed_at(c))

            def copy(out, in_, s):
                nc.scalar.activation(out, in_, ACT.Copy).then_inc(s, 1)

            def xT_hi(n):
                act.wait_ge(xT_out, n)
                copy(xTh[:].rearrange("p (a b) n -> p a (b n)", a=2), ps[:, 2:4, 0:HALF], xTh_ready)

            act.dma_start(small[:], small_d).then_inc(small_in, 16)
            act.dma_start(pa[:, 0:D], wqb_d).then_inc(wq_in, 16)
            act.dma_start(brow[0:2, :], brow_d[0:2, :]).then_inc(brow_in, 16)
            act.dma_start(brow[32:34, :], brow_d[2:4, :]).then_inc(brow_in, 16)
            act.dma_start(brow[64:65, :], brow_d[4:5, :]).then_inc(brow_in, 16)

            act.dma_start(wkm, wk_d).then_inc(wk_in, 16)

            def qkv_copy(i, bank):
                act.wait_ge(used, i + 1)
                n = 512 if i < 4 else 256
                copy(qkv[:, 512 * i:512 * i + n], ps[:, bank, 0:n], qkv_copied)

            def mix_softmax(n):
                act.wait_ge(mix_dve, n)
                nc.scalar.activation(awt[:], ps[0:12, 5, 128:256], ACT.Exp, bias=mst[0:12, 1:2], scale=0.125,
                                     accum_out=mst[0:12, 2:3]).then_inc(mix_act, 1)

            def h_copy(h, d, part, s, v):
                act.wait_ge(s, v)
                wait(act, agg_out, h - 1)
                n = 512 if part == 0 else 256
                copy(hsb[:, d, 512 * part:512 * part + n], ps[:, part, 0:n], h_copied)

            def soft_exp(n):
                act.wait_ge(score_ready, n)
                nc.scalar.activation(zt1, zt1, ACT.Exp, bias=nm[:, 0:1]).then_inc(exp_done, 1)

            def AT_copy(n):
                act.wait_ge(AT_out, n)
                copy(ATs, ps[:, 4, 128:256], AT_copied)

            def hT_copy(h):
                act.wait_ge(hT_out, h + 1)
                wait(act, al_out, h)
                copy(hTs[:, 0:512], ps[:, 7, :], hT_copied)
                copy(hTs[:, 512:768], ps[:, 4, 256:512], hT_copied)

            def elu_exp(n):
                act.wait_ge(y_ready, n)
                nc.scalar.activation(eb[:], yb[:], ACT.Exp).then_inc(ey_done, 1)

            def o_hi(n, free):
                act.wait_ge(elu_ready, n)
                wait(act, used, free)
                copy(oTh[:], yb[:], oTh_ready)

            xT_hi(1)
            his(0)
            his(1)
            his(2)
            act.wait_ge(count_out, 1)
            qkv_copy(0, 0)
            his(3)
            qkv_copy(1, 1)
            his(4)
            qkv_copy(2, 2)
            mix_softmax(2)
            his(5)
            qkv_copy(3, 3)
            act.wait_ge(mix_pe, 2)
            copy(mixa, ps[:, 5, 256:268], mix_act)
            his(6)
            qkv_copy(4, 7)
            his(7)
            h_copy(0, 0, 0, used, 6)
            his(8)
            h_copy(0, 0, 1, used, 7)
            hT_copy(0)
            mix_softmax(6)
            his(9)
            h_copy(1, 1, 0, used, 8)
            act.wait_ge(mix_pe, 6)
            copy(mixa, ps[:, 5, 256:268], mix_act)
            his(10)
            soft_exp(1)
            h_copy(1, 1, 1, used, 9)
            AT_copy(1)
            hT_copy(1)
            elu_exp(1)
            o_hi(1, 0)

            def step(h, c, d, k, land):
                hi(c + 2, k + 2, land(k + 2))
                h_copy(h, d, 0, used, c + 1)
                soft_exp(h)
                h_copy(h, d, 1, hb_out, h - 1)
                hi(c + 3, k + 3, land(k + 3))
                AT_copy(h)
                hi(c + 4, k + 4, land(k + 4))
                hT_copy(h)
                elu_exp(h)
                o_hi(h, c + 3)

            with act.Fori(2, H0, 2) as h:
                for d in range(2):
                    step(h + d, 3 * h + (3 + 3 * d), d, 9 + 3 * d, lambda k: 8 * h + (landed_at(k) - 16))

            soft_exp(8)
            his(29)
            AT_copy(8)
            elu_exp(8)
            o_hi(8, 28)
            act.wait_ge(mix_pe, 9)
            copy(xTh[:].rearrange("p b n -> p (b n)")[:, 0:512], ps[:, 7, :], mix_act)
            copy(xTh[:].rearrange("p b n -> p (b n)")[:, 512:768], ps[:, 4, 256:512], mix_act)
            hi(30, 30, landed_at(30), need=30)
            hi(31, 31, landed_at(31), need=30)
            hi(32, 32, landed_at(32), need=30)
            his(33)
            act.wait_ge(used, 32)
            copy(hsb[:, 0, :].rearrange("p (a n) -> p a n", a=2), ps[:, 5:7, 0:HALF], g_copied)
            soft_exp(9)
            AT_copy(9)
            xT_hi(2)
            act.wait_ge(rscore, 1)
            nc.scalar.activation(stat[:, 128:136], stat[:, 128:136], ACT.Exp, bias=nm[:, 0:1],
                                 accum_out=den[:, 0:1]).then_inc(rexp_done, 1)

            def silu(j, d, done):
                act.wait_ge(used, done)
                wait(act, hh_ready, j - 1)
                nc.scalar.activation(asb[d], ps[:, d, :], ACT.Silu).then_inc(silu_done, 1)

            def hT_hi(j, free):
                act.wait_ge(T_out, j + 1)
                act.wait_ge(used, free)
                copy(oTh[:, 0:FB], ps[:, 4, :], hTh_ready)

            his(34)
            silu(0, 0, 33)
            his(35)

            def fstep(j, c, d, k, land):
                hi(c + 2, k + 2, land(k + 2))
                silu(j, d, c + 1)
                hT_hi(j - 1, c)
                hi(c + 3, k + 3, land(k + 3))
                hi(c + 4, k + 4, land(k + 4))

            with act.Fori(1, FS, 2) as j:
                for d in range(2):
                    fstep(j + d, 3 * j + (31 + 3 * d), 1 - d, 34 + 3 * d,
                          lambda k: 8 * j + (landed_at(k) - 8))
            hT_hi(FS - 1, L1 - 1)
            his(L1 + 1)
            xT_hi(3)
            his(L1 + 2)

            def l1_copy(out, in_, n, s=l1_pe):
                act.wait_ge(s, n)
                copy(out, in_, l1_act)

            def relu2(out, col, name, n):
                act.wait_ge(l1_pe, n)
                for b in range(2):
                    nc.scalar.activation(out[:, b * P:(b + 1) * P], ps[:, 7, col + b * P:col + (b + 1) * P], ACT.Relu,
                                         bias=sm(name)[:, b:b + 1]).then_inc(l1_act, 1)

            halves = lambda t: t.rearrange("p (a n) -> p a n", a=2)
            l1_copy(qkv[:, 0:512], ps[:, 0, :], L1 + 1, used)
            l1_copy(gqm[:, 0:256], ps[:, 5, 0:256], L1 + 2, used)
            his(L1 + 3)
            l1_copy(qkv[:, 512:1024], ps[:, 1, :], L1 + 3, used)
            his(L1 + 4)
            act.wait_ge(score_ready, 10)
            for h in range(4):
                nc.scalar.activation(L1Z[:, h * P:(h + 1) * P], L1Z[:, h * P:(h + 1) * P], ACT.Exp,
                                     bias=nm[:, h:h + 1]).then_inc(exp_done, 1)
            l1_copy(qkv[:, 1024:1536], ps[:, 2, :], L1 + 4, used)
            his(L1 + 5)
            l1_copy(qkv[:, 1536:2048], ps[:, 3, :], L1 + 5, used)
            l1_copy(L1AT, ps[:, 6, :], 2)
            his(L1 + 6)
            l1_copy(qkv[:, 2048:2304], ps[:, 4, 0:256], L1 + 6, used)
            relu2(gT, 0, "gb1", 3)
            l1_copy(halves(qT), ps[:, 0:2, 0:HALF], 4)
            l1_copy(halves(kT), ps[:, 2:4, 0:HALF], 5)
            l1_copy(gqm[:, 256:512], ps[:, 5, 256:512], 6)
            l1_copy(halves(vT), ps[:, 0:2, 0:HALF], 7)
            his(L1 + 7)
            act.wait_ge(score_ready, 11)
            nc.scalar.activation(L1Z[:, 0:P], L1Z[:, 0:P], ACT.Exp, bias=nm[:, 0:1]).then_inc(exp_done, 1)
            l1_copy(L1AT[:, 0:P], ps[:, 6, 0:P], 9)
            relu2(gT, 0, "gb2", 10)
            relu2(gT2, 256, "bm1", 11)
            act.wait_ge(l1_dve, 3)
            copy(xTh[:].rearrange("p b n -> p (b n)"), qT, l1_act)
            act.wait_ge(fw_in, 16)
            act.wait_ge(used, L1 + 7)
            for g in range(2):
                copy(w1h[g], w1[g], w1h_ready)

            own = lambda t, r, s4: t[r, :].rearrange("p (g s n) -> p g s n", g=2, s=4)[:, :, s4, :]
            act.wait_ge(xT_out, 4)
            copy(hTs[:].rearrange("p (a n) -> p a n", a=2), ps[:, 2:4, 0:HALF], f_act)
            act.wait_ge(f_pe, 1)
            copy(zT, ps[:, 6, 0:256], f_act)
            act.wait_ge(f_pool, 2)
            for s4 in range(4):
                r = slice(32 * s4, 32 * s4 + 32)
                copy(own(zh, r, s4), ps[r, 6, 0:256].rearrange("p (g n) -> p g n", g=2), zh_ready)
            act.wait_ge(f_pe, 2)
            copy(scs, ps[:, 4, :], f_act)
            act.wait_ge(f_dve, 1)
            nc.scalar.activation(se, se, ACT.Exp).then_inc(f_act, 1)

            def gelu(u, d):
                act.wait_ge(hid_out, u + 1)
                wait(act, Y_out, u - 3)
                nc.scalar.activation(hg[:, 512 * d:512 * d + 512], ps[:, d, :], ACT.Gelu_apprx_tanh).then_inc(gelu_done, 1)

            for d in range(4):
                gelu(d, d)
            with act.Fori(4, UNITS, 4) as u:
                for d in range(4):
                    gelu(u + d, d)
            act.wait_ge(Y_out, UNITS)
            copy(cT.rearrange("p (g n) -> p g n", g=2), ps[:, 6:8, 0:P], f_act)
            for b in range(2):
                act.wait_ge(f_pe, 4)
                nc.scalar.activation(fT[:, b * P:(b + 1) * P], ps[:, 1, b * P:(b + 1) * P], ACT.Gelu_apprx_tanh,
                                     bias=sm("fg1b")[:, b:b + 1]).then_inc(f_act, 1)

        @block.vector
        def _(dve):
            ch = Chain(dve, dve_chain)
            link = ch.link
            V = nc.vector

            def lo(c, k):
                n = chunk_len(k)
                dve.wait_ge(hi_ready, c + 1)
                V.tensor_tensor(wlo[:, k % S, 0:n], raw[:, k % R, 0:n], whi[:, k % S, 0:n].bitcast(F32),
                                ALU.subtract).then_inc(lo_ready, 1)

            def los(c):
                lo(c, c)

            def layernorm(n):
                V.bn_stats(bst[:, 0:6], xres[:, 0:HALF])
                link(V.bn_stats(bst[:, 6:12], xres[:, HALF:D]))
                link(V.bn_aggr(mv, bst))
                V.tensor_scalar(veps, mv[:, 1:2], EPS, None, ALU.add).then_inc(ln_var, 1)
                dve.wait_ge(ln_rstd, n)
                V.tensor_scalar(xn[:], xres[:], mv[:, 0:1], rstd, ALU.subtract, ALU.mult).then_inc(xn_ready, 1)

            def xT_lo(n):
                dve.wait_ge(xTh_ready, n)
                V.tensor_tensor(xTl[:].rearrange("p (a b) n -> p a (b n)", a=2), ps[:, 2:4, 0:HALF],
                                xTh[:].bitcast(F32).rearrange("p (a b) n -> p a (b n)", a=2),
                                ALU.subtract).then_inc(xTl_ready, 1)

            dve.wait_ge(x_in, 16)
            layernorm(1)
            dve.wait_ge(edges_in, 32)
            dve.wait_ge(consts, 6)
            link(V.tensor_copy(edg, edg.bitcast(I32)))
            for t in range(16):
                V.tensor_scalar(soh[:, t, :], iota[:], edg[:, t:t + 1], None, ALU.is_equal)
                ins = V.tensor_scalar(doh[:, t, :], iota[:], edg[:, 16 + t:17 + t], None, ALU.is_equal)
            ins.then_inc(onehots, 1)
            xT_lo(1)
            los(0)
            dve.wait_ge(count_out, 1)
            link(V.tensor_tensor(cnt[:], ps[:, 4, 0:P], ident[:], ALU.add))
            V.tensor_scalar(cneg[:], cnt[:], 0.5, BIG, ALU.is_lt, ALU.mult)
            los(1)
            dve.wait_ge(wk_in, 16)
            link(V.tensor_tensor(wkm, wkm, hm, ALU.mult))
            los(2)

            def head_scores():
                V.tensor_reduce(mixa, xn[:].rearrange("p (h c) -> p h c", c=64), AX, ALU.add).then_inc(mix_dve, 1)

            halves = lambda t: t.rearrange("p (a n) -> p a n", a=2)

            def mix_max(n_pe):
                dve.wait_ge(mix_pe, n_pe)
                link(V.tensor_reduce(mst[0:12, 0:1], ps[0:12, 5, 128:256], AX, ALU.max))
                V.tensor_scalar(mst[0:12, 1:2], mst[0:12, 0:1], -0.125, None, ALU.mult).then_inc(mix_dve, 1)

            def mix_norm(n_act):
                dve.wait_ge(mix_act, n_act)
                link(V.reciprocal(mst[0:12, 3:4], mst[0:12, 2:3]))
                V.tensor_scalar(awt[:], awt[:], mst[0:12, 3:4], None, ALU.mult).then_inc(mix_dve, 1)

            dve.wait_ge(wq_in, 16)
            dve.wait_ge(qkv_copied, 2)
            link(V.tensor_tensor(xn[:], qkv[:, 0:D], pa[:, 0:D], ALU.mult))
            head_scores()
            los(3)
            mix_max(1)
            mix_norm(1)
            los(4)
            los(5)
            los(6)
            dve.wait_ge(mix_pe, 3)
            V.tensor_tensor(halves(gqm[0:12, :]), ps[0:12, 5:7, 0:HALF], halves(wkm), ALU.mult).then_inc(mix_dve, 1)
            los(7)
            dve.wait_ge(qkv_copied, 3)
            dve.wait_ge(mix_pe, 4)
            link(V.tensor_tensor(halves(xn[:]), ps[:, 5:7, 0:HALF], halves(qkv[:, D:2 * D]), ALU.mult))
            head_scores()
            los(8)

            def alpha_diag(h):
                dve.wait_ge(al_out, h + 1)
                wait(dve, E_out, h)
                link(V.tensor_copy(al[:, 0:2], ps[:, 4, 0:2]))
                V.tensor_scalar(dg, ident[:], al[:, 0:1], None, ALU.mult).then_inc(diag_ready, 1)

            def scores(n, e_ap, z, ad):
                dve.wait_ge(E_out, n)
                link(V.tensor_scalar(z, e_ap, ad, None, ALU.add))
                link(V.scalar_tensor_tensor(z, z, 0.2, z, ALU.mult, ALU.max))
                link(V.tensor_tensor(z, z, cneg[:], ALU.add))
                link(V.tensor_reduce(mx[:, 0:1], z, AX, ALU.max))
                V.tensor_scalar(nm[:, 0:1], mx[:, 0:1], -1.0, None, ALU.mult).then_inc(score_ready, 1)

            def weights(n, z):
                dve.wait_ge(exp_done, n)
                link(V.tensor_tensor(z, z, cnt[:], ALU.mult))
                link(V.tensor_reduce(den[:, 0:1], z, AX, ALU.add))
                link(V.reciprocal(rcp[:, 0:1], den[:, 0:1]))
                V.tensor_scalar(z, z, rcp[:, 0:1], None, ALU.mult).then_inc(A_ready, 1)

            def bias_add(h):
                dve.wait_ge(agg_out, h + 1)
                a0 = PC["b1T"][0]
                for half in range(2):
                    b = (small[:, a0 + 6 * h + 3 * half:a0 + 6 * h + 3 * half + 3] if isinstance(h, int)
                         else small[:, bass.ds(h * 6 + (a0 + 3 * half), 3)])
                    ins = V.tensor_tensor(yb[:, HALF * half:HALF * (half + 1)].rearrange("p (b n) -> p b n", n=P),
                                          ps[:, 2 + half, 0:HALF].rearrange("p (b n) -> p b n", n=P),
                                          b.unsqueeze(2).broadcast_to([P, 3, P]), ALU.add)
                ins.then_inc(y_ready, 1)

            def elu(n):
                dve.wait_ge(ey_done, n)
                link(V.tensor_scalar(eb[:], eb[:], 1.0, -1.0, ALU.min, ALU.add))
                V.scalar_tensor_tensor(yb[:], yb[:], 0.0, eb[:], ALU.max, ALU.add).then_inc(elu_ready, 1)

            def o_lo(n):
                dve.wait_ge(oTh_ready, n)
                V.tensor_tensor(oTl[:], yb[:], oTh[:].bitcast(F32), ALU.subtract).then_inc(oTl_ready, 1)

            def bias_add(h):
                dve.wait_ge(agg_out, h + 1)
                a0 = PC["b1T"][0]
                for half in range(2):
                    b = (small[:, a0 + 6 * h + 3 * half:a0 + 6 * h + 3 * half + 3] if isinstance(h, int)
                         else small[:, bass.ds(h * 6 + (a0 + 3 * half), 3)])
                    ins = V.tensor_tensor(yb[:, HALF * half:HALF * (half + 1)].rearrange("p (b n) -> p b n", n=P),
                                          ps[:, 2 + half, 0:HALF].rearrange("p (b n) -> p b n", n=P),
                                          b.unsqueeze(2).broadcast_to([P, 3, P]), ALU.add)
                    ins.then_inc(y_ready, 1) if half else None

            mix_max(5)
            mix_norm(3)
            alpha_diag(0)
            los(9)
            scores(1, ps[:, 4, P:2 * P], zt1, al[:, 1:2])
            weights(1, zt1)
            los(10)
            dve.wait_ge(mix_pe, 7)
            V.tensor_tensor(halves(gqm[0:12, :]), ps[0:12, 5:7, 0:HALF], halves(hm), ALU.mult).then_inc(mix_dve, 1)
            dve.wait_ge(mix_pe, 8)
            dve.wait_ge(qkv_copied, 5)
            V.tensor_tensor(halves(qkv[:, 2 * D:3 * D]), ps[:, 5:7, 0:HALF], halves(qkv[:, 2 * D:3 * D]),
                            ALU.mult).then_inc(mix_dve, 1)
            bias_add(0)
            elu(1)
            o_lo(1)
            alpha_diag(1)

            def step(h, c, d, k):
                lo(c + 2, k + 2)
                scores(h, ps[:, 4, P:2 * P], zt1, al[:, 1:2])
                weights(h, zt1)
                lo(c + 3, k + 3)
                lo(c + 4, k + 4)
                bias_add(h - 1)
                elu(h)
                o_lo(h)
                alpha_diag(h)

            per = 2 * (4 + 3 + 1 + 1)
            k0 = ch.k
            with dve.Fori(2, H0, 2) as h:
                ch.base, ch.k = (per // 2) * h + (k0 - per), 0
                for d in range(2):
                    step(h + d, 3 * h + (3 + 3 * d), d, 9 + 3 * d)
                assert ch.k == per
            ch.base, ch.k = 0, k0 + per * (H0 - 2) // 2

            scores(8, ps[:, 4, P:2 * P], zt1, al[:, 1:2])
            weights(8, zt1)
            los(29)
            bias_add(7)
            elu(8)
            o_lo(8)
            dve.wait_ge(mix_act, 6)
            V.tensor_tensor(xTl[:].rearrange("p b n -> p (b n)")[:, 0:512], ps[:, 7, :],
                            xTh[:].rearrange("p b n -> p (b n)")[:, 0:512].bitcast(F32), ALU.subtract)
            V.tensor_tensor(xTl[:].rearrange("p b n -> p (b n)")[:, 512:768], ps[:, 4, 256:512],
                            xTh[:].rearrange("p b n -> p (b n)")[:, 512:768].bitcast(F32), ALU.subtract).then_inc(mix_dve, 1)
            los(30)
            los(31)
            los(32)
            link(V.tensor_tensor(xres[:], xres[:], qkv[:, 0:D], ALU.add))
            dve.wait_ge(as2_in, 16)
            dve.wait_ge(ad2_in, 16)
            dve.wait_ge(g_copied, 1)
            for i, a in enumerate((pa[:, 0:D], qkv[:, D:2 * D])):
                link(V.tensor_tensor(eb[:], hsb[:, 0, :], a, ALU.mult))
                link(V.tensor_reduce(al[:, i:i + 1], eb[:], AX, ALU.add))
            V.tensor_scalar(dg, ident[:], al[:, 0:1], None, ALU.mult).then_inc(diag_ready, 1)
            scores(9, ps[:, 4, P:2 * P], zt1, al[:, 1:2])
            weights(9, zt1)
            los(33)

            def residual(n, b0, s, v):
                dve.wait_ge(s, v)
                V.tensor_tensor(xres[:].rearrange("p (a n) -> p a n", a=2), ps[:, b0:b0 + 2, 0:HALF],
                                xres[:].rearrange("p (a n) -> p a n", a=2), ALU.add).then_inc(x_ready, 1)
                dve.wait_ge(x_ready, n)

            residual(1, 0, F_out, 1)
            layernorm(2)
            xT_lo(2)

            sc = stat[:, 128:136]
            sel = stat[:, 136:144]
            v8 = stat[:, 144:152]
            dve.wait_ge(router_out, 1)
            link(V.tensor_copy(sc, ps[:, 7, 0:8]))
            link(V.tensor_reduce(mx[:, 0:1], sc, AX, ALU.max))
            V.tensor_scalar(nm[:, 0:1], mx[:, 0:1], -1.0, None, ALU.mult).then_inc(rscore, 1)
            dve.wait_ge(rexp_done, 1)
            link(V.reciprocal(rcp[:, 0:1], den[:, 0:1]))
            link(V.tensor_scalar(sc, sc, rcp[:, 0:1], None, ALU.mult))
            link(V.tensor_tensor(sel, sc, sm("ebias"), ALU.add))
            link(V.max(v8, sel))
            link(V.max_index(stat[:, 152:160].bitcast(U32), v8, sel))
            link(V.tensor_copy(v8[:, 0:2], stat[:, 152:154].bitcast(U32)))
            link(V.tensor_scalar(sel, iota[:, 0:8], v8[:, 0:1], None, ALU.is_equal))
            link(V.scalar_tensor_tensor(sel, iota[:, 0:8], v8[:, 1:2], sel, ALU.is_equal, ALU.add))
            link(V.tensor_tensor(sel, sel, sc, ALU.mult))
            link(V.tensor_reduce(den[:, 0:1], sel, AX, ALU.add))
            link(V.tensor_scalar(den[:, 0:1], den[:, 0:1], 1e-9, None, ALU.add))
            link(V.reciprocal(rcp[:, 0:1], den[:, 0:1]))
            link(V.memset(comb[:, 24:27], 1.0))
            link(V.tensor_scalar(comb[:, 0:24].rearrange("p (e t) -> p e t", t=3),
                                 sel.unsqueeze(2).broadcast_to([P, 8, 3]), rcp[:, 0:1], None, ALU.mult))

            def hT_lo(j):
                dve.wait_ge(hTh_ready, j + 1)
                V.tensor_tensor(oTl[:, 0:FB], ps[:, 4, :], oTh[:, 0:FB].bitcast(F32), ALU.subtract).then_inc(hTl_ready, 1)

            def hid(j, d, done):
                dve.wait_ge(silu_done, j + 1)
                dve.wait_ge(used, done)
                wait(dve, T_out, j - 1)
                cj = comb[:, j:j + 1] if isinstance(j, int) else stat[:, bass.ds(j + 51, 1)]
                V.scalar_tensor_tensor(hhb[d], asb[d], cj, ps[:, 2 + d, :], ALU.mult, ALU.mult).then_inc(hh_ready, 1)

            los(34)
            hid(0, 0, 34)
            los(35)

            def fstep(j, c, d, k):
                lo(c + 2, k + 2)
                hT_lo(j - 1)
                lo(c + 3, k + 3)
                hid(j, d, c + 2)
                lo(c + 4, k + 4)

            with dve.Fori(1, FS, 2) as j:
                for d in range(2):
                    fstep(j + d, 3 * j + (31 + 3 * d), 1 - d, 34 + 3 * d)
            hT_lo(FS - 1)
            residual(2, 5, used, L1)
            layernorm(3)
            los(L1 + 1)
            xT_lo(3)

            los(L1 + 2)
            dve.wait_ge(ga_in, 16)
            dve.wait_ge(l1_act, 2)
            al4 = [al[:, 0:4], al[:, 4:8]]
            for i in range(2):
                link(V.tensor_tensor(eb[:, 0:256], gqm[:, 0:256], pa[:, 256 * i:256 * i + 256], ALU.mult))
                link(V.tensor_reduce(al4[i], eb[:, 0:256].rearrange("p (h c) -> p h c", c=64), AX, ALU.add))
            for h in range(4):
                ins = V.tensor_scalar(L1D[:, h * P:(h + 1) * P], ident[:], al[:, h:h + 1], None, ALU.mult)
            ins.then_inc(diag_ready, 1)
            los(L1 + 3)
            dve.wait_ge(l1_pe, 1)
            hd = lambda t, h: t[:, h * P:(h + 1) * P]
            for h in range(4):
                ins = V.tensor_scalar(hd(L1Z, h), ps[:, 6, h * P:(h + 1) * P], al[:, 4 + h:5 + h], None, ALU.add)
            link(ins)
            link(V.scalar_tensor_tensor(L1Z, L1Z, 0.2, L1Z, ALU.mult, ALU.max))
            for h in range(4):
                ins = V.tensor_tensor(hd(L1Z, h), hd(L1Z, h), cneg[:], ALU.add)
            link(ins)
            link(V.tensor_reduce(mx, L1Z.rearrange("p (h n) -> p h n", n=P), AX, ALU.max))
            V.tensor_scalar(nm, mx, -1.0, None, ALU.mult).then_inc(score_ready, 1)
            dve.wait_ge(exp_done, 13)
            for h in range(4):
                ins = V.tensor_tensor(hd(L1Z, h), hd(L1Z, h), cnt[:], ALU.mult)
            link(ins)
            link(V.tensor_reduce(den, L1Z.rearrange("p (h n) -> p h n", n=P), AX, ALU.add))
            link(V.tensor_scalar(den, den, 1e-16, None, ALU.add))
            link(V.reciprocal(rcp, den))
            for h in range(4):
                ins = V.tensor_scalar(hd(L1Z, h), hd(L1Z, h), rcp[:, h:h + 1], None, ALU.mult)
            ins.then_inc(A_ready, 1)
            los(L1 + 4)
            los(L1 + 5)
            los(L1 + 6)
            dve.wait_ge(l1_act, 12)
            for i in range(2):
                link(V.tensor_tensor(eb[:, 0:256], gqm[:, 256:512], pa[:, 512 + 256 * i:768 + 256 * i], ALU.mult))
                link(V.tensor_reduce(al[:, i:i + 1], eb[:, 0:256], AX, ALU.add))
            V.tensor_scalar(hd(L1D, 0), ident[:], al[:, 0:1], None, ALU.mult).then_inc(diag_ready, 1)
            sums = stat[:, 124:136]
            sq = stat[:, 100:112]
            rn = stat[:, 112:124]
            for i, t in enumerate((qT, kT)):
                link(V.tensor_reduce(sums[:, 6 * i:6 * i + 6], t.rearrange("p (b n) -> p b n", n=P), AX, ALU.add))
                link(V.tensor_tensor(eb[:], t, t, ALU.mult))
                ins = V.tensor_reduce(sq[:, 6 * i:6 * i + 6], eb[:].rearrange("p (b n) -> p b n", n=P), AX, ALU.add)
                ins.then_inc(l1_dve, 1)
            dve.wait_ge(l1_dve, 2)
            dve.wait_ge(l1_pe, 8)
            z = hd(L1Z, 0)
            link(V.tensor_scalar(z, ps[:, 6, 0:P], al[:, 1:2], None, ALU.add))
            link(V.scalar_tensor_tensor(z, z, 0.2, z, ALU.mult, ALU.max))
            link(V.tensor_tensor(z, z, cneg[:], ALU.add))
            link(V.tensor_reduce(mx[:, 0:1], z, AX, ALU.max))
            V.tensor_scalar(nm[:, 0:1], mx[:, 0:1], -1.0, None, ALU.mult).then_inc(score_ready, 1)
            dve.wait_ge(l1_pool, 1)
            fct = stat[:, 136:142]
            link(V.tensor_tensor(sums, sums, rn, ALU.mult))
            link(V.tensor_tensor(fct, sums[:, 0:6], sums[:, 6:12], ALU.mult))
            link(V.tensor_scalar(fct, fct, float(N), None, ALU.add))
            link(V.reciprocal(fct, fct))
            link(V.tensor_tensor(rn[:, 0:6], rn[:, 0:6], fct, ALU.mult))
            dve.wait_ge(exp_done, 14)
            link(V.tensor_tensor(z, z, cnt[:], ALU.mult))
            link(V.tensor_reduce(den[:, 0:1], z, AX, ALU.add))
            link(V.tensor_scalar(den[:, 0:1], den[:, 0:1], 1e-16, None, ALU.add))
            link(V.reciprocal(rcp[:, 0:1], den[:, 0:1]))
            V.tensor_scalar(z, z, rcp[:, 0:1], None, ALU.mult).then_inc(A_ready, 1)
            b6 = lambda t: t.rearrange("p (b n) -> p b n", n=P)
            bc = lambda t: t.unsqueeze(2).broadcast_to([P, 6, P])
            link(V.tensor_tensor(b6(kT), b6(kT), bc(rn[:, 6:12]), ALU.mult))
            link(V.tensor_tensor(b6(qT), b6(qT), bc(rn[:, 0:6]), ALU.mult))
            link(V.tensor_tensor(qT, qT, kT, ALU.mult))
            dve.wait_ge(l1_act, 13)
            link(V.tensor_tensor(vT, vT, kT, ALU.mult))
            V.tensor_tensor(qT, qT, vT, ALU.mult).then_inc(l1_dve, 1)
            dve.wait_ge(l1_act, 19)
            V.tensor_tensor(xTl[:].rearrange("p b n -> p (b n)"), qT, xTh[:].rearrange("p b n -> p (b n)").bitcast(F32),
                            ALU.subtract).then_inc(l1_dve, 1)
            los(L1 + 7)
            residual(3, 2, F_out, 2)

            layernorm(4)
            for g in range(2):
                dve.wait_ge(w1h_ready, g + 1)
                V.tensor_tensor(w1l[g], w1[g], w1h[g].bitcast(F32), ALU.subtract).then_inc(w1l_ready, 1)
            for s4 in range(4):
                dve.wait_ge(zh_ready, s4 + 1)
                r = slice(32 * s4, 32 * s4 + 32)
                own = lambda t: t[r, :].rearrange("p (g s n) -> p g s n", g=2, s=4)[:, :, s4, :]
                V.tensor_tensor(own(zl), ps[r, 6, 0:256].rearrange("p (g n) -> p g n", g=2), own(zh).bitcast(F32),
                                ALU.subtract).then_inc(zl_ready, 1)
            dve.wait_ge(f_act, 3)
            for s in range(8):
                ins = V.max(tv[:, 8 * s:8 * s + 8], scs[:, 64 * s:64 * s + 64])
            link(ins)
            v3 = tv.rearrange("p (s k) -> p s k", k=8)
            by_s = lambda t: t.rearrange("p (s m) -> p s m", s=8)
            V.tensor_tensor(by_s(se), by_s(scs), v3[:, :, 0:1].broadcast_to([P, 8, 64]), ALU.subtract).then_inc(f_dve, 1)
            dve.wait_ge(f_dve, 1)
            link(V.memset(v3[:, :, 4:8], 3e38))
            for s in range(8):
                ins = V.match_replace(out=taken[:, 64 * s:64 * s + 64], in_to_replace=tv[:, 8 * s:8 * s + 8],
                                      in_values=scs[:, 64 * s:64 * s + 64], imm_value=-3e38)
            link(ins)
            link(V.tensor_tensor(taken, taken, scs, ALU.not_equal))
            dve.wait_ge(f_act, 4)
            link(V.tensor_tensor(se, se, taken, ALU.mult))
            link(V.tensor_reduce(tden, by_s(se), AX, ALU.add))
            link(V.reciprocal(tden, tden))
            link(V.tensor_tensor(by_s(ww), by_s(se), tden.unsqueeze(2).broadcast_to([P, 8, 64]), ALU.mult))
            w4 = wcat.rearrange("p (s a m) -> p s a m", s=8, a=2)
            w3 = ww.rearrange("p (s m) -> p s m", s=8)
            link(V.tensor_copy(w4[:, :, 0, :].bitcast(F32R), w3))
            V.tensor_tensor(w4[:, :, 1, :], w3, w4[:, :, 0, :], ALU.subtract).then_inc(f_dve, 1)
            dve.wait_ge(f_pe, 3)
            V.tensor_copy(wTs.rearrange("p (a n) -> p a n", a=2), ps[:, 4:6, :]).then_inc(f_dve, 1)

            def weigh_hidden(u, d):
                dve.wait_ge(gelu_done, u + 1)
                dve.wait_ge(spread_out, u + 1)
                b = hg[:, 512 * d:512 * d + 512]
                V.tensor_tensor(b, b, ps[:, 4 + d % 2, :], ALU.mult).then_inc(weighted, 1)

            with dve.Fori(0, UNITS, 4) as u:
                for d in range(4):
                    weigh_hidden(u + d, d)
            residual(4, 2, F_out, 3)

        @block.tensor
        def _(pe):
            mm = nc.tensor.matmul

            def ready(c):
                pe.wait_ge(lo_ready, c + 1)

            def part3(out, sh, sl, wh, wl, first, last, shared=False):
                mm(out, sh, wh, start=first, stop=False, skip_group_check=shared)
                mm(out, sh, wl, start=False, stop=False, skip_group_check=shared)
                return mm(out, sl, wh, start=False, stop=last, skip_group_check=shared)

            def up(out, k, n, xh, xl):
                for t in range(KD):
                    ins = part3(out, xh[:, t, :], xl[:, t, :], whi[:, k % S, t * n:(t + 1) * n],
                                wlo[:, k % S, t * n:(t + 1) * n], t == 0, t == KD - 1)
                return ins

            def down(banks, k, off, ts, sh, sl, first=False, last=False):
                for i, t in enumerate(ts):
                    for half in range(2):
                        a = off + i * D + half * HALF
                        ins = part3(ps[:, banks[half], 0:HALF], sh[:, t * P:(t + 1) * P], sl[:, t * P:(t + 1) * P],
                                    whi[:, k % S, a:a + HALF], wlo[:, k % S, a:a + HALF],
                                    first and i == 0, last and i == len(ts) - 1)
                return ins

            def transpose6(src, n):
                pe.wait_ge(xn_ready, n)
                for b in range(KD):
                    ins = nc.tensor.transpose(ps[:, 2 + b // 3, (b % 3) * P:(b % 3 + 1) * P], src[:, b * P:(b + 1) * P], ident[:])
                ins.then_inc(xT_out, 1)

            def x_split(n):
                pe.wait_ge(xTh_ready, n)
                pe.wait_ge(xTl_ready, n)

            def bias(banks, row, n, first=False, last=False):
                pe.wait_ge(brow_in, 48)
                for half in range(2):
                    ins = mm(ps[:, banks[half], 0:HALF], ones[row:row + n, :], brow[row:row + n, half * HALF:(half + 1) * HALF],
                             start=first, stop=last)
                return ins

            pe.wait_ge(consts, 6)
            transpose6(xn, 1)
            pe.wait_ge(onehots, 1)
            for t in range(16):
                ins = mm(ps[:, 4, 0:P], doh[:, t, :], soh[:, t, :], start=t == 0, stop=t == 15)
            ins.then_inc(count_out, 1)

            def up_chunk(c, k, n, bank):
                ready(c)
                up(ps[:, bank, 0:n], k, n, xTh, xTl).then_inc(used, 1)

            def to_rows(v):
                pe.wait_ge(mix_dve, v)
                nc.tensor.transpose(ps[0:12, 5, 128:256], mixa, ident[:]).then_inc(mix_pe, 1)

            def to_columns(v):
                pe.wait_ge(mix_dve, v)
                nc.tensor.transpose(ps[:, 5, 256:268], awt[:], ident[0:12, 0:12]).then_inc(mix_pe, 1)

            def weigh(v, t):
                pe.wait_ge(mix_act, v)
                for half in range(2):
                    ins = mm(ps[0:12, 5 + half, 0:HALF], mixa, t[:, half * HALF:(half + 1) * HALF], start=True, stop=True)
                ins.then_inc(mix_pe, 1)

            def spread(v):
                pe.wait_ge(mix_dve, v)
                for half in range(2):
                    ins = mm(ps[:, 5 + half, 0:HALF], ones[0:12, :], gqm[0:12, half * HALF:(half + 1) * HALF],
                             start=True, stop=True)
                ins.then_inc(mix_pe, 1)

            def src_spread(h, n):
                pe.wait_ge(diag_ready, n)
                mm(ps[:, 4, P:2 * P], ones[:], dg, start=True, stop=True).then_inc(E_out, 1)

            def A_transpose(n):
                pe.wait_ge(A_ready, n)
                nc.tensor.transpose(ps[:, 4, P:2 * P], zt1, ident[:]).then_inc(AT_out, 1)

            def h_transpose(h, d):
                pe.wait_ge(h_copied, 2 * h + 2)
                wait(pe, hT_copied, 2 * h)
                for b in range(4):
                    nc.tensor.transpose(ps[:, 7, b * P:(b + 1) * P], hsb[:, d, b * P:(b + 1) * P], ident[:])
                wait(pe, AT_copied, h)
                for b in range(4, 6):
                    ins = nc.tensor.transpose(ps[:, 4, (b - 2) * P:(b - 1) * P], hsb[:, d, b * P:(b + 1) * P], ident[:])
                ins.then_inc(hT_out, 1)

            def aggregate(h, d):
                pe.wait_ge(AT_copied, h + 1)
                wait(pe, y_ready, h)
                for b in range(KD):
                    ins = mm(ps[:, 2 + b // 3, (b % 3) * P:(b % 3 + 1) * P], hsb[:, d, b * P:(b + 1) * P], ATs,
                             start=True, stop=True)
                ins.then_inc(agg_out, 1)

            def alphas(h):
                pe.wait_ge(hT_copied, 2 * h + 2)
                for b in range(KD):
                    a = (small[:, 12 * h + 2 * b:12 * h + 2 * b + 2] if isinstance(h, int)
                         else small[:, bass.ds(h * 12 + 2 * b, 2)])
                    ins = mm(ps[:, 4, 0:2], hTs[:, b * P:(b + 1) * P], a, start=b == 0, stop=b == KD - 1)
                ins.then_inc(al_out, 1)

            def zero_start(banks):
                for b in banks:
                    mm(ps[:, b, 0:HALF], brow[96:97, 0:P], brow[96:97, 0:HALF], start=True, stop=False)

            x_split(1)
            up_chunk(0, 0, 512, 0)
            up_chunk(1, 1, 512, 1)
            up_chunk(2, 2, 512, 2)
            to_rows(1)
            up_chunk(3, 3, 512, 3)
            to_columns(3)
            up_chunk(4, 4, 256, 7)
            weigh(2, qkv[:, 0:D])
            pe.wait_ge(qkv_copied, 1)
            up_chunk(5, 5, 512, 0)
            spread(4)
            pe.wait_ge(qkv_copied, 2)
            up_chunk(6, 6, 256, 1)
            pe.wait_ge(qkv_copied, 5)
            pe.wait_ge(small_in, 16)
            h_transpose(0, 0)
            to_rows(5)
            alphas(0)
            up_chunk(7, 7, 512, 0)
            to_columns(7)
            src_spread(0, 1)
            up_chunk(8, 8, 256, 1)
            weigh(4, qkv[:, D:2 * D])
            A_transpose(1)
            h_transpose(1, 1)
            spread(8)
            aggregate(0, 0)
            alphas(1)
            pe.wait_ge(mix_dve, 9)
            zero_start((5, 6))

            def step(h, c, d, k):
                pe.wait_ge(h_copied, 2 * h - 1)
                up_chunk(c, k, 512, 0)
                src_spread(h - 1, h)
                ready(c + 1)
                pe.wait_ge(h_copied, 2 * h)
                up(ps[:, 1, 0:256], k + 1, 256, xTh, xTl).then_inc(hb_out, 1)
                pe.wait_ge(oTl_ready, h - 1)
                down((5, 6), k + 1, 1536, (0, 1), oTh, oTl).then_inc(used, 1)
                A_transpose(h)
                h_transpose(h, d)
                aggregate(h - 1, 1 - d)
                ready(c + 2)
                down((5, 6), k + 2, 0, (2, 3, 4, 5), oTh, oTl).then_inc(used, 1)
                alphas(h)

            with pe.Fori(2, H0, 2) as h:
                for d in range(2):
                    step(h + d, 3 * h + (3 + 3 * d), d, 9 + 3 * d)

            src_spread(7, 8)
            ready(27)
            pe.wait_ge(oTl_ready, 7)
            down((5, 6), 27, 0, (0, 1), oTh, oTl)
            A_transpose(8)
            ready(28)
            down((5, 6), 28, 0, (2, 3, 4, 5), oTh, oTl).then_inc(used, 1)
            aggregate(7, 1)
            pe.wait_ge(hT_copied, 16)
            for b in range(4):
                nc.tensor.transpose(ps[:, 7, b * P:(b + 1) * P], qkv[:, 2 * D + b * P:2 * D + (b + 1) * P], ident[:])
            for b in range(4, 6):
                ins = nc.tensor.transpose(ps[:, 4, (b - 2) * P:(b - 1) * P], qkv[:, 2 * D + b * P:2 * D + (b + 1) * P], ident[:])
            ins.then_inc(mix_pe, 1)
            xhf, xlf = (t[:].rearrange("p b n -> p (b n)") for t in (xTh, xTl))
            ready(29)
            pe.wait_ge(mix_dve, 10)
            pe.wait_ge(h_copied, 16)
            down((0, 1), 29, 0, (0, 1, 2), xhf, xlf, first=True).then_inc(used, 1)
            pe.wait_ge(oTl_ready, 8)
            down((5, 6), 27, 1536, (0, 1), oTh, oTl).then_inc(used, 1)
            ready(30)
            down((0, 1), 30, 0, (3, 4, 5), xhf, xlf).then_inc(used, 1)
            ready(31)
            down((5, 6), 31, 0, (2, 3, 4, 5), oTh, oTl, last=True).then_inc(used, 1)
            bias((0, 1), 0, 2)
            src_spread(8, 9)
            A_transpose(9)
            pe.wait_ge(AT_copied, 9)
            for half in range(2):
                ins = mm(ps[:, half, 0:HALF], ATs, hsb[:, 0, half * HALF:(half + 1) * HALF], start=False, stop=True)
            ins.then_inc(F_out, 1)

            transpose6(xn, 2)
            x_split(2)
            a0 = PC["wr"][0]
            for i in range(2 * KD):
                t, x = i // 2, (xTh, xTl)[i % 2]
                ins = mm(ps[:, 7, 0:8], x[:, t, :].bitcast(F32), small[:, a0 + 8 * t:a0 + 8 * t + 8],
                         start=i == 0, stop=i == 2 * KD - 1)
            ins.then_inc(router_out, 1)
            zero_start((5, 6))

            def T(j, d):
                pe.wait_ge(hh_ready, j + 1)
                wait(pe, hTl_ready, j)
                for b in range(4):
                    ins = nc.tensor.transpose(ps[:, 4, b * P:(b + 1) * P], hhb[d][:, b * P:(b + 1) * P], ident[:])
                ins.then_inc(T_out, 1)

            up_chunk(FFN0, FFN0, 512, 0)
            up_chunk(FFN0 + 1, FFN0 + 1, 512, 2)

            def fstep(j, c, d, k):
                wait(pe, silu_done, j - 1)
                up_chunk(c, k, 512, d)
                T(j - 1, 1 - d)
                up_chunk(c + 1, k + 1, 512, 2 + d)
                ready(c + 2)
                pe.wait_ge(hTl_ready, j)
                down((5, 6), k + 2, 0, (0, 1, 2, 3), oTh, oTl).then_inc(used, 1)

            with pe.Fori(1, FS, 2) as j:
                for d in range(2):
                    fstep(j + d, 3 * j + (31 + 3 * d), 1 - d, 34 + 3 * d)
            T(FS - 1, 0)
            ready(L1 - 1)
            pe.wait_ge(hTl_ready, FS)
            down((5, 6), L1 - 1, 0, (0, 1, 2, 3), oTh, oTl, last=True).then_inc(used, 1)

            transpose6(xn, 3)
            x_split(3)
            up_chunk(L1, L1, 512, 0)
            up_chunk(L1 + 1, L1 + 1, 256, 5)
            up_chunk(L1 + 2, L1 + 2, 512, 1)

            def l1(s, v):
                pe.wait_ge(s, v)

            l1(diag_ready, 10)
            mm(ps[:, 6, :], ones[:], L1D, start=True, stop=True).then_inc(l1_pe, 1)
            up_chunk(L1 + 3, L1 + 3, 512, 2)
            up_chunk(L1 + 4, L1 + 4, 512, 3)
            l1(A_ready, 10)
            for h in range(4):
                ins = nc.tensor.transpose(ps[:, 6, h * P:(h + 1) * P], L1Z[:, h * P:(h + 1) * P], ident[:])
            ins.then_inc(l1_pe, 1)
            up_chunk(L1 + 5, L1 + 5, 256, 4)
            l1(l1_act, 6)
            for h in range(4):
                ins = mm(ps[64 * (h % 2):64 * (h % 2) + 64, 7, (h // 2) * P:(h // 2 + 1) * P],
                         gqm[:, 64 * h:64 * h + 64], L1AT[:, h * P:(h + 1) * P], start=True, stop=True)
            ins.then_inc(l1_pe, 1)

            def tr6(src, b0):
                for b in range(KD):
                    ins = nc.tensor.transpose(ps[:, b0 + b // 3, (b % 3) * P:(b % 3 + 1) * P], src[:, b * P:(b + 1) * P], ident[:])
                ins.then_inc(l1_pe, 1)

            l1(l1_act, 7)
            tr6(qkv[:, 0:D], 0)
            tr6(qkv[:, D:2 * D], 2)
            wsm = raw[:, (NCH - 1) % R, :]
            l1(landed[(NCH - 1) % R], landed_at(NCH - 1))
            l1(l1_act, 9)
            for t in range(2):
                ins = mm(ps[:, 5, 256:512], gT[:, t * P:(t + 1) * P], wsm[:, 256 * t:256 * t + 256], start=t == 0, stop=t == 1)
            ins.then_inc(l1_pe, 1)
            l1(l1_act, 10)
            tr6(qkv[:, 2 * D:3 * D], 0)
            l1(diag_ready, 11)
            mm(ps[:, 6, 0:P], ones[:], L1D[:, 0:P], start=True, stop=True).then_inc(l1_pe, 1)
            l1(l1_act, 11)
            bias((2, 3), 32, 2, first=True)
            l1(A_ready, 11)
            nc.tensor.transpose(ps[:, 6, 0:P], L1Z[:, 0:P], ident[:]).then_inc(l1_pe, 1)
            l1(l1_act, 14)
            for b in range(2):
                ins = mm(ps[:, 7, b * P:(b + 1) * P], gqm[:, 256 + b * P:256 + (b + 1) * P], L1AT[:, 0:P], start=True, stop=True)
            ins.then_inc(l1_pe, 1)
            l1(l1_act, 16)
            for b in range(2):
                for t in range(2):
                    ins = mm(ps[:, 7, 256 + b * P:256 + (b + 1) * P], wsm[:, 512 + 256 * t + b * P:512 + 256 * t + (b + 1) * P],
                             gT[:, t * P:(t + 1) * P], start=t == 0, stop=t == 1)
            ins.then_inc(l1_pe, 1)
            l1(l1_act, 18)
            for t in range(2):
                for half in range(2):
                    ins = mm(ps[:, 2 + half, 0:HALF], gT2[:, t * P:(t + 1) * P],
                             wsm[:, 1024 + D * t + half * HALF:1024 + D * t + (half + 1) * HALF], start=False, stop=False)
            ins.then_inc(l1_pe, 1)
            l1(l1_dve, 4)
            ready(L1 + 6)
            down((2, 3), L1 + 6, 0, (0, 1, 2), xhf, xlf).then_inc(used, 1)
            ready(L1 + 7)
            down((2, 3), L1 + 7, 0, (3, 4, 5), xhf, xlf, last=True).then_inc(F_out, 1)

            transpose6(xn, 4)
            pe.wait_ge(f_act, 1)
            pe.wait_ge(fw_in, 16)
            for g in range(2):
                for t in range(KD):
                    a = (2 * t + g) * P
                    mm(ps[:, 6, g * P:(g + 1) * P], fw("P")[:, a:a + P], hTs[:, t * P:(t + 1) * P], start=t == 0, stop=False)
                ins = mm(ps[:, 6, g * P:(g + 1) * P], fw("one")[0:1, :], ones[0:1, :], start=False, stop=True)
            ins.then_inc(f_pe, 1)
            pe.wait_ge(f_act, 2)
            for g in range(2):
                ins = mm(ps[:, 4, 256 * g:256 * g + 256], zT[:, g * P:(g + 1) * P], fw("C")[:, 256 * g:256 * g + 256],
                         start=True, stop=True)
            ins.then_inc(f_pe, 1)

            def hidden(u):
                wait(pe, gelu_done, u - 3)
                b, g = u // 2, u % 2
                wh, wl = (t[:, b * P:(b + 1) * P] for t in (w1h[g], w1l[g]))
                h, l = (t[:, 512 * g:512 * g + 512] for t in (zh, zl))
                mm(ps[:, u % 4, :], wh, h, start=True, stop=False)
                mm(ps[:, u % 4, :], wh, l, start=False, stop=False)
                mm(ps[:, u % 4, :], wl, h, start=False, stop=True).then_inc(hid_out, 1)

            def spread_weights(u):
                wait(pe, weighted, u - 1)
                b, g = u // 2, u % 2
                mm(ps[:, 4 + g, :], expand[:, b * P:(b + 1) * P], wTs[:, 512 * g:512 * g + 512],
                   start=True, stop=True).then_inc(spread_out, 1)

            def project(u, last=False):
                pe.wait_ge(weighted, u + 1)
                b, g = u // 2, u % 2
                for s4 in range(4):
                    at = ((4 * g + s4) * 16 + b) * 16
                    ins = mm(ps[32 * s4:32 * s4 + 16, 6 + g, 0:P], fw("W2")[:, at:at + 16],
                             hg[:, 512 * (u % 4) + s4 * P:512 * (u % 4) + (s4 + 1) * P], start=False, stop=last,
                             skip_group_check=True)
                ins.then_inc(Y_out, 1)

            pe.wait_ge(zl_ready, 4)
            pe.wait_ge(w1l_ready, 2)
            for u in range(4):
                hidden(u)
            for g in range(2):
                mm(ps[:, 6 + g, 0:P], brow[96:97, 0:P], brow[96:97, 0:P], start=True, stop=False, skip_group_check=True)
            pe.wait_ge(f_dve, 2)
            for s in range(8):
                ins = nc.tensor.transpose(ps[:, 4 + s // 4, (s % 4) * P:(s % 4 + 1) * P], wcat[:, s * P:(s + 1) * P], ident[:])
            ins.then_inc(f_pe, 1)
            pe.wait_ge(f_dve, 3)
            pe.wait_ge(f_pool, 1)
            spread_weights(0)
            spread_weights(1)
            for s in range(8):
                mm(ps[32 * (s % 4):32 * (s % 4) + 16, 6 + s // 4, 0:P], fw("b2")[:, 16 * s:16 * s + 16],
                   wTs[:, s * P:(s + 1) * P].bitcast(F32), start=False, stop=False, skip_group_check=True)
            for u in range(UNITS):
                if u + 4 < UNITS:
                    hidden(u + 4)
                project(u, last=u >= UNITS - 2)
                if u + 2 < UNITS:
                    spread_weights(u + 2)
            pe.wait_ge(f_act, 5)
            for b in range(2):
                for g in range(2):
                    ins = mm(ps[:, 1, b * P:(b + 1) * P], fw("G1")[:, 256 * g + b * P:256 * g + (b + 1) * P],
                             cT[:, g * P:(g + 1) * P], start=g == 0, stop=g == 1)
            ins.then_inc(f_pe, 1)
            bias((2, 3), 64, 1, first=True)
            pe.wait_ge(f_act, 7)
            pe.wait_ge(g2_in, 16)
            for t in range(2):
                for half in range(2):
                    ins = mm(ps[:, 2 + half, 0:HALF], fT[:, t * P:(t + 1) * P],
                             qkv[:, D * t + half * HALF:D * t + (half + 1) * HALF], start=False, stop=t == 1)
            ins.then_inc(F_out, 1)


def kernel(**inputs):
    import concourse.bacc as bacc
    import numpy as np
    from concourse.bass_utils import run_bass_kernel_spmd

    a = {k: np.asarray(v) for k, v in inputs.items()}

    def up(w, c0, n):
        return w[:, c0:c0 + n].reshape(KD, P, n).transpose(1, 0, 2).reshape(P, KD * n)

    def down(w, k0, n):
        return w[k0 * P:(k0 + n) * P].reshape(n, P, D).transpose(1, 0, 2).reshape(P, n * D)

    stream = np.zeros((NCH, P, SLOT), np.float32)

    def put(c, *parts):
        at = 0
        for p in parts:
            stream[c, :, at:at + p.shape[1]] = p
            at += p.shape[1]
        assert at == chunk_len(c)

    def put_qkv(cs, w):
        for i, c in enumerate(cs):
            put(c, up(w, 512 * i, 512 if i < 4 else 256))

    w1, w2 = a["L0_gnn_W1"], a["L0_gnn_W2"]
    put_qkv(range(5), a["L0_mix_Wqkv"].T)
    for h in range(2):
        put(5 + 2 * h, up(w1, D * h, 512))
        put(6 + 2 * h, up(w1, D * h + 512, 256))
    for h in range(2, H0):
        put(3 * h + 3, up(w1, D * h, 512))
        put(3 * h + 4, up(w1, D * h + 512, 256), down(w2, KD * (h - 2), 2))
        put(3 * h + 5, down(w2, KD * (h - 2) + 2, 4))
    put(27, down(w2, KD * 6, 2), down(w2, KD * 7, 2))
    put(28, down(w2, KD * 6 + 2, 4))
    wp = a["L0_mix_Wp"].T
    put(29, down(wp, 0, 3))
    put(30, down(wp, 3, 3))
    put(31, down(w2, KD * 7 + 2, 4))
    for e in range(9):
        wg, wu, wd = ((a["L0_ffn_Wg"][e], a["L0_ffn_Wu"][e], a["L0_ffn_Wd"][e]) if e < 8
                      else (a["L0_ffn_sg"], a["L0_ffn_su"], a["L0_ffn_sd"]))
        for b in range(3):
            j = 3 * e + b
            put(FFN0 if j == 0 else 31 + 3 * j, up(wg.T, FB * b, FB))
            put(FFN0 + 1 if j == 0 else 32 + 3 * j, up(wu.T, FB * b, FB))
            put(36 + 3 * j if j < FS - 1 else L1 - 1, down(wd.T, 4 * b, 4))
    put_qkv((L1, L1 + 2, L1 + 3, L1 + 4, L1 + 5), a["L1_mix_w_qkv"])
    put(L1 + 1, up(a["L1_gnn_W1"], 0, 256))
    put(L1 + 6, down(a["L1_mix_w_proj"], 0, 3))
    put(L1 + 7, down(a["L1_mix_w_proj"], 3, 3))
    sq = lambda w: w.reshape(2, P, 256).transpose(1, 0, 2).reshape(P, 512)
    put(L1 + 8, sq(a["L1_gnn_W2"]), sq(a["L1_gnn_Wm1"]), down(a["L1_gnn_Wm2"], 0, 2))

    part = lambda v, n: v.reshape(n, P).T
    a1 = np.stack([a["L0_gnn_a_src1"], a["L0_gnn_a_dst1"]], -1)
    small = np.concatenate([
        a1.reshape(H0, KD, P, 2).transpose(2, 0, 1, 3).reshape(P, 96),
        part(a["L0_gnn_b1"], 48),
        a["L0_ffn_w_router"].T.reshape(KD, P, 8).transpose(1, 0, 2).reshape(P, 48),
        np.broadcast_to(a["L0_ffn_expert_bias"], (P, 8)),
        part(a["L1_gnn_b1"], 2), part(a["L1_gnn_b2"], 2), part(a["L1_gnn_bm1"], 2), part(a["L1_ffn_g1b"], 2)], 1)
    rows = lambda v, n=P: np.broadcast_to(v.reshape(1, -1), (n, v.size))
    ga = np.concatenate([rows(a["L1_gnn_a_src1"]), rows(a["L1_gnn_a_dst1"]),
                         rows(a["L1_gnn_a_src2"]), rows(a["L1_gnn_a_dst2"])], 1)
    a2b = np.concatenate([rows(a["L0_gnn_a_src2"]), rows(a["L0_gnn_a_dst2"])], 1)
    brow = np.stack([a["L0_gnn_b2"], a["L0_mix_bp"], a["L1_gnn_bm2"], a["L1_mix_b_proj"], a["L1_ffn_g2b"]])

    fwt = np.zeros((P, NF), np.float32)

    def place(name, v):
        fwt[:, FC[name][0]:FC[name][1]] = v.reshape(P, -1)

    pz = np.zeros((D, 2, 4, 32), np.float32)
    pz[:, :, :, 0:16] = a["L1_ffn_P"].reshape(2, 4, D, 16).transpose(2, 0, 1, 3)
    place("P", pz.reshape(KD, P, 2 * P).transpose(1, 0, 2))
    g1 = np.zeros((4, 32, 2, 256), np.float32)
    g1[:, 0:16] = a["L1_ffn_G1"].reshape(2, 4, 16, 256).transpose(1, 2, 0, 3)
    place("G1", g1)
    one = np.zeros((P, 4, 32), np.float32)
    one[0, :, 16] = 1.0
    place("one", one)
    cc = np.zeros((4, 32, 2, 4, 64), np.float32)
    bb = np.zeros((2, 64, 8, 16), np.float32)
    ww = np.zeros((4, 32, 2, 2048), np.float32)
    for s in range(8):
        cc[s % 4, 0:16, s // 4, s % 4] = a["L1_ffn_C"][s].T
        bb[:, :, s] = a["L1_ffn_b2"][s]
        ww[s % 4, 0:16, s // 4] = a["L1_ffn_W1"][s].transpose(1, 0, 2).reshape(16, 2048)
        ww[s % 4, 16, s // 4] = a["L1_ffn_b1"][s].reshape(2048)
    place("C", cc)
    place("W1", ww)
    place("b2", bb)
    place("W2", a["L1_ffn_W2"].reshape(8, 16, 4, 32, 16).transpose(2, 3, 0, 1, 4))

    arrays = {
        "x_in_d": a["x"], "src_d": a["src"].reshape(P, 16), "dst_d": a["dst"].reshape(P, 16), "stream_d": stream,
        "small_d": small, "wqb_d": rows(a["L0_mix_w_q"]), "wk_d": rows(a["L0_mix_w_k"], 12), "a2b_d": a2b, "ga_d": ga,
        "brow_d": brow, "fw_d": fwt, "g2_d": down(a["L1_ffn_G2"], 0, 2),
    }
    arrays = {k: np.ascontiguousarray(v) for k, v in arrays.items()}
    nc = bacc.Bacc("TRN2", target_bir_lowering=False, num_devices=1)
    aps = [nc.dram_tensor(k, v.shape, mybir.dt.from_np(v.dtype), kind="ExternalInput").ap() for k, v in arrays.items()]
    out = nc.dram_tensor("out_d", (N, D), F32, kind="ExternalOutput").ap()
    build(nc, *aps, out)
    return run_bass_kernel_spmd(nc, [arrays], core_ids=[0]).results[0]["out_d"]
```

```python
from contextlib import ExitStack

import concourse.bass as bass
from concourse import mybir

P = 128
N = 128
D = 768
KD = D // P
HALF = D // 2
SLOT = 3072
R = 6
S = 3
H0 = 8
FS = 27
FB = 512

QKV0 = 0
TAIL0 = 27
FFN0 = 32
L1 = FFN0 + 3 * FS
NCH = L1 + 9

F32 = mybir.dt.float32
F32R = mybir.dt.float32r
BF16 = mybir.dt.bfloat16
I32 = mybir.dt.int32
U32 = mybir.dt.uint32
ALU = mybir.AluOpType
ACT = mybir.ActivationFunctionType
AX = mybir.AxisListType.X

PC = {}
_at = 0
for _n, _w in (("a1T", 96), ("b1", P), ("wr", 48), ("ebias", 8), ("gb1", 2), ("gb2", 2), ("bm1", 2), ("fg1b", 2)):
    PC[_n] = (_at, _at + _w)
    _at += _w
NSMALL = _at

FC = {}
_at = 0
for _n, _w in (("P", 2 * D), ("C", 512), ("W1", 4096), ("W2", 2048), ("b2", 128), ("G1", 512), ("cst", 4)):
    FC[_n] = (_at, _at + _w)
    _at += _w
NF = _at
EPS = 1e-5
UNITS = 32
BIG = -1e30


def chunk_len(c):
    if c in (4, 6, 8, 31, L1, L1 + 5):
        return 1536
    if c in (L1 + 6, L1 + 7):
        return 2304
    if c == NCH - 1:
        return 2560
    return SLOT


def landed_at(c):
    return 16 * (c // R + 1)


def build(nc, x_d, src_d, dst_d, stream_d, small_d, wqb_d, wk_d, a2b_d, ga_d, brow_d, fw_d, w1b_d, g2_d, out_d):
    with ExitStack() as ctx:
        def sb(name, shape, dt=F32):
            return ctx.enter_context(nc.sbuf_tensor(name, shape, dt))

        def sem(name):
            return ctx.enter_context(nc.semaphore(name))

        ps = ctx.enter_context(nc.psum_tensor("ps", [P, 8, 512], F32))

        raw = sb("raw", [P, R, SLOT])
        whi = sb("whi", [P, S, SLOT], F32R)
        wlo = sb("wlo", [P, S, SLOT], F32R)
        small = sb("small", [P, NSMALL])
        b1s = sb("b1s", [112, P], F32R)
        pick = sb("pick", [112, 48], F32R)
        pa = sb("pa", [P, 1024])
        xres = sb("xres", [P, D])
        xn = sb("xn", [P, D])
        xTh = sb("xTh", [P, KD, P], F32R)
        xTl = sb("xTl", [P, KD, P], F32R)
        ident = sb("ident", [P, P])
        ones = sb("ones", [P, P])
        iota = sb("iota", [P, P])
        cnt = sb("cnt", [P, P])
        cneg = sb("cneg", [P, P])
        brow = sb("brow", [97, D])
        stat = sb("stat", [P, 160])
        qkv = sb("qkv", [P, 3 * D])
        hsb = sb("hsb", [P, 2, D])
        hTs = sb("hTs", [P, D])
        yb = sb("yb", [P, D])
        eb = sb("eb", [P, D])
        oTh = sb("oTh", [P, D], F32R)
        oTl = sb("oTl", [P, D], F32R)
        gz = sb("gz", [P, 1536])
        gqm = sb("gqm", [P, D])

        def sm(name):
            a, b = PC[name]
            return small[:, a:b]

        fbase = raw[:, 2:5, :].rearrange("p s c -> p (s c)")

        def fw(name):
            a, b = FC[name]
            return fbase[:, a:b]

        al = stat[:, 0:8]
        mx = stat[:, 8:12]
        nm = stat[:, 12:16]
        den = stat[:, 16:20]
        rcp = stat[:, 20:24]
        bst = stat[:, 24:36]
        mv = stat[:, 36:38]
        rstd = stat[:, 38:39]
        mhalf = stat[:, 39:51]
        comb = stat[:, 51:78]
        veps = stat[:, 78:79]
        mixa = stat[:, 80:92]
        mst = stat[:, 92:96]
        edg = stat[:, 96:128]
        awt = sb("awt", [12, P])
        soh = qkv[:, 0:1024].bitcast(BF16).rearrange("p (t n) -> p t n", t=16)
        doh = qkv[:, 1024:2048].bitcast(BF16).rearrange("p (t n) -> p t n", t=16)
        hm = eb[0:12, :]
        wkm = gz[0:12, 384:384 + D]
        zt1, ATs, dg = gz[:, 0:P], gz[:, P:2 * P], gz[:, 2 * P:3 * P]
        hsf = hsb[:].rearrange("p a n -> p (a n)")
        asb = [hsf[:, 0:FB], hsf[:, FB:2 * FB]]
        hhb = [gz[:, 0:FB], gz[:, FB:2 * FB]]
        L1Z, L1D, L1AT = gz[:, 0:512], gz[:, 512:1024], gz[:, 1024:1536]
        qT, kT, vT = hsb[:, 0, :], hsb[:, 1, :], hTs[:]
        gT, gT2 = yb[:, 0:256], yb[:, 256:512]
        zr, zT, fT = yb[:, 0:256], yb[:, 256:512], yb[:, 512:768]
        scs, se, ww = ps[:, 4, :], gz[:, 512:1024], gz[:, 1024:1536]
        hg = raw[:, 5, 0:2048]
        z_a, z_b = whi[:, 0, 0:8 * P], wlo[:, 0, 0:8 * P]
        w_a = [whi[:, 2, 0:2048], wlo[:, 2, 0:2048]]
        w_b = [whi[:, 0, 1024:3072], wlo[:, 0, 1024:3072]]
        w1b = [(0, 0, raw[:, 0, 0:2048]), (1, 0, raw[:, 0, 2048:3072]), (1, 1024, raw[:, 5, 2048:3072])]
        wcat, taken = raw[:, 1, 0:1024], raw[:, 1, 1024:1536]
        expand = whi[:, 1, 0:2048]
        wTs = wlo[:, 1, 0:1024]
        cT = eb[:, 0:256]
        at = FC["W1"][0]
        w1 = [fbase[:, at + 2048 * g:at + 2048 * (g + 1)] for g in range(2)]
        tv, tden = gqm[:, 0:64], gqm[:, 64:72]

        landed = [sem(f"landed{i}") for i in range(R)]
        hi_ready = sem("hi_ready")
        lo_ready = sem("lo_ready")
        used = sem("used")
        x_in = sem("x_in")
        edges_in = sem("edges_in")
        small_in = sem("small_in")
        wq_in = sem("wq_in")
        wk_in = sem("wk_in")
        brow_in = sem("brow_in")
        as2_in = sem("as2_in")
        ad2_in = sem("ad2_in")
        ga_in = sem("ga_in")
        fw_in = sem("fw_in")
        g2_in = sem("g2_in")
        out_in = sem("out_in")
        pool_chain = sem("pool_chain")
        consts = sem("consts")
        dve_chain = sem("dve_chain")
        onehots = sem("onehots")
        count_out = sem("count_out")
        ln_var = sem("ln_var")
        ln_rstd = sem("ln_rstd")
        xn_ready = sem("xn_ready")
        xT_out = sem("xT_out")
        xTh_ready = sem("xTh_ready")
        xTl_ready = sem("xTl_ready")
        qkv_copied = sem("qkv_copied")
        mix_pe = sem("mix_pe")
        mix_dve = sem("mix_dve")
        mix_act = sem("mix_act")
        h_copied = sem("h_copied")
        hb_out = sem("hb_out")
        hT_out = sem("hT_out")
        hT_copied = sem("hT_copied")
        al_out = sem("al_out")
        diag_ready = sem("diag_ready")
        E_out = sem("E_out")
        score_ready = sem("score_ready")
        exp_done = sem("exp_done")
        A_ready = sem("A_ready")
        AT_out = sem("AT_out")
        AT_copied = sem("AT_copied")
        agg_out = sem("agg_out")
        y_ready = sem("y_ready")
        b1_ready = sem("b1_ready")
        elu_ready = sem("elu_ready")
        o6_used = sem("o6_used")
        oTh_ready = sem("oTh_ready")
        oTl_ready = sem("oTl_ready")
        g_copied = sem("g_copied")
        F_out = sem("F_out")
        x_ready = sem("x_ready")
        router_out = sem("router_out")
        rexp_done = sem("rexp_done")
        rscore = sem("rscore")
        comb_ready = sem("comb_ready")
        silu_done = sem("silu_done")
        hh_ready = sem("hh_ready")
        T_out = sem("T_out")
        hTh_ready = sem("hTh_ready")
        hTl_ready = sem("hTl_ready")
        l1_pe = sem("l1_pe")
        l1_act = sem("l1_act")
        l1_dve = sem("l1_dve")
        l1_pool = sem("l1_pool")
        f_pe = sem("f_pe")
        f_act = sem("f_act")
        f_dve = sem("f_dve")
        f_pool = sem("f_pool")
        hid_out = sem("hid_out")
        w1b_in = sem("w1b_in")
        w1_rounded = sem("w1_rounded")
        w_b_ready = sem("w_b_ready")
        z_a_ready = sem("z_a_ready")
        z_b_ready = sem("z_b_ready")
        gelu_done = sem("gelu_done")
        Y_out = sem("Y_out")
        spread_out = sem("spread_out")
        weighted = sem("weighted")

        def onehot_of(a):
            return (iota[:].unsqueeze(1).broadcast_to([P, 16, P]), edg[:, a:a + 16].unsqueeze(2).broadcast_to([P, 16, P]))

        def wait(eng, s, v):
            if not (isinstance(v, int) and v <= 0):
                eng.wait_ge(s, v)

        class Chain:

            def __init__(self, eng, s):
                self.eng, self.s, self.base, self.k = eng, s, 0, 0

            def link(self, ins):
                self.k += 1
                ins.then_inc(self.s, 1)
                self.eng.wait_ge(self.s, self.base + self.k)

        block = ctx.enter_context(nc.Block())

        @block.sync
        def _(sp):
            def load(c, k, land_extra=0):
                n = chunk_len(k)
                sp.dma_start(raw[:, k % R, 0:n], stream_d[c, :, 0:n] if isinstance(c, int)
                             else stream_d[bass.ds(c, 1), :, 0:n].rearrange("a p n -> (a p) n")).then_inc(landed[k % R], 16)

            sp.dma_start(xres[:], x_d).then_inc(x_in, 16)
            sp.dma_start(edg[:, 0:16].bitcast(I32), src_d).then_inc(edges_in, 16)
            sp.dma_start(edg[:, 16:32].bitcast(I32), dst_d).then_inc(edges_in, 16)
            load(0, 0)
            sp.dma_start(small[:], small_d).then_inc(small_in, 16)
            load(1, 1)
            sp.dma_start(pa[:, 0:D], wqb_d).then_inc(wq_in, 16)
            sp.dma_start(wkm, wk_d).then_inc(wk_in, 16)
            load(2, 2)
            sp.dma_start(brow[0:2, :], brow_d[0:2, :]).then_inc(brow_in, 16)
            sp.dma_start(brow[32:34, :], brow_d[2:4, :]).then_inc(brow_in, 16)
            sp.dma_start(brow[64:65, :], brow_d[4:5, :]).then_inc(brow_in, 16)
            for c in range(3, R):
                load(c, c)
            for c in range(R, 9):
                sp.wait_ge(lo_ready, c - R + 1)
                load(c, c)
            with sp.Fori(9, TAIL0, R) as c:
                for k in range(R):
                    sp.wait_ge(lo_ready, c + (k - R + 1))
                    load(c + k, 9 + k)
            for c in range(TAIL0, 34):
                if c == 28:
                    sp.wait_ge(mix_dve, 9)
                    sp.dma_start(pa[:, 0:D], a2b_d[:, 0:D]).then_inc(as2_in, 16)
                    sp.dma_start(qkv[:, D:2 * D], a2b_d[:, D:2 * D]).then_inc(ad2_in, 16)
                sp.wait_ge(lo_ready, c - R + 1)
                load(c, c)
            with sp.Fori(34, L1 - 1, R) as c:
                for k in range(R):
                    sp.wait_ge(lo_ready, c + (k - R + 1))
                    load(c + k, 34 + k)
            for c in range(L1 - 1, NCH):
                if c == L1:
                    sp.wait_ge(x_ready, 1)
                    sp.dma_start(pa[:, 0:1024], ga_d).then_inc(ga_in, 16)
                sp.wait_ge(lo_ready, c - R + 1)
                load(c, c)
            sp.wait_ge(lo_ready, L1 + 6)
            sp.dma_start(fbase[:, 0:NF], fw_d).then_inc(fw_in, 16)
            sp.wait_ge(l1_pe, 5)
            sp.dma_start(qkv[:, 0:2 * D], g2_d).then_inc(g2_in, 16)
            sp.wait_ge(lo_ready, L1 + 8)
            for i, (g, at, place) in enumerate(w1b):
                a = 2048 * g + at
                sp.dma_start(place, w1b_d[:, a:a + (1024 if g else 2048)]).then_inc(w1b_in, 16)
            sp.wait_ge(x_ready, 4)
            sp.dma_start(out_d, xres[:]).then_inc(out_in, 16)
            sp.wait_ge(out_in, 16)

        @block.gpsimd
        def _(pool):
            ch = Chain(pool, pool_chain)
            ch.link(nc.gpsimd.memset(ident[:], 0.0))
            nc.gpsimd.affine_select(out=ident[:], in_=ident[:], compare_op=ALU.not_equal, fill=1.0, base=0,
                                    pattern=[[-1, P]], channel_multiplier=1).then_inc(consts, 1)
            nc.gpsimd.memset(ones[:], 1.0).then_inc(consts, 1)
            nc.gpsimd.iota(iota[:], pattern=[[1, P]], base=0, channel_multiplier=0,
                           allow_small_or_imprecise_dtypes=True).then_inc(consts, 1)
            nc.gpsimd.memset(mhalf, -0.5).then_inc(consts, 1)
            ch.link(nc.gpsimd.memset(hm, 0.0))
            nc.gpsimd.memset(brow[96:97, :], 0.0).then_inc(consts, 1)
            nc.gpsimd.affine_select(out=hm.rearrange("p (h c) -> p h c", c=64),
                                    in_=hm.rearrange("p (h c) -> p h c", c=64),
                                    compare_op=ALU.not_equal, fill=1.0, base=0,
                                    pattern=[[-1, 12], [0, 64]], channel_multiplier=1).then_inc(consts, 1)

            def rsqrt(n):
                pool.wait_ge(ln_var, n)
                nc.gpsimd.tensor_tensor(rstd, veps, mhalf[:, 0:1], ALU.pow).then_inc(ln_rstd, 1)

            pool.wait_ge(consts, 6)
            rsqrt(1)
            rsqrt(2)
            rsqrt(3)
            pool.wait_ge(l1_dve, 1)
            nc.gpsimd.tensor_tensor(stat[:, 112:118], stat[:, 100:106], mhalf[:, 0:6], ALU.pow).then_inc(l1_pool, 1)
            pool.wait_ge(l1_act, 12)
            nc.gpsimd.tensor_tensor(stat[:, 118:124], stat[:, 106:112], mhalf[:, 0:6], ALU.pow).then_inc(l1_pool, 1)
            pool.wait_ge(used, L1 + 6)
            nc.gpsimd.tensor_tensor(expand.rearrange("p (m h) -> p m h", h=32),
                                    ident[:, 0:64].unsqueeze(2).broadcast_to([P, 64, 32]),
                                    ident[:, 64:128].unsqueeze(2).broadcast_to([P, 64, 32]), ALU.add).then_inc(f_pool, 1)
            pool.wait_ge(used, L1 + 8)
            for t in (z_a, z_b):
                nc.gpsimd.tensor_tensor(t.rearrange("p (s n) -> p s n", s=8), *(ident[:].unsqueeze(1).broadcast_to([P, 8, P]),) * 2,
                                        ALU.subtract).then_inc(f_pool, 1)
            rsqrt(4)

        @block.scalar
        def _(act):
            def hi(c, k, land, need=None):
                n = chunk_len(k)
                act.wait_ge(landed[k % R], land)
                need = c - S + 1 if need is None else need
                wait(act, used, need)
                nc.scalar.activation(whi[:, k % S, 0:n], raw[:, k % R, 0:n], ACT.Copy).then_inc(hi_ready, 1)

            def his(c):
                hi(c, c, landed_at(c))

            def copy(out, in_, s):
                nc.scalar.activation(out, in_, ACT.Copy).then_inc(s, 1)

            def xT_hi(n):
                act.wait_ge(xT_out, n)
                copy(xTh[:].rearrange("p (a b) n -> p a (b n)", a=2), ps[:, 2:4, 0:HALF], xTh_ready)

            def qkv_copy(i, bank):
                act.wait_ge(used, i + 1)
                n = 512 if i < 4 else 256
                copy(qkv[:, 512 * i:512 * i + n], ps[:, bank, 0:n], qkv_copied)

            def mix_softmax(n):
                act.wait_ge(mix_dve, n)
                nc.scalar.activation(awt[:], ps[0:12, 5, 128:256], ACT.Exp, bias=mst[0:12, 1:2], scale=0.125,
                                     accum_out=mst[0:12, 2:3]).then_inc(mix_act, 1)

            def h_copy(h, d, part, s, v):
                act.wait_ge(s, v)
                wait(act, agg_out, h - 1)
                n = 512 if part == 0 else 256
                copy(hsb[:, d, 512 * part:512 * part + n], ps[:, part, 0:n], h_copied)

            def soft_exp(n):
                act.wait_ge(score_ready, n)
                nc.scalar.activation(zt1, zt1, ACT.Exp, bias=nm[:, 0:1]).then_inc(exp_done, 1)

            def AT_copy(n):
                act.wait_ge(AT_out, n)
                copy(ATs, ps[:, 4, 128:256], AT_copied)

            def hT_copy(h):
                act.wait_ge(hT_out, h + 1)
                wait(act, al_out, h)
                copy(hTs[:, 0:512], ps[:, 7, :], hT_copied)
                copy(hTs[:, 512:768], ps[:, 4, 256:512], hT_copied)

            def elu_exp(n):
                act.wait_ge(agg_out, n)
                y = ps[:, 2:4, 0:HALF]
                wait(act, oTl_ready, n - 1)
                nc.scalar.activation(eb[:].rearrange("p (a n) -> p a n", a=2), y, ACT.Exp)
                nc.scalar.activation(yb[:].rearrange("p (a n) -> p a n", a=2), y, ACT.Relu).then_inc(y_ready, 1)

            def o_hi(n, free, s=used):
                act.wait_ge(elu_ready, n)
                wait(act, s, free)
                nc.scalar.activation(oTh[:], yb[:], ACT.Copy, bias=-1.0).then_inc(oTh_ready, 1)

            xT_hi(1)
            his(0)
            his(1)
            his(2)
            act.wait_ge(count_out, 1)
            qkv_copy(0, 0)
            his(3)
            qkv_copy(1, 1)
            his(4)
            qkv_copy(2, 2)
            mix_softmax(2)
            his(5)
            qkv_copy(3, 3)
            act.wait_ge(mix_pe, 2)
            copy(mixa, ps[:, 5, 256:268], mix_act)
            his(6)
            qkv_copy(4, 7)
            his(7)
            h_copy(0, 0, 0, used, 6)
            his(8)
            h_copy(0, 0, 1, used, 7)
            hT_copy(0)
            mix_softmax(6)
            his(9)
            h_copy(1, 1, 0, used, 8)
            act.wait_ge(mix_pe, 6)
            copy(mixa, ps[:, 5, 256:268], mix_act)
            his(10)
            soft_exp(1)
            h_copy(1, 1, 1, used, 9)
            AT_copy(1)
            hT_copy(1)
            elu_exp(1)
            o_hi(1, 0)

            def step(h, c, d, k, land, last=False):
                hi(c + 2, k + 2, land(k + 2))
                h_copy(h, d, 0, used, c + 1)
                hi(c + 3, k + 3, land(k + 3))
                soft_exp(h)
                h_copy(h, d, 1, hb_out, h - 1)
                AT_copy(h)
                if not last:
                    hi(c + 4, k + 4, land(k + 4))
                hT_copy(h)
                elu_exp(h)
                o_hi(h, c + 3)
                if last:
                    hi(c + 4, k + 4, land(k + 4))

            with act.Fori(2, H0 - 2, 2) as h:
                for d in range(2):
                    step(h + d, 3 * h + (3 + 3 * d), d, 9 + 3 * d, lambda k: 8 * h + (landed_at(k) - 16))
            for h in (H0 - 2, H0 - 1):
                step(h, 3 * h + 3, h % 2, 3 * h + 3, landed_at, last=h == H0 - 1)

            soft_exp(8)
            AT_copy(8)
            act.wait_ge(mix_pe, 9)
            copy(xTh[:].rearrange("p b n -> p (b n)")[:, 0:512], ps[:, 7, :], mix_act)
            copy(xTh[:].rearrange("p b n -> p (b n)")[:, 512:768], ps[:, 4, 256:512], mix_act)
            his(29)
            elu_exp(8)
            his(30)
            o_hi(8, 1, o6_used)
            his(31)
            his(32)
            act.wait_ge(used, 32)
            copy(hsb[:, 0, :].rearrange("p (a n) -> p a n", a=2), ps[:, 5:7, 0:HALF], g_copied)
            soft_exp(9)
            AT_copy(9)
            his(33)
            xT_hi(2)
            his(34)
            act.wait_ge(rscore, 1)
            nc.scalar.activation(stat[:, 128:136], stat[:, 128:136], ACT.Exp, bias=nm[:, 0:1],
                                 accum_out=den[:, 0:1]).then_inc(rexp_done, 1)

            def silu(j, d, done):
                act.wait_ge(used, done)
                wait(act, hh_ready, j - 1)
                nc.scalar.activation(asb[d], ps[:, d, :], ACT.Silu).then_inc(silu_done, 1)

            def hT_hi(j, free):
                act.wait_ge(T_out, j + 1)
                act.wait_ge(used, free)
                copy(oTh[:, 0:FB], ps[:, 4, :], hTh_ready)

            silu(0, 0, 33)
            his(35)

            def fstep(j, c, d, k, land):
                hi(c + 2, k + 2, land(k + 2))
                silu(j, d, c + 1)
                hT_hi(j - 1, c)
                hi(c + 3, k + 3, land(k + 3))
                hi(c + 4, k + 4, land(k + 4))

            with act.Fori(1, FS, 2) as j:
                for d in range(2):
                    fstep(j + d, 3 * j + (31 + 3 * d), 1 - d, 34 + 3 * d,
                          lambda k: 8 * j + (landed_at(k) - 8))
            hT_hi(FS - 1, L1 - 1)
            his(L1 + 1)
            his(L1 + 2)
            xT_hi(3)

            def l1_copy(out, in_, n, s=l1_pe):
                act.wait_ge(s, n)
                copy(out, in_, l1_act)

            def relu2(out, col, name, n):
                act.wait_ge(l1_pe, n)
                for b in range(2):
                    nc.scalar.activation(out[:, b * P:(b + 1) * P], ps[:, 7, col + b * P:col + (b + 1) * P], ACT.Relu,
                                         bias=sm(name)[:, b:b + 1]).then_inc(l1_act, 1)

            halves = lambda t: t.rearrange("p (a n) -> p a n", a=2)
            l1_copy(gqm[:, 0:256], ps[:, 5, 0:256], L1 + 1, used)
            his(L1 + 3)
            l1_copy(qkv[:, 0:512], ps[:, 0, :], L1 + 2, used)
            his(L1 + 4)
            act.wait_ge(score_ready, 10)
            for h in range(4):
                nc.scalar.activation(L1Z[:, h * P:(h + 1) * P], L1Z[:, h * P:(h + 1) * P], ACT.Exp,
                                     bias=nm[:, h:h + 1]).then_inc(exp_done, 1)
            l1_copy(qkv[:, 512:1024], ps[:, 1, :], L1 + 3, used)
            his(L1 + 5)
            l1_copy(qkv[:, 1024:1536], ps[:, 2, :], L1 + 4, used)
            l1_copy(halves(qT), ps[:, 0:2, 0:HALF], 2)
            l1_copy(L1AT, ps[:, 6, :], 3)
            l1_copy(qkv[:, 1536:2048], ps[:, 4, :], L1 + 5, used)
            relu2(gT, 0, "gb1", 4)
            his(L1 + 6)
            l1_copy(gqm[:, 256:512], ps[:, 5, 256:512], 6)
            for b in range(KD):
                if b == 3:
                    l1_copy(qkv[:, 2048:2304], ps[:, 0, 0:256], L1 + 6, used)
                src = ps[:, 2 + b // 3, (b % 3) * P:(b % 3 + 1) * P]
                nc.scalar.activation(oTh[:, b * P:(b + 1) * P], src, ACT.Square, accum_out=stat[:, 106 + b:107 + b])
                ins = nc.scalar.activation(kT[:, b * P:(b + 1) * P], src, ACT.Copy, accum_out=stat[:, 130 + b:131 + b])
            ins.then_inc(l1_act, 1)
            l1_copy(halves(vT), ps[:, 0:2, 0:HALF], 8)
            act.wait_ge(score_ready, 11)
            nc.scalar.activation(L1Z[:, 0:P], L1Z[:, 0:P], ACT.Exp, bias=nm[:, 0:1]).then_inc(exp_done, 1)
            his(L1 + 7)
            l1_copy(L1AT[:, 0:P], ps[:, 6, 0:P], 9)
            relu2(gT, 0, "gb2", 10)
            relu2(gT2, 256, "bm1", 11)
            act.wait_ge(l1_dve, 2)
            copy(xTh[:].rearrange("p b n -> p (b n)"), qT, l1_act)
            act.wait_ge(fw_in, 16)
            act.wait_ge(used, L1 + 7)
            for g in range(2):
                copy(w_a[g], w1[g], w1_rounded)
            act.wait_ge(w1b_in, 48)
            act.wait_ge(used, L1 + 8)
            for g, at, place in w1b:
                copy(w_b[g][:, at:at + (1024 if g else 2048)], place, w1_rounded)

            own = lambda t, r, s4: t[r, :].rearrange("p (g s n) -> p g s n", g=2, s=4)[:, :, s4, :]
            act.wait_ge(xT_out, 4)
            copy(hTs[:].rearrange("p (a n) -> p a n", a=2), ps[:, 2:4, 0:HALF], f_act)
            act.wait_ge(f_pe, 1)
            copy(zT, ps[:, 6, 0:256], f_act)
            act.wait_ge(f_pool, 3)
            cst = fw("cst")
            for s4 in range(4):
                r = slice(32 * s4, 32 * s4 + 32)
                nc.scalar.activation(own(z_b, r, s4), ps[r, 6, 0:256].rearrange("p (g n) -> p g n", g=2), ACT.Identity,
                                     bias=cst[r, 3:4], scale=cst[r, 2:3]).then_inc(z_b_ready, 1)
            act.wait_ge(f_dve, 1)
            nc.scalar.activation(se, se, ACT.Exp).then_inc(f_act, 1)

            def gelu(u, d):
                act.wait_ge(hid_out, u + 1)
                wait(act, Y_out, u - 3)
                nc.scalar.activation(hg[:, 512 * d:512 * d + 512], ps[:, d, :], ACT.Gelu_apprx_tanh).then_inc(gelu_done, 1)

            for d in range(4):
                gelu(d, d)
            with act.Fori(4, UNITS, 4) as u:
                for d in range(4):
                    gelu(u + d, d)
            act.wait_ge(Y_out, UNITS)
            copy(cT.rearrange("p (g n) -> p g n", g=2), ps[:, 6:8, 0:P], f_act)
            for b in range(2):
                act.wait_ge(f_pe, 5)
                nc.scalar.activation(fT[:, b * P:(b + 1) * P], ps[:, 1, b * P:(b + 1) * P], ACT.Gelu_apprx_tanh,
                                     bias=sm("fg1b")[:, b:b + 1]).then_inc(f_act, 1)

        @block.vector
        def _(dve):
            ch = Chain(dve, dve_chain)
            link = ch.link
            V = nc.vector

            def lo(c, k):
                n = chunk_len(k)
                dve.wait_ge(hi_ready, c + 1)
                V.tensor_tensor(wlo[:, k % S, 0:n], raw[:, k % R, 0:n], whi[:, k % S, 0:n].bitcast(F32),
                                ALU.subtract).then_inc(lo_ready, 1)

            def los(c):
                lo(c, c)

            def layernorm(n):
                V.bn_stats(bst[:, 0:6], xres[:, 0:HALF])
                link(V.bn_stats(bst[:, 6:12], xres[:, HALF:D]))
                link(V.bn_aggr(mv, bst))
                V.tensor_scalar(veps, mv[:, 1:2], EPS, None, ALU.add).then_inc(ln_var, 1)
                dve.wait_ge(ln_rstd, n)
                V.tensor_scalar(xn[:], xres[:], mv[:, 0:1], rstd, ALU.subtract, ALU.mult).then_inc(xn_ready, 1)

            def xT_lo(n):
                dve.wait_ge(xTh_ready, n)
                V.tensor_tensor(xTl[:].rearrange("p (a b) n -> p a (b n)", a=2), ps[:, 2:4, 0:HALF],
                                xTh[:].bitcast(F32).rearrange("p (a b) n -> p a (b n)", a=2),
                                ALU.subtract).then_inc(xTl_ready, 1)

            dve.wait_ge(x_in, 16)
            layernorm(1)
            dve.wait_ge(edges_in, 32)
            dve.wait_ge(consts, 6)
            link(V.tensor_copy(edg, edg.bitcast(I32)))
            V.tensor_tensor(soh, *onehot_of(0), ALU.is_equal).then_inc(onehots, 1)
            xT_lo(1)
            V.tensor_tensor(doh, *onehot_of(16), ALU.is_equal).then_inc(onehots, 1)
            los(0)
            los(1)
            dve.wait_ge(count_out, 1)
            link(V.tensor_tensor(cnt[:], ps[:, 4, 0:P], ident[:], ALU.add))
            V.tensor_scalar(cneg[:], cnt[:], 0.5, BIG, ALU.is_lt, ALU.mult)
            dve.wait_ge(small_in, 16)
            V.tensor_tensor(pick[:], ident[0:112, 0:48], ident[0:112, 64:112], ALU.add)
            link(V.tensor_copy(b1s[:], sm("b1")[0:112, :]))
            V.tensor_tensor(b1s[64:112, :], sm("b1")[64:112, :], b1s[64:112, :].bitcast(F32), ALU.subtract).then_inc(b1_ready, 1)
            dve.wait_ge(wk_in, 16)
            link(V.tensor_tensor(wkm, wkm, hm, ALU.mult))
            los(2)

            def head_scores():
                V.tensor_reduce(mixa, xn[:].rearrange("p (h c) -> p h c", c=64), AX, ALU.add).then_inc(mix_dve, 1)

            halves = lambda t: t.rearrange("p (a n) -> p a n", a=2)

            def mix_max(n_pe):
                dve.wait_ge(mix_pe, n_pe)
                link(V.tensor_reduce(mst[0:12, 0:1], ps[0:12, 5, 128:256], AX, ALU.max))
                V.tensor_scalar(mst[0:12, 1:2], mst[0:12, 0:1], -0.125, None, ALU.mult).then_inc(mix_dve, 1)

            def mix_norm(n_act):
                dve.wait_ge(mix_act, n_act)
                link(V.reciprocal(mst[0:12, 3:4], mst[0:12, 2:3]))
                V.tensor_scalar(awt[:], awt[:], mst[0:12, 3:4], None, ALU.mult).then_inc(mix_dve, 1)

            dve.wait_ge(wq_in, 16)
            dve.wait_ge(qkv_copied, 2)
            link(V.tensor_tensor(xn[:], qkv[:, 0:D], pa[:, 0:D], ALU.mult))
            head_scores()
            los(3)
            mix_max(1)
            mix_norm(1)
            los(4)
            los(5)
            los(6)
            dve.wait_ge(mix_pe, 3)
            V.tensor_tensor(halves(gqm[0:12, :]), ps[0:12, 5:7, 0:HALF], halves(wkm), ALU.mult).then_inc(mix_dve, 1)
            los(7)
            dve.wait_ge(qkv_copied, 3)
            dve.wait_ge(mix_pe, 4)
            link(V.tensor_tensor(halves(xn[:]), ps[:, 5:7, 0:HALF], halves(qkv[:, D:2 * D]), ALU.mult))
            head_scores()
            los(8)

            def alpha_diag(h):
                dve.wait_ge(al_out, h + 1)
                wait(dve, E_out, h)
                link(V.tensor_copy(al[:, 0:2], ps[:, 4, 0:2]))
                V.tensor_scalar(dg, ident[:], al[:, 0:1], None, ALU.mult).then_inc(diag_ready, 1)

            def scores(n, e_ap, z, ad):
                dve.wait_ge(E_out, n)
                link(V.scalar_tensor_tensor(z, e_ap, ad, cneg[:], ALU.add, ALU.add))
                link(V.scalar_tensor_tensor(z, z, 0.2, z, ALU.mult, ALU.max))
                V.tensor_reduce(nm[:, 0:1], z, AX, ALU.max, negate=True).then_inc(score_ready, 1)

            def weights(n, z):
                dve.wait_ge(exp_done, n)
                link(V.scalar_tensor_tensor(z, z, 1.0, cnt[:], ALU.mult, ALU.mult, accum_out=den[:, 0:1]))
                link(V.reciprocal(rcp[:, 0:1], den[:, 0:1]))
                V.tensor_scalar(z, z, rcp[:, 0:1], None, ALU.mult).then_inc(A_ready, 1)

            def elu(n):
                dve.wait_ge(y_ready, n)
                V.scalar_tensor_tensor(yb[:], eb[:], 1.0, yb[:], ALU.min, ALU.add).then_inc(elu_ready, 1)

            def o_lo(n):
                dve.wait_ge(oTh_ready, n)
                V.scalar_tensor_tensor(oTl[:], yb[:], -1.0, oTh[:].bitcast(F32), ALU.add, ALU.subtract).then_inc(oTl_ready, 1)

            mix_max(5)
            mix_norm(3)
            alpha_diag(0)
            los(9)
            scores(1, ps[:, 4, P:2 * P], zt1, al[:, 1:2])
            weights(1, zt1)
            dve.wait_ge(mix_pe, 7)
            V.tensor_tensor(halves(gqm[0:12, :]), ps[0:12, 5:7, 0:HALF], halves(hm), ALU.mult).then_inc(mix_dve, 1)
            los(10)
            dve.wait_ge(mix_pe, 8)
            dve.wait_ge(qkv_copied, 5)
            V.tensor_tensor(halves(qkv[:, 2 * D:3 * D]), ps[:, 5:7, 0:HALF], halves(qkv[:, 2 * D:3 * D]),
                            ALU.mult).then_inc(mix_dve, 1)
            elu(1)
            o_lo(1)
            alpha_diag(1)

            def step(h, c, d, k, last=False):
                lo(c + 2, k + 2)
                scores(h, ps[:, 4, P:2 * P], zt1, al[:, 1:2])
                weights(h, zt1)
                lo(c + 3, k + 3)
                if not last:
                    lo(c + 4, k + 4)
                elu(h)
                alpha_diag(h)
                o_lo(h)

            per = 2 * (2 + 2 + 1)
            k0 = ch.k
            with dve.Fori(2, H0 - 2, 2) as h:
                ch.base, ch.k = (per // 2) * h + (k0 - per), 0
                for d in range(2):
                    step(h + d, 3 * h + (3 + 3 * d), d, 9 + 3 * d)
                assert ch.k == per
            ch.base, ch.k = 0, k0 + per * (H0 - 4) // 2
            for h in (H0 - 2, H0 - 1):
                step(h, 3 * h + 3, h % 2, 3 * h + 3, last=h == H0 - 1)

            scores(8, ps[:, 4, P:2 * P], zt1, al[:, 1:2])
            weights(8, zt1)
            los(28)
            dve.wait_ge(mix_act, 6)
            V.tensor_tensor(xTl[:].rearrange("p b n -> p (b n)")[:, 0:512], ps[:, 7, :],
                            xTh[:].rearrange("p b n -> p (b n)")[:, 0:512].bitcast(F32), ALU.subtract)
            V.tensor_tensor(xTl[:].rearrange("p b n -> p (b n)")[:, 512:768], ps[:, 4, 256:512],
                            xTh[:].rearrange("p b n -> p (b n)")[:, 512:768].bitcast(F32), ALU.subtract).then_inc(mix_dve, 1)
            los(29)
            elu(8)
            los(30)
            o_lo(8)
            los(31)
            V.tensor_tensor(xres[:], xres[:], qkv[:, 0:D], ALU.add)
            dve.wait_ge(as2_in, 16)
            dve.wait_ge(ad2_in, 16)
            dve.wait_ge(g_copied, 1)
            for i, a in enumerate((pa[:, 0:D], qkv[:, D:2 * D])):
                link(V.scalar_tensor_tensor(eb[:], hsb[:, 0, :], 1.0, a, ALU.mult, ALU.mult, accum_out=al[:, i:i + 1]))
            V.tensor_scalar(dg, ident[:], al[:, 0:1], None, ALU.mult).then_inc(diag_ready, 1)
            scores(9, ps[:, 4, P:2 * P], zt1, al[:, 1:2])
            weights(9, zt1)
            los(32)

            def residual(n, b0, s, v):
                dve.wait_ge(s, v)
                V.tensor_tensor(xres[:].rearrange("p (a n) -> p a n", a=2), ps[:, b0:b0 + 2, 0:HALF],
                                xres[:].rearrange("p (a n) -> p a n", a=2), ALU.add).then_inc(x_ready, 1)
                dve.wait_ge(x_ready, n)

            residual(1, 0, F_out, 1)
            layernorm(2)
            xT_lo(2)
            los(33)
            los(34)

            sc = stat[:, 128:136]
            sel = stat[:, 136:144]
            v8 = stat[:, 144:152]
            dve.wait_ge(router_out, 1)
            link(V.tensor_copy(sc, ps[:, 7, 0:8]))
            link(V.tensor_reduce(mx[:, 0:1], sc, AX, ALU.max))
            V.tensor_scalar(nm[:, 0:1], mx[:, 0:1], -1.0, None, ALU.mult).then_inc(rscore, 1)
            dve.wait_ge(rexp_done, 1)
            link(V.reciprocal(rcp[:, 0:1], den[:, 0:1]))
            link(V.tensor_scalar(sc, sc, rcp[:, 0:1], None, ALU.mult))
            link(V.tensor_tensor(sel, sc, sm("ebias"), ALU.add))
            link(V.max(v8, sel))
            link(V.max_index(stat[:, 152:160].bitcast(U32), v8, sel))
            link(V.tensor_copy(v8[:, 0:2], stat[:, 152:154].bitcast(U32)))
            link(V.tensor_scalar(sel, iota[:, 0:8], v8[:, 0:1], None, ALU.is_equal))
            link(V.scalar_tensor_tensor(sel, iota[:, 0:8], v8[:, 1:2], sel, ALU.is_equal, ALU.add))
            link(V.tensor_tensor(sel, sel, sc, ALU.mult))
            link(V.tensor_reduce(den[:, 0:1], sel, AX, ALU.add))
            link(V.tensor_scalar(den[:, 0:1], den[:, 0:1], 1e-9, None, ALU.add))
            link(V.reciprocal(rcp[:, 0:1], den[:, 0:1]))
            link(V.memset(comb[:, 24:27], 1.0))
            link(V.tensor_scalar(comb[:, 0:24].rearrange("p (e t) -> p e t", t=3),
                                 sel.unsqueeze(2).broadcast_to([P, 8, 3]), rcp[:, 0:1], None, ALU.mult))

            def hT_lo(j):
                dve.wait_ge(hTh_ready, j + 1)
                V.tensor_tensor(oTl[:, 0:FB], ps[:, 4, :], oTh[:, 0:FB].bitcast(F32), ALU.subtract).then_inc(hTl_ready, 1)

            def hid(j, d, done):
                dve.wait_ge(silu_done, j + 1)
                dve.wait_ge(used, done)
                wait(dve, T_out, j - 1)
                cj = comb[:, j:j + 1] if isinstance(j, int) else stat[:, bass.ds(j + 51, 1)]
                V.scalar_tensor_tensor(hhb[d], asb[d], cj, ps[:, 2 + d, :], ALU.mult, ALU.mult).then_inc(hh_ready, 1)

            hid(0, 0, 34)
            los(35)

            def fstep(j, c, d, k, last=False):
                lo(c + 2, k + 2)
                hT_lo(j - 1)
                lo(c + 3, k + 3)
                hid(j, d, c + 2)
                if not last:
                    lo(c + 4, k + 4)

            with dve.Fori(1, FS - 2, 2) as j:
                for d in range(2):
                    fstep(j + d, 3 * j + (31 + 3 * d), 1 - d, 34 + 3 * d)
            for j in (FS - 2, FS - 1):
                fstep(j, 3 * j + 31, j % 2, 3 * j + 31, last=j == FS - 1)
            hT_lo(FS - 1)
            los(L1)
            residual(2, 5, used, L1)
            layernorm(3)
            xT_lo(3)
            los(L1 + 1)

            los(L1 + 2)
            dve.wait_ge(ga_in, 16)
            dve.wait_ge(l1_act, 1)
            al4 = [al[:, 0:4], al[:, 4:8]]
            for i in range(2):
                link(V.tensor_tensor(eb[:, 0:256], gqm[:, 0:256], pa[:, 256 * i:256 * i + 256], ALU.mult))
                link(V.tensor_reduce(al4[i], eb[:, 0:256].rearrange("p (h c) -> p h c", c=64), AX, ALU.add))
            for h in range(4):
                ins = V.tensor_scalar(L1D[:, h * P:(h + 1) * P], ident[:], al[:, h:h + 1], None, ALU.mult)
            ins.then_inc(diag_ready, 1)
            los(L1 + 3)
            dve.wait_ge(l1_pe, 1)
            hd = lambda t, h: t[:, h * P:(h + 1) * P]
            for h in range(4):
                ins = V.scalar_tensor_tensor(hd(L1Z, h), ps[:, 6, h * P:(h + 1) * P], al[:, 4 + h:5 + h], cneg[:],
                                             ALU.add, ALU.add)
            link(ins)
            link(V.scalar_tensor_tensor(L1Z, L1Z, 0.2, L1Z, ALU.mult, ALU.max))
            V.tensor_reduce(nm, L1Z.rearrange("p (h n) -> p h n", n=P), AX, ALU.max, negate=True).then_inc(score_ready, 1)
            los(L1 + 4)
            dve.wait_ge(exp_done, 13)
            for h in range(4):
                ins = V.tensor_tensor(hd(L1Z, h), hd(L1Z, h), cnt[:], ALU.mult)
            link(ins)
            link(V.tensor_reduce(den, L1Z.rearrange("p (h n) -> p h n", n=P), AX, ALU.add))
            link(V.tensor_scalar(den, den, 1e-16, None, ALU.add))
            link(V.reciprocal(rcp, den))
            for h in range(4):
                ins = V.tensor_scalar(hd(L1Z, h), hd(L1Z, h), rcp[:, h:h + 1], None, ALU.mult)
            ins.then_inc(A_ready, 1)
            los(L1 + 5)
            sums = stat[:, 124:136]
            rn = stat[:, 112:124]
            dve.wait_ge(l1_act, 5)
            link(V.tensor_tensor(eb[:], qT, qT, ALU.mult))
            V.tensor_reduce(stat[:, 100:106], eb[:].rearrange("p (b n) -> p b n", n=P), AX, ALU.add).then_inc(l1_dve, 1)
            dve.wait_ge(l1_dve, 1)
            V.tensor_reduce(sums[:, 0:6], qT.rearrange("p (b n) -> p b n", n=P), AX, ALU.add)
            dve.wait_ge(l1_act, 10)
            for i in range(2):
                link(V.scalar_tensor_tensor(eb[:, 0:256], gqm[:, 256:512], 1.0, pa[:, 512 + 256 * i:768 + 256 * i],
                                            ALU.mult, ALU.mult, accum_out=al[:, i:i + 1]))
            V.tensor_scalar(hd(L1D, 0), ident[:], al[:, 0:1], None, ALU.mult).then_inc(diag_ready, 1)
            los(L1 + 6)
            z = hd(L1Z, 0)
            dve.wait_ge(l1_pe, 7)
            link(V.scalar_tensor_tensor(z, ps[:, 6, 0:P], al[:, 1:2], cneg[:], ALU.add, ALU.add))
            link(V.scalar_tensor_tensor(z, z, 0.2, z, ALU.mult, ALU.max))
            V.tensor_reduce(nm[:, 0:1], z, AX, ALU.max, negate=True).then_inc(score_ready, 1)
            dve.wait_ge(exp_done, 14)
            link(V.scalar_tensor_tensor(z, z, 1.0, cnt[:], ALU.mult, ALU.mult, accum_out=den[:, 0:1]))
            link(V.tensor_scalar(den[:, 0:1], den[:, 0:1], 1e-16, None, ALU.add))
            link(V.reciprocal(rcp[:, 0:1], den[:, 0:1]))
            V.tensor_scalar(z, z, rcp[:, 0:1], None, ALU.mult).then_inc(A_ready, 1)
            dve.wait_ge(l1_act, 12)
            link(V.tensor_tensor(qT, qT, kT, ALU.mult))
            dve.wait_ge(l1_act, 13)
            link(V.tensor_tensor(vT, vT, kT, ALU.mult))
            link(V.tensor_tensor(qT, qT, vT, ALU.mult))
            dve.wait_ge(l1_pool, 2)
            fct = stat[:, 136:142]
            link(V.tensor_tensor(sums, sums, rn, ALU.mult))
            link(V.tensor_tensor(fct, sums[:, 0:6], sums[:, 6:12], ALU.mult))
            link(V.tensor_scalar(fct, fct, float(N), None, ALU.add))
            link(V.reciprocal(fct, fct))
            link(V.tensor_tensor(rn[:, 0:6], rn[:, 0:6], rn[:, 6:12], ALU.mult))
            link(V.tensor_tensor(rn[:, 0:6], rn[:, 0:6], rn[:, 6:12], ALU.mult))
            link(V.tensor_tensor(fct, fct, rn[:, 0:6], ALU.mult))
            b6 = lambda t: t.rearrange("p (b n) -> p b n", n=P)
            V.tensor_tensor(b6(qT), b6(qT), fct.unsqueeze(2).broadcast_to([P, 6, P]), ALU.mult).then_inc(l1_dve, 1)
            dve.wait_ge(l1_act, 19)
            V.tensor_tensor(xTl[:].rearrange("p b n -> p (b n)"), qT, xTh[:].rearrange("p b n -> p (b n)").bitcast(F32),
                            ALU.subtract).then_inc(l1_dve, 1)
            los(L1 + 7)
            residual(3, 2, F_out, 2)

            layernorm(4)
            cst = fw("cst")
            for i, (g, at, place) in enumerate(w1b):
                dve.wait_ge(w1_rounded, 3 + i)
                t = w_b[g][:, at:at + (1024 if g else 2048)]
                V.scalar_tensor_tensor(t, place, cst[:, 0:1], t.bitcast(F32), ALU.mult, ALU.subtract).then_inc(w_b_ready, 1)
            dve.wait_ge(f_act, 2)
            link(V.tensor_copy(zr.bitcast(F32R), zT))
            dve.wait_ge(f_pool, 3)
            for s4 in range(4):
                r = slice(32 * s4, 32 * s4 + 32)
                both = lambda t: t[r, :].rearrange("p (g n) -> p g n", g=2)
                V.scalar_tensor_tensor(z_a[r, :].rearrange("p (g s n) -> p g s n", g=2, s=4)[:, :, s4, :], both(zr),
                                       cst[r, 1:2], both(zT), ALU.mult, ALU.add).then_inc(z_a_ready, 1)
            dve.wait_ge(f_pe, 2)
            for s in range(8):
                ins = V.max(tv[:, 8 * s:8 * s + 8], scs[:, 64 * s:64 * s + 64])
            link(ins)
            v3 = tv.rearrange("p (s k) -> p s k", k=8)
            by_s = lambda t: t.rearrange("p (s m) -> p s m", s=8)
            V.tensor_tensor(by_s(se), by_s(scs), v3[:, :, 0:1].broadcast_to([P, 8, 64]), ALU.subtract).then_inc(f_dve, 1)
            dve.wait_ge(f_dve, 1)
            link(V.memset(v3[:, :, 4:8], 3e38))
            for s in range(8):
                ins = V.match_replace(out=taken[:, 64 * s:64 * s + 64], in_to_replace=tv[:, 8 * s:8 * s + 8],
                                      in_values=scs[:, 64 * s:64 * s + 64], imm_value=-3e38)
            link(ins)
            link(V.tensor_tensor(taken, taken, scs, ALU.not_equal))
            dve.wait_ge(f_act, 3)
            link(V.tensor_tensor(se, se, taken, ALU.mult))
            link(V.tensor_reduce(tden, by_s(se), AX, ALU.add))
            link(V.reciprocal(tden, tden))
            link(V.tensor_tensor(by_s(ww), by_s(se), tden.unsqueeze(2).broadcast_to([P, 8, 64]), ALU.mult))
            for g in range(2):
                w4 = wcat[:, 512 * g:512 * g + 512].rearrange("p (s a m) -> p s a m", s=4, a=2)
                w3 = ww[:, 256 * g:256 * g + 256].rearrange("p (s m) -> p s m", s=4)
                link(V.tensor_copy(w4[:, :, 0, :].bitcast(F32R), w3))
                V.tensor_tensor(w4[:, :, 1, :], w3, w4[:, :, 0, :], ALU.subtract).then_inc(f_dve, 1)
            for g in range(2):
                dve.wait_ge(f_pe, 3 + g)
                V.tensor_copy(wTs[:, 512 * g:512 * g + 512], ps[:, 4 + g, :]).then_inc(f_dve, 1)

            def weigh_hidden(u, d):
                dve.wait_ge(gelu_done, u + 1)
                dve.wait_ge(spread_out, u + 1)
                b = hg[:, 512 * d:512 * d + 512]
                V.tensor_tensor(b, b, ps[:, 4 + d % 2, :], ALU.mult).then_inc(weighted, 1)

            with dve.Fori(0, UNITS, 4) as u:
                for d in range(4):
                    weigh_hidden(u + d, d)
            residual(4, 2, F_out, 3)

        @block.tensor
        def _(pe):
            mm = nc.tensor.matmul

            def ready(c):
                pe.wait_ge(lo_ready, c + 1)

            def part3(out, sh, sl, wh, wl, first, last, shared=False):
                mm(out, sh, wh, start=first, stop=False, skip_group_check=shared)
                mm(out, sh, wl, start=False, stop=False, skip_group_check=shared)
                return mm(out, sl, wh, start=False, stop=last, skip_group_check=shared)

            def up(out, k, n, xh, xl):
                for t in range(KD):
                    ins = part3(out, xh[:, t, :], xl[:, t, :], whi[:, k % S, t * n:(t + 1) * n],
                                wlo[:, k % S, t * n:(t + 1) * n], t == 0, t == KD - 1)
                return ins

            def down(banks, k, off, ts, sh, sl, first=False, last=False):
                for i, t in enumerate(ts):
                    for half in range(2):
                        a = off + i * D + half * HALF
                        ins = part3(ps[:, banks[half], 0:HALF], sh[:, t * P:(t + 1) * P], sl[:, t * P:(t + 1) * P],
                                    whi[:, k % S, a:a + HALF], wlo[:, k % S, a:a + HALF],
                                    first and i == 0, last and i == len(ts) - 1)
                return ins

            def transpose6(src, n):
                pe.wait_ge(xn_ready, n)
                for b in range(KD):
                    ins = nc.tensor.transpose(ps[:, 2 + b // 3, (b % 3) * P:(b % 3 + 1) * P], src[:, b * P:(b + 1) * P], ident[:])
                ins.then_inc(xT_out, 1)

            def x_split(n):
                pe.wait_ge(xTh_ready, n)
                pe.wait_ge(xTl_ready, n)

            def bias(banks, row, n, first=False, last=False):
                pe.wait_ge(brow_in, 48)
                for half in range(2):
                    ins = mm(ps[:, banks[half], 0:HALF], ones[row:row + n, :], brow[row:row + n, half * HALF:(half + 1) * HALF],
                             start=first, stop=last)
                return ins

            pe.wait_ge(consts, 6)
            transpose6(xn, 1)

            def up_chunk(c, k, n, bank):
                ready(c)
                up(ps[:, bank, 0:n], k, n, xTh, xTl).then_inc(used, 1)

            def to_rows(v):
                pe.wait_ge(mix_dve, v)
                nc.tensor.transpose(ps[0:12, 5, 128:256], mixa, ident[:]).then_inc(mix_pe, 1)

            def to_columns(v):
                pe.wait_ge(mix_dve, v)
                nc.tensor.transpose(ps[:, 5, 256:268], awt[:], ident[0:12, 0:12]).then_inc(mix_pe, 1)

            def weigh(v, t):
                pe.wait_ge(mix_act, v)
                for half in range(2):
                    ins = mm(ps[0:12, 5 + half, 0:HALF], mixa, t[:, half * HALF:(half + 1) * HALF], start=True, stop=True)
                ins.then_inc(mix_pe, 1)

            def spread(v):
                pe.wait_ge(mix_dve, v)
                for half in range(2):
                    ins = mm(ps[:, 5 + half, 0:HALF], ones[0:12, :], gqm[0:12, half * HALF:(half + 1) * HALF],
                             start=True, stop=True)
                ins.then_inc(mix_pe, 1)

            def src_spread(h, n):
                pe.wait_ge(diag_ready, n)
                mm(ps[:, 4, P:2 * P], ones[:], dg, start=True, stop=True).then_inc(E_out, 1)

            def A_transpose(n):
                pe.wait_ge(A_ready, n)
                nc.tensor.transpose(ps[:, 4, P:2 * P], zt1, ident[:]).then_inc(AT_out, 1)

            def h_transpose(h, d):
                pe.wait_ge(h_copied, 2 * h + 2)
                wait(pe, hT_copied, 2 * h)
                for b in range(4):
                    nc.tensor.transpose(ps[:, 7, b * P:(b + 1) * P], hsb[:, d, b * P:(b + 1) * P], ident[:])
                wait(pe, AT_copied, h)
                for b in range(4, 6):
                    ins = nc.tensor.transpose(ps[:, 4, (b - 2) * P:(b - 1) * P], hsb[:, d, b * P:(b + 1) * P], ident[:])
                ins.then_inc(hT_out, 1)

            def aggregate(h, d):
                pe.wait_ge(AT_copied, h + 1)
                wait(pe, y_ready, h)
                for b in range(KD):
                    out = ps[:, 2 + b // 3, (b % 3) * P:(b % 3 + 1) * P]
                    mm(out, hsb[:, d, b * P:(b + 1) * P], ATs, start=True, stop=False)
                    r = pick[:, 6 * h + b:6 * h + b + 1] if isinstance(h, int) else pick[:, bass.ds(h * 6 + b, 1)]
                    ins = mm(out, b1s[:], r.broadcast_to([112, P]), start=False, stop=True)
                ins.then_inc(agg_out, 1)

            def alphas(h):
                pe.wait_ge(hT_copied, 2 * h + 2)
                for b in range(KD):
                    a = (small[:, 12 * h + 2 * b:12 * h + 2 * b + 2] if isinstance(h, int)
                         else small[:, bass.ds(h * 12 + 2 * b, 2)])
                    ins = mm(ps[:, 4, 0:2], hTs[:, b * P:(b + 1) * P], a, start=b == 0, stop=b == KD - 1)
                ins.then_inc(al_out, 1)

            def zero_start(banks):
                for b in banks:
                    mm(ps[:, b, 0:HALF], brow[96:97, 0:P], brow[96:97, 0:HALF], start=True, stop=False)

            x_split(1)
            up_chunk(0, 0, 512, 0)
            pe.wait_ge(onehots, 2)
            for t in range(16):
                ins = mm(ps[:, 4, 0:P], doh[:, t, :], soh[:, t, :], start=t == 0, stop=t == 15)
            ins.then_inc(count_out, 1)
            up_chunk(1, 1, 512, 1)
            up_chunk(2, 2, 512, 2)
            to_rows(1)
            up_chunk(3, 3, 512, 3)
            to_columns(3)
            up_chunk(4, 4, 256, 7)
            weigh(2, qkv[:, 0:D])
            pe.wait_ge(qkv_copied, 1)
            up_chunk(5, 5, 512, 0)
            spread(4)
            pe.wait_ge(qkv_copied, 2)
            up_chunk(6, 6, 256, 1)
            pe.wait_ge(qkv_copied, 5)
            pe.wait_ge(small_in, 16)
            h_transpose(0, 0)
            to_rows(5)
            alphas(0)
            up_chunk(7, 7, 512, 0)
            to_columns(7)
            src_spread(0, 1)
            up_chunk(8, 8, 256, 1)
            weigh(4, qkv[:, D:2 * D])
            A_transpose(1)
            h_transpose(1, 1)
            spread(8)
            pe.wait_ge(b1_ready, 1)
            aggregate(0, 0)
            alphas(1)
            pe.wait_ge(mix_dve, 9)
            zero_start((5, 6))

            def step(h, c, d, k):
                pe.wait_ge(h_copied, 2 * h - 1)
                up_chunk(c, k, 512, 0)
                src_spread(h - 1, h)
                ready(c + 1)
                pe.wait_ge(h_copied, 2 * h)
                up(ps[:, 1, 0:256], k + 1, 256, xTh, xTl).then_inc(hb_out, 1)
                pe.wait_ge(oTl_ready, h - 1)
                down((5, 6), k + 1, 1536, (0, 1), oTh, oTl).then_inc(used, 1)
                A_transpose(h)
                h_transpose(h, d)
                ready(c + 2)
                down((5, 6), k + 2, 0, (2,), oTh, oTl)
                aggregate(h - 1, 1 - d)
                down((5, 6), k + 2, D, (3, 4, 5), oTh, oTl).then_inc(used, 1)
                alphas(h)

            with pe.Fori(2, H0, 2) as h:
                for d in range(2):
                    step(h + d, 3 * h + (3 + 3 * d), d, 9 + 3 * d)

            src_spread(7, 8)
            ready(27)
            pe.wait_ge(oTl_ready, 7)
            down((5, 6), 27, 0, (0, 1, 2, 3), oTh, oTl).then_inc(used, 1)
            A_transpose(8)
            pe.wait_ge(hT_copied, 16)
            for b in range(4):
                nc.tensor.transpose(ps[:, 7, b * P:(b + 1) * P], qkv[:, 2 * D + b * P:2 * D + (b + 1) * P], ident[:])
            pe.wait_ge(AT_copied, 8)
            for b in range(4, 6):
                ins = nc.tensor.transpose(ps[:, 4, (b - 2) * P:(b - 1) * P], qkv[:, 2 * D + b * P:2 * D + (b + 1) * P], ident[:])
            ins.then_inc(mix_pe, 1)
            xhf, xlf = (t[:].rearrange("p b n -> p (b n)") for t in (xTh, xTl))
            ready(28)
            down((5, 6), 28, 0, (4, 5), oTh, oTl).then_inc(o6_used, 1)
            aggregate(7, 1)
            pe.wait_ge(mix_dve, 10)
            pe.wait_ge(h_copied, 16)
            down((0, 1), 28, 1536, (0, 1), xhf, xlf, first=True).then_inc(used, 1)
            ready(29)
            down((0, 1), 29, 0, (2, 3, 4, 5), xhf, xlf).then_inc(used, 1)
            ready(30)
            pe.wait_ge(oTl_ready, 8)
            down((5, 6), 30, 0, (0, 1, 2, 3), oTh, oTl).then_inc(used, 1)
            ready(31)
            down((5, 6), 31, 0, (4, 5), oTh, oTl, last=True).then_inc(used, 1)
            bias((0, 1), 0, 2)
            src_spread(8, 9)
            A_transpose(9)
            pe.wait_ge(AT_copied, 9)
            pe.wait_ge(g_copied, 1)
            for half in range(2):
                ins = mm(ps[:, half, 0:HALF], ATs, hsb[:, 0, half * HALF:(half + 1) * HALF], start=False, stop=True)
            ins.then_inc(F_out, 1)

            zero_start((5, 6))
            transpose6(xn, 2)
            x_split(2)
            def T(j, d):
                pe.wait_ge(hh_ready, j + 1)
                wait(pe, hTl_ready, j)
                for b in range(4):
                    ins = nc.tensor.transpose(ps[:, 4, b * P:(b + 1) * P], hhb[d][:, b * P:(b + 1) * P], ident[:])
                ins.then_inc(T_out, 1)

            up_chunk(FFN0, FFN0, 512, 0)
            a0 = PC["wr"][0]
            for i in range(2 * KD):
                t, x = i // 2, (xTh, xTl)[i % 2]
                ins = mm(ps[:, 7, 0:8], x[:, t, :].bitcast(F32), small[:, a0 + 8 * t:a0 + 8 * t + 8],
                         start=i == 0, stop=i == 2 * KD - 1)
            ins.then_inc(router_out, 1)
            up_chunk(FFN0 + 1, FFN0 + 1, 512, 2)

            def fstep(j, c, d, k):
                wait(pe, silu_done, j - 1)
                up_chunk(c, k, 512, d)
                T(j - 1, 1 - d)
                up_chunk(c + 1, k + 1, 512, 2 + d)
                ready(c + 2)
                pe.wait_ge(hTl_ready, j)
                down((5, 6), k + 2, 0, (0, 1, 2, 3), oTh, oTl).then_inc(used, 1)

            with pe.Fori(1, FS, 2) as j:
                for d in range(2):
                    fstep(j + d, 3 * j + (31 + 3 * d), 1 - d, 34 + 3 * d)
            T(FS - 1, 0)
            ready(L1 - 1)
            pe.wait_ge(hTl_ready, FS)
            down((5, 6), L1 - 1, 0, (0, 1, 2, 3), oTh, oTl, last=True).then_inc(used, 1)

            transpose6(xn, 3)
            x_split(3)
            up_chunk(L1, L1, 256, 5)
            up_chunk(L1 + 1, L1 + 1, 512, 0)

            def l1(s, v):
                pe.wait_ge(s, v)

            def tr6(src, b0):
                for b in range(KD):
                    ins = nc.tensor.transpose(ps[:, b0 + b // 3, (b % 3) * P:(b % 3 + 1) * P], src[:, b * P:(b + 1) * P], ident[:])
                ins.then_inc(l1_pe, 1)

            l1(diag_ready, 10)
            mm(ps[:, 6, :], ones[:], L1D, start=True, stop=True).then_inc(l1_pe, 1)
            up_chunk(L1 + 2, L1 + 2, 512, 1)
            up_chunk(L1 + 3, L1 + 3, 512, 2)
            l1(l1_act, 3)
            tr6(qkv[:, 0:D], 0)
            up_chunk(L1 + 4, L1 + 4, 512, 4)
            l1(A_ready, 10)
            for h in range(4):
                ins = nc.tensor.transpose(ps[:, 6, h * P:(h + 1) * P], L1Z[:, h * P:(h + 1) * P], ident[:])
            ins.then_inc(l1_pe, 1)
            l1(l1_act, 6)
            for h in range(4):
                ins = mm(ps[64 * (h % 2):64 * (h % 2) + 64, 7, (h // 2) * P:(h // 2 + 1) * P],
                         gqm[:, 64 * h:64 * h + 64], L1AT[:, h * P:(h + 1) * P], start=True, stop=True)
            ins.then_inc(l1_pe, 1)
            tr6(qkv[:, D:2 * D], 2)
            wsm = raw[:, (NCH - 1) % R, :]
            l1(landed[(NCH - 1) % R], landed_at(NCH - 1))
            l1(l1_act, 9)
            for t in range(2):
                ins = mm(ps[:, 5, 256:512], gT[:, t * P:(t + 1) * P], wsm[:, 256 * t:256 * t + 256], start=t == 0, stop=t == 1)
            ins.then_inc(l1_pe, 1)
            l1(l1_act, 5)
            up_chunk(L1 + 5, L1 + 5, 256, 0)
            l1(diag_ready, 11)
            mm(ps[:, 6, 0:P], ones[:], L1D[:, 0:P], start=True, stop=True).then_inc(l1_pe, 1)
            l1(l1_act, 11)
            tr6(qkv[:, 2 * D:3 * D], 0)
            l1(l1_act, 12)
            bias((2, 3), 32, 2, first=True)
            l1(A_ready, 11)
            nc.tensor.transpose(ps[:, 6, 0:P], L1Z[:, 0:P], ident[:]).then_inc(l1_pe, 1)
            l1(l1_act, 14)
            for b in range(2):
                ins = mm(ps[:, 7, b * P:(b + 1) * P], gqm[:, 256 + b * P:256 + (b + 1) * P], L1AT[:, 0:P], start=True, stop=True)
            ins.then_inc(l1_pe, 1)
            l1(l1_act, 16)
            for b in range(2):
                for t in range(2):
                    ins = mm(ps[:, 7, 256 + b * P:256 + (b + 1) * P], wsm[:, 512 + 256 * t + b * P:512 + 256 * t + (b + 1) * P],
                             gT[:, t * P:(t + 1) * P], start=t == 0, stop=t == 1)
            ins.then_inc(l1_pe, 1)
            l1(l1_dve, 3)
            ready(L1 + 6)
            down((2, 3), L1 + 6, 0, (0, 1, 2), xhf, xlf).then_inc(used, 1)
            ready(L1 + 7)
            down((2, 3), L1 + 7, 0, (3, 4, 5), xhf, xlf).then_inc(used, 1)
            l1(l1_act, 18)
            for t in range(2):
                for half in range(2):
                    ins = mm(ps[:, 2 + half, 0:HALF], gT2[:, t * P:(t + 1) * P],
                             wsm[:, 1024 + D * t + half * HALF:1024 + D * t + (half + 1) * HALF], start=False, stop=t == 1)
            ins.then_inc(F_out, 1)

            transpose6(xn, 4)
            pe.wait_ge(f_act, 1)
            pe.wait_ge(fw_in, 16)
            for g in range(2):
                for t in range(KD):
                    a = (2 * t + g) * P
                    ins = mm(ps[:, 6, g * P:(g + 1) * P], fw("P")[:, a:a + P], hTs[:, t * P:(t + 1) * P],
                             start=t == 0, stop=t == KD - 1)
            ins.then_inc(f_pe, 1)
            pe.wait_ge(f_act, 2)
            for g in range(2):
                ins = mm(ps[:, 4, 256 * g:256 * g + 256], zT[:, g * P:(g + 1) * P], fw("C")[:, 256 * g:256 * g + 256],
                         start=True, stop=True)
            ins.then_inc(f_pe, 1)

            def hidden(u):
                wait(pe, gelu_done, u - 3)
                b, g = u // 2, u % 2
                cols, own = slice(b * P, (b + 1) * P), slice(512 * g, 512 * g + 512)
                mm(ps[:, u % 4, :], w_a[g][:, cols], z_a[:, own], start=True, stop=False)
                mm(ps[:, u % 4, :], w_b[g][:, cols], z_b[:, own], start=False, stop=True).then_inc(hid_out, 1)

            def spread_weights(u):
                wait(pe, weighted, u - 1)
                b, g = u // 2, u % 2
                mm(ps[:, 4 + g, :], expand[:, b * P:(b + 1) * P], wTs[:, 512 * g:512 * g + 512],
                   start=True, stop=True).then_inc(spread_out, 1)

            def project(u, last=False):
                pe.wait_ge(weighted, u + 1)
                b, g = u // 2, u % 2
                for s4 in range(4):
                    at = ((4 * g + s4) * 16 + b) * 16
                    ins = mm(ps[32 * s4:32 * s4 + 16, 6 + g, 0:P], fw("W2")[:, at:at + 16],
                             hg[:, 512 * (u % 4) + s4 * P:512 * (u % 4) + (s4 + 1) * P], start=False, stop=last,
                             skip_group_check=True)
                ins.then_inc(Y_out, 1)

            pe.wait_ge(z_a_ready, 4)
            pe.wait_ge(z_b_ready, 4)
            pe.wait_ge(w_b_ready, 3)
            for u in range(4):
                hidden(u)
            for g in range(2):
                mm(ps[:, 6 + g, 0:P], brow[96:97, 0:P], brow[96:97, 0:P], start=True, stop=False, skip_group_check=True)
            for g in range(2):
                pe.wait_ge(f_dve, 2 + g)
                for s in range(4):
                    at = 512 * g + s * P
                    ins = nc.tensor.transpose(ps[:, 4 + g, s * P:(s + 1) * P], wcat[:, at:at + P], ident[:])
                ins.then_inc(f_pe, 1)
            pe.wait_ge(f_pool, 1)
            for g in range(2):
                pe.wait_ge(f_dve, 4 + g)
                spread_weights(g)
            for s in range(8):
                mm(ps[32 * (s % 4):32 * (s % 4) + 16, 6 + s // 4, 0:P], fw("b2")[:, 16 * s:16 * s + 16],
                   wTs[:, s * P:(s + 1) * P].bitcast(F32), start=False, stop=False, skip_group_check=True)
            for u in range(UNITS):
                if u + 4 < UNITS:
                    hidden(u + 4)
                project(u, last=u >= UNITS - 2)
                if u + 2 < UNITS:
                    spread_weights(u + 2)
            pe.wait_ge(f_act, 4)
            for b in range(2):
                for g in range(2):
                    ins = mm(ps[:, 1, b * P:(b + 1) * P], fw("G1")[:, 256 * g + b * P:256 * g + (b + 1) * P],
                             cT[:, g * P:(g + 1) * P], start=g == 0, stop=g == 1)
            ins.then_inc(f_pe, 1)
            bias((2, 3), 64, 1, first=True)
            pe.wait_ge(f_act, 6)
            pe.wait_ge(g2_in, 16)
            for t in range(2):
                for half in range(2):
                    ins = mm(ps[:, 2 + half, 0:HALF], fT[:, t * P:(t + 1) * P],
                             qkv[:, D * t + half * HALF:D * t + (half + 1) * HALF], start=False, stop=t == 1)
            ins.then_inc(F_out, 1)


def kernel(**inputs):
    import concourse.bacc as bacc
    import numpy as np
    from concourse.bass_utils import run_bass_kernel_spmd

    a = {k: np.asarray(v) for k, v in inputs.items()}

    def up(w, c0, n):
        return w[:, c0:c0 + n].reshape(KD, P, n).transpose(1, 0, 2).reshape(P, KD * n)

    def down(w, k0, n):
        return w[k0 * P:(k0 + n) * P].reshape(n, P, D).transpose(1, 0, 2).reshape(P, n * D)

    stream = np.zeros((NCH, P, SLOT), np.float32)

    def put(c, *parts):
        at = 0
        for p in parts:
            stream[c, :, at:at + p.shape[1]] = p
            at += p.shape[1]
        assert at == chunk_len(c)

    def put_qkv(cs, w):
        for i, c in enumerate(cs):
            put(c, up(w, 512 * i, 512 if i < 4 else 256))

    w1, w2 = a["L0_gnn_W1"], a["L0_gnn_W2"]
    put_qkv(range(5), a["L0_mix_Wqkv"].T)
    for h in range(2):
        put(5 + 2 * h, up(w1, D * h, 512))
        put(6 + 2 * h, up(w1, D * h + 512, 256))
    for h in range(2, H0):
        put(3 * h + 3, up(w1, D * h, 512))
        put(3 * h + 4, up(w1, D * h + 512, 256), down(w2, KD * (h - 2), 2))
        put(3 * h + 5, down(w2, KD * (h - 2) + 2, 4))
    wp = a["L0_mix_Wp"].T
    put(27, down(w2, KD * 6, 4))
    put(28, down(w2, KD * 6 + 4, 2), down(wp, 0, 2))
    put(29, down(wp, 2, 4))
    put(30, down(w2, KD * 7, 4))
    put(31, down(w2, KD * 7 + 4, 2))
    for e in range(9):
        wg, wu, wd = ((a["L0_ffn_Wg"][e], a["L0_ffn_Wu"][e], a["L0_ffn_Wd"][e]) if e < 8
                      else (a["L0_ffn_sg"], a["L0_ffn_su"], a["L0_ffn_sd"]))
        for b in range(3):
            j = 3 * e + b
            put(FFN0 if j == 0 else 31 + 3 * j, up(wg.T, FB * b, FB))
            put(FFN0 + 1 if j == 0 else 32 + 3 * j, up(wu.T, FB * b, FB))
            put(36 + 3 * j if j < FS - 1 else L1 - 1, down(wd.T, 4 * b, 4))
    put_qkv(range(L1 + 1, L1 + 6), a["L1_mix_w_qkv"])
    put(L1, up(a["L1_gnn_W1"], 0, 256))
    put(L1 + 6, down(a["L1_mix_w_proj"], 0, 3))
    put(L1 + 7, down(a["L1_mix_w_proj"], 3, 3))
    sq = lambda w: w.reshape(2, P, 256).transpose(1, 0, 2).reshape(P, 512)
    put(L1 + 8, sq(a["L1_gnn_W2"]), sq(a["L1_gnn_Wm1"]), down(a["L1_gnn_Wm2"], 0, 2))

    part = lambda v, n: v.reshape(n, P).T
    a1 = np.stack([a["L0_gnn_a_src1"], a["L0_gnn_a_dst1"]], -1)
    b1 = np.zeros((P, P), np.float32)
    b1[0:48] = b1[64:112] = a["L0_gnn_b1"].reshape(48, P)
    small = np.concatenate([
        a1.reshape(H0, KD, P, 2).transpose(2, 0, 1, 3).reshape(P, 96),
        b1,
        a["L0_ffn_w_router"].T.reshape(KD, P, 8).transpose(1, 0, 2).reshape(P, 48),
        np.broadcast_to(a["L0_ffn_expert_bias"], (P, 8)),
        part(a["L1_gnn_b1"], 2), part(a["L1_gnn_b2"], 2), part(a["L1_gnn_bm1"], 2), part(a["L1_ffn_g1b"], 2)], 1)
    rows = lambda v, n=P: np.broadcast_to(v.reshape(1, -1), (n, v.size))
    ga = np.concatenate([rows(a["L1_gnn_a_src1"]), rows(a["L1_gnn_a_dst1"]),
                         rows(a["L1_gnn_a_src2"]), rows(a["L1_gnn_a_dst2"])], 1)
    a2b = np.concatenate([rows(a["L0_gnn_a_src2"]), rows(a["L0_gnn_a_dst2"])], 1)
    brow = np.stack([a["L0_gnn_b2"], a["L0_mix_bp"], a["L1_gnn_bm2"], a["L1_mix_b_proj"], a["L1_ffn_g2b"]])

    fwt = np.zeros((P, NF), np.float32)

    def place(name, v):
        fwt[:, FC[name][0]:FC[name][1]] = v.reshape(P, -1)

    pz = np.zeros((D, 2, 4, 32), np.float32)
    pz[:, :, :, 0:16] = pz[:, :, :, 16:32] = a["L1_ffn_P"].reshape(2, 4, D, 16).transpose(2, 0, 1, 3)
    place("P", pz.reshape(KD, P, 2 * P).transpose(1, 0, 2))
    g1 = np.zeros((4, 32, 2, 256), np.float32)
    g1[:, 0:16] = a["L1_ffn_G1"].reshape(2, 4, 16, 256).transpose(1, 2, 0, 3)
    place("G1", g1)
    row = np.arange(P) % 32
    place("cst", np.stack([row != 16, -1.0 * (row >= 16), row < 16, 1.0 * (row == 17) - (row == 16)], 1))
    cc = np.zeros((4, 32, 2, 4, 64), np.float32)
    bb = np.zeros((2, 64, 8, 16), np.float32)
    ww = np.zeros((4, 32, 2, 2048), np.float32)
    wb = np.zeros((4, 32, 2, 2048), np.float32)
    for s in range(8):
        cc[s % 4, 0:16, s // 4, s % 4] = a["L1_ffn_C"][s].T
        bb[:, :, s] = a["L1_ffn_b2"][s]
        w1s = a["L1_ffn_W1"][s].transpose(1, 0, 2).reshape(16, 2048)
        ww[s % 4, 0:16, s // 4] = ww[s % 4, 16:32, s // 4] = wb[s % 4, 0:16, s // 4] = w1s
        wb[s % 4, 16:18, s // 4] = a["L1_ffn_b1"][s].reshape(2048)
    place("C", cc)
    place("W1", ww)
    place("b2", bb)
    place("W2", a["L1_ffn_W2"].reshape(8, 16, 4, 32, 16).transpose(2, 3, 0, 1, 4))

    arrays = {
        "x_in_d": a["x"], "src_d": a["src"].reshape(P, 16), "dst_d": a["dst"].reshape(P, 16), "stream_d": stream,
        "small_d": small, "wqb_d": rows(a["L0_mix_w_q"]), "wk_d": rows(a["L0_mix_w_k"], 12), "a2b_d": a2b, "ga_d": ga,
        "brow_d": brow, "fw_d": fwt, "w1b_d": wb.reshape(P, 4096), "g2_d": down(a["L1_ffn_G2"], 0, 2),
    }
    arrays = {k: np.ascontiguousarray(v) for k, v in arrays.items()}
    nc = bacc.Bacc("TRN2", target_bir_lowering=False, num_devices=1)
    aps = [nc.dram_tensor(k, v.shape, mybir.dt.from_np(v.dtype), kind="ExternalInput").ap() for k, v in arrays.items()]
    out = nc.dram_tensor("out_d", (N, D), F32, kind="ExternalOutput").ap()
    build(nc, *aps, out)
    return run_bass_kernel_spmd(nc, [arrays], core_ids=[0]).results[0]["out_d"]
```
